# Optimizing a Trainium2 kernel written in Bass

```python
import numpy as np
import jax
import jax.numpy as jnp

def _softmax(x, axis=-1):
    return jax.nn.softmax(x, axis=axis)

def _gelu(x):
    return jax.nn.gelu(x, approximate=True)

def _silu(x):
    return jax.nn.silu(x)

def _sigmoid(x):
    return jax.nn.sigmoid(x)

def _layernorm(x, axis=-1, eps=1e-05):
    m = jnp.mean(x, axis=axis, keepdims=True)
    v = jnp.var(x, axis=axis, keepdims=True)
    return (x - m) / jnp.sqrt(v + eps)

def _scatter_add(tgt, idx, src, axis=0):
    return tgt.at[idx].add(src)

def _segment_sum(src, seg, n):
    return jax.ops.segment_sum(src, seg, n)
kernel_name = 'mk_seq_postln_d4_jaxref_r8_31d799'

def setup_inputs(seed: int=0):
    np.random.seed(seed)
    _w = jnp.asarray

    def _L0_attn_setup():
        import jax, jax.numpy as jnp
        import numpy as np
        B, T, D = (2, 256, 256)
        QH, KVH = (16, 4)
        HD = D // QH

        def rotate_half(x):
            d = x.shape[-1] // 2
            return jnp.concatenate([-x[..., d:], x[..., :d]], axis=-1)

        def rope_tables(head_dim, seq_len, theta=10000.0):
            freqs = 1.0 / theta ** (jnp.arange(0, head_dim, 2, dtype=jnp.float32) / head_dim)
            t = jnp.arange(seq_len, dtype=jnp.float32)
            ang = t[:, None] * freqs[None, :]
            cos = jnp.tile(jnp.cos(ang), (1, 2))
            sin = jnp.tile(jnp.sin(ang), (1, 2))
            return (cos, sin)

        def apply_rope(x, cos, sin):
            c = cos[None, None, :, :]
            s = sin[None, None, :, :]
            return x * c + rotate_half(x) * s
        key = jax.random.key(seed)
        kx, kq, kk, kv, ko = jax.random.split(key, 5)
        scale = D ** (-0.5)
        return {'x': jax.random.normal(kx, (B, T, D), dtype=jnp.float32), 'wq': jax.random.normal(kq, (D, D), dtype=jnp.float32) * scale, 'wk': jax.random.normal(kk, (D, KVH * HD), dtype=jnp.float32) * scale, 'wv': jax.random.normal(kv, (D, KVH * HD), dtype=jnp.float32) * scale, 'wo': jax.random.normal(ko, (D, D), dtype=jnp.float32) * scale}
    _L0_attn_in = _L0_attn_setup()

    def _L0_ffn_setup():
        import jax, jax.numpy as jnp
        import numpy as np
        H, LAT, INTER, E, G, TOPK_G, TOP_K = (256, 128, 128, 32, 4, 2, 8)
        SHARED_INTER = 512
        ROUTED_SCALE = 2.5
        B, S = (2, 128)

        def relu2(x):
            return jnp.square(jax.nn.relu(x))
        key = jax.random.key(seed)
        ks = jax.random.split(key, 9)
        w = 0.02
        return {'hidden_states': jax.random.normal(ks[0], (B, S, H), jnp.float32), 'gate_w': jax.random.normal(ks[1], (E, H), jnp.float32) * w, 'gate_bias': jax.random.normal(ks[2], (E,), jnp.float32) * w, 'fc1_w': jax.random.normal(ks[3], (LAT, H), jnp.float32) * w, 'fc2_w': jax.random.normal(ks[4], (H, LAT), jnp.float32) * w, 'w1': jax.random.normal(ks[5], (E, INTER, LAT), jnp.float32) * w, 'w2': jax.random.normal(ks[6], (E, LAT, INTER), jnp.float32) * w, 'shared_up_w': jax.random.normal(ks[7], (SHARED_INTER, H), jnp.float32) * w, 'shared_down_w': jax.random.normal(ks[8], (H, SHARED_INTER), jnp.float32) * w}
    _L0_ffn_in = _L0_ffn_setup()

    def _L1_attn_setup():
        import jax, jax.numpy as jnp
        import numpy as np
        N_HEADS = 16
        HEAD_DIM = 128
        D_MODEL = 256
        EPS = 1e-05

        def _rmsnorm(x, w):
            rms = jnp.sqrt(jnp.mean(x * x, axis=-1, keepdims=True) + EPS)
            return x / rms * w
        key = jax.random.key(seed)
        ks = jax.random.split(key, 8)
        B, T = (4, 256)
        s = D_MODEL ** (-0.5)
        return {'x': jax.random.normal(ks[0], (B, T, D_MODEL), dtype=jnp.float32), 'Wq': jax.random.normal(ks[1], (N_HEADS * HEAD_DIM, D_MODEL), dtype=jnp.float32) * s, 'Wk': jax.random.normal(ks[2], (N_HEADS * HEAD_DIM, D_MODEL), dtype=jnp.float32) * s, 'Wv': jax.random.normal(ks[3], (N_HEADS * HEAD_DIM, D_MODEL), dtype=jnp.float32) * s, 'Wo': jax.random.normal(ks[4], (D_MODEL, N_HEADS * HEAD_DIM), dtype=jnp.float32) * s, 'gq': jnp.ones((HEAD_DIM,), dtype=jnp.float32), 'gk': jnp.ones((HEAD_DIM,), dtype=jnp.float32)}
    _L1_attn_in = _L1_attn_setup()

    def _L1_ffn_setup():
        import jax, jax.numpy as jnp
        import numpy as np
        H = 256
        I = 128
        K = 8
        E = 128
        TOPK = 4
        EPS = 1e-08
        key = jax.random.key(seed)
        ks = jax.random.split(key, 10)
        s = 0.02
        return {'x': jax.random.normal(ks[0], (4, 256, H), jnp.float32), 'w_router': jax.random.normal(ks[1], (H, E), jnp.float32) * s, 'w_gate': jax.random.normal(ks[2], (H, K * I), jnp.float32) * s, 'w_up': jax.random.normal(ks[3], (H, K * I), jnp.float32) * s, 'w_down': jax.random.normal(ks[4], (I, H), jnp.float32) * s, 'amplitudes': jax.random.normal(ks[5], (E, K, 2), jnp.float32) * 0.1, 'expert_scale': jnp.ones((E,), jnp.float32), 'shared_w_gate': jax.random.normal(ks[6], (H, 2 * I), jnp.float32) * s, 'shared_w_up': jax.random.normal(ks[7], (H, 2 * I), jnp.float32) * s, 'shared_w_down': jax.random.normal(ks[8], (2 * I, H), jnp.float32) * s}
    _L1_ffn_in = _L1_ffn_setup()

    def _L2_attn_setup():
        import jax, jax.numpy as jnp
        import numpy as np
        from jax import lax
        B, L, D = (4, 256, 256)
        R = 256
        DH = D // 4
        key = jax.random.key(seed)
        ks = jax.random.split(key, 12)
        s = 0.02
        x = jax.random.normal(ks[0], (B, L, D), dtype=jnp.float32)
        Wu = jax.random.normal(ks[1], (R, D), dtype=jnp.float32) * s
        bu = jnp.zeros((R,), dtype=jnp.float32)
        Wv = jax.random.normal(ks[2], (R, D), dtype=jnp.float32) * s
        bv = jnp.zeros((R,), dtype=jnp.float32)
        Wg1 = jax.random.normal(ks[3], (DH, D), dtype=jnp.float32) * s
        bg1 = jnp.zeros((DH,), dtype=jnp.float32)
        Wg2 = jax.random.normal(ks[4], (R, DH), dtype=jnp.float32) * s
        bg2 = jnp.zeros((R,), dtype=jnp.float32)
        conv_w = jax.random.normal(ks[5], (D, 1, 3), dtype=jnp.float32) * s
        conv_b = jnp.zeros((D,), dtype=jnp.float32)
        return {'x': x, 'Wu': Wu, 'bu': bu, 'Wv': Wv, 'bv': bv, 'Wg1': Wg1, 'bg1': bg1, 'Wg2': Wg2, 'bg2': bg2, 'conv_w': conv_w, 'conv_b': conv_b}
    _L2_attn_in = _L2_attn_setup()

    def _L2_ffn_setup():
        import jax, jax.numpy as jnp
        import numpy as np

        def _sparsify_2to4(h):
            B, S, I = h.shape
            g = h.reshape(B, S, I // 4, 4)
            a = jnp.abs(g)
            _, idx = jax.lax.top_k(a, 2)
            pos = jnp.arange(4)
            mask = (pos == idx[..., 0:1]) | (pos == idx[..., 1:2])
            return (g * mask.astype(g.dtype)).reshape(B, S, I)
        key = jax.random.key(seed)
        k1, k2, k3, k4 = jax.random.split(key, 4)
        B, S, H, I = (4, 256, 256, 1024)
        x = jax.random.normal(k1, (B, S, H), dtype=jnp.float32)
        w_gate = jax.random.normal(k2, (H, I), dtype=jnp.float32) / np.sqrt(H)
        w_up = jax.random.normal(k3, (H, I), dtype=jnp.float32) / np.sqrt(H)
        w_down = jax.random.normal(k4, (I, H), dtype=jnp.float32) / np.sqrt(I)
        return {'x': x, 'w_gate': w_gate, 'w_up': w_up, 'w_down': w_down}
    _L2_ffn_in = _L2_ffn_setup()

    def _L3_attn_setup():
        import jax, jax.numpy as jnp
        import numpy as np
        B, S, E, H, KVH = (2, 128, 256, 16, 4)
        D = E // H
        RATIO = H // KVH
        NEG = -1e+30
        EPS = 1e-08
        LAM_INIT = 0.8 - 0.6 * float(np.exp(-0.3 * 0))

        def _rope(t):
            d2 = t.shape[-1]
            theta = 1.0 / 10000.0 ** (jnp.arange(0, d2, 2, dtype=jnp.float32) / d2)
            ang = jnp.arange(t.shape[1], dtype=jnp.float32)[:, None] * theta[None, :]
            cos = jnp.cos(ang)[None, :, None, :]
            sin = jnp.sin(ang)[None, :, None, :]
            tr = t.reshape(*t.shape[:-1], d2 // 2, 2)
            re, im = (tr[..., 0], tr[..., 1])
            out = jnp.stack([re * cos - im * sin, re * sin + im * cos], axis=-1)
            return out.reshape(t.shape)
        key = jax.random.key(seed)
        ks = jax.random.split(key, 10)
        sc = 0.02
        return {'x': jax.random.normal(ks[0], (B, S, E), jnp.float32), 'Wq': jax.random.normal(ks[1], (E, 2 * H * D), jnp.float32) * sc, 'Wk': jax.random.normal(ks[2], (E, 2 * KVH * D), jnp.float32) * sc, 'Wv': jax.random.normal(ks[3], (E, KVH * D), jnp.float32) * sc, 'Wo': jax.random.normal(ks[4], (E, E), jnp.float32) * sc, 'lq1': jax.random.normal(ks[5], (H, D), jnp.float32) * 0.1, 'lq2': jax.random.normal(ks[6], (H, D), jnp.float32) * 0.1, 'lk1': jax.random.normal(ks[7], (H, D), jnp.float32) * 0.1, 'lk2': jax.random.normal(ks[8], (H, D), jnp.float32) * 0.1, 'rms_w': jnp.ones((D,), jnp.float32)}
    _L3_attn_in = _L3_attn_setup()

    def _L3_ffn_setup():
        import jax, jax.numpy as jnp
        import numpy as np
        NUM_EXPERTS = 32
        TOP_K = 4
        HIDDEN = 256
        INTER = 96
        key = jax.random.key(seed)
        k1, k2, k3, k4 = jax.random.split(key, 4)
        hidden_states = jax.random.normal(k1, (4, 64, HIDDEN), dtype=jnp.float32)
        gate = jax.random.normal(k2, (HIDDEN, NUM_EXPERTS), dtype=jnp.float32) * 0.02
        gate_up_proj = jax.random.normal(k3, (NUM_EXPERTS, HIDDEN, 2 * INTER), dtype=jnp.float32) * 0.02
        down_proj = jax.random.normal(k4, (NUM_EXPERTS, INTER, HIDDEN), dtype=jnp.float32) * 0.02
        return {'hidden_states': hidden_states, 'gate': gate, 'gate_up_proj': gate_up_proj, 'down_proj': down_proj}
    _L3_ffn_in = _L3_ffn_setup()
    _d = {'L0_attn_x': _L0_attn_in['x'], 'L0_attn_wq': _L0_attn_in['wq'], 'L0_attn_wk': _L0_attn_in['wk'], 'L0_attn_wv': _L0_attn_in['wv'], 'L0_attn_wo': _L0_attn_in['wo'], 'L0_ffn_gate_w': _L0_ffn_in['gate_w'], 'L0_ffn_gate_bias': _L0_ffn_in['gate_bias'], 'L0_ffn_fc1_w': _L0_ffn_in['fc1_w'], 'L0_ffn_fc2_w': _L0_ffn_in['fc2_w'], 'L0_ffn_w1': _L0_ffn_in['w1'], 'L0_ffn_w2': _L0_ffn_in['w2'], 'L0_ffn_shared_up_w': _L0_ffn_in['shared_up_w'], 'L0_ffn_shared_down_w': _L0_ffn_in['shared_down_w'], 'L1_attn_Wq': _L1_attn_in['Wq'], 'L1_attn_Wk': _L1_attn_in['Wk'], 'L1_attn_Wv': _L1_attn_in['Wv'], 'L1_attn_Wo': _L1_attn_in['Wo'], 'L1_attn_gq': _L1_attn_in['gq'], 'L1_attn_gk': _L1_attn_in['gk'], 'L1_ffn_w_router': _L1_ffn_in['w_router'], 'L1_ffn_w_gate': _L1_ffn_in['w_gate'], 'L1_ffn_w_up': _L1_ffn_in['w_up'], 'L1_ffn_w_down': _L1_ffn_in['w_down'], 'L1_ffn_amplitudes': _L1_ffn_in['amplitudes'], 'L1_ffn_expert_scale': _L1_ffn_in['expert_scale'], 'L1_ffn_shared_w_gate': _L1_ffn_in['shared_w_gate'], 'L1_ffn_shared_w_up': _L1_ffn_in['shared_w_up'], 'L1_ffn_shared_w_down': _L1_ffn_in['shared_w_down'], 'L2_attn_Wu': _L2_attn_in['Wu'], 'L2_attn_bu': _L2_attn_in['bu'], 'L2_attn_Wv': _L2_attn_in['Wv'], 'L2_attn_bv': _L2_attn_in['bv'], 'L2_attn_Wg1': _L2_attn_in['Wg1'], 'L2_attn_bg1': _L2_attn_in['bg1'], 'L2_attn_Wg2': _L2_attn_in['Wg2'], 'L2_attn_bg2': _L2_attn_in['bg2'], 'L2_attn_conv_w': _L2_attn_in['conv_w'], 'L2_attn_conv_b': _L2_attn_in['conv_b'], 'L2_ffn_w_gate': _L2_ffn_in['w_gate'], 'L2_ffn_w_up': _L2_ffn_in['w_up'], 'L2_ffn_w_down': _L2_ffn_in['w_down'], 'L3_attn_Wq': _L3_attn_in['Wq'], 'L3_attn_Wk': _L3_attn_in['Wk'], 'L3_attn_Wv': _L3_attn_in['Wv'], 'L3_attn_Wo': _L3_attn_in['Wo'], 'L3_attn_lq1': _L3_attn_in['lq1'], 'L3_attn_lq2': _L3_attn_in['lq2'], 'L3_attn_lk1': _L3_attn_in['lk1'], 'L3_attn_lk2': _L3_attn_in['lk2'], 'L3_attn_rms_w': _L3_attn_in['rms_w'], 'L3_ffn_gate': _L3_ffn_in['gate'], 'L3_ffn_gate_up_proj': _L3_ffn_in['gate_up_proj'], 'L3_ffn_down_proj': _L3_ffn_in['down_proj']}
    _x0 = _d['L0_attn_x']
    _d['L0_attn_x'] = jax.random.normal(jax.random.fold_in(jax.random.key(seed), 1), (8, 256, 256), dtype=_x0.dtype)
    del _x0
    return _d

def reference(L0_attn_x, L0_attn_wq, L0_attn_wk, L0_attn_wv, L0_attn_wo, L0_ffn_gate_w, L0_ffn_gate_bias, L0_ffn_fc1_w, L0_ffn_fc2_w, L0_ffn_w1, L0_ffn_w2, L0_ffn_shared_up_w, L0_ffn_shared_down_w, L1_attn_Wq, L1_attn_Wk, L1_attn_Wv, L1_attn_Wo, L1_attn_gq, L1_attn_gk, L1_ffn_w_router, L1_ffn_w_gate, L1_ffn_w_up, L1_ffn_w_down, L1_ffn_amplitudes, L1_ffn_expert_scale, L1_ffn_shared_w_gate, L1_ffn_shared_w_up, L1_ffn_shared_w_down, L2_attn_Wu, L2_attn_bu, L2_attn_Wv, L2_attn_bv, L2_attn_Wg1, L2_attn_bg1, L2_attn_Wg2, L2_attn_bg2, L2_attn_conv_w, L2_attn_conv_b, L2_ffn_w_gate, L2_ffn_w_up, L2_ffn_w_down, L3_attn_Wq, L3_attn_Wk, L3_attn_Wv, L3_attn_Wo, L3_attn_lq1, L3_attn_lq2, L3_attn_lk1, L3_attn_lk2, L3_attn_rms_w, L3_ffn_gate, L3_ffn_gate_up_proj, L3_ffn_down_proj):

    def _L0_attn_ref(x, wq, wk, wv, wo):
        import jax, jax.numpy as jnp
        import numpy as np
        B, T, D = (2, 256, 256)
        QH, KVH = (16, 4)
        HD = D // QH

        def rotate_half(x):
            d = x.shape[-1] // 2
            return jnp.concatenate([-x[..., d:], x[..., :d]], axis=-1)

        def rope_tables(head_dim, seq_len, theta=10000.0):
            freqs = 1.0 / theta ** (jnp.arange(0, head_dim, 2, dtype=jnp.float32) / head_dim)
            t = jnp.arange(seq_len, dtype=jnp.float32)
            ang = t[:, None] * freqs[None, :]
            cos = jnp.tile(jnp.cos(ang), (1, 2))
            sin = jnp.tile(jnp.sin(ang), (1, 2))
            return (cos, sin)

        def apply_rope(x, cos, sin):
            c = cos[None, None, :, :]
            s = sin[None, None, :, :]
            return x * c + rotate_half(x) * s
        b, t, d = x.shape
        cos, sin = rope_tables(HD, t)
        q = (x @ wq).reshape(b, t, QH, HD).transpose(0, 2, 1, 3)
        k = (x @ wk).reshape(b, t, KVH, HD).transpose(0, 2, 1, 3)
        v = (x @ wv).reshape(b, t, KVH, HD).transpose(0, 2, 1, 3)
        q = apply_rope(q, cos, sin)
        k = apply_rope(k, cos, sin)
        g = QH // KVH
        k = jnp.repeat(k, g, axis=1)
        v = jnp.repeat(v, g, axis=1)
        attn = jnp.einsum('bhqd,bhkd->bhqk', q, k) / np.sqrt(HD)
        mask = jnp.triu(jnp.ones((t, t), dtype=bool), k=1)
        attn = jnp.where(mask[None, None], -jnp.inf, attn)
        attn = jax.nn.softmax(attn, axis=-1)
        out = jnp.einsum('bhqk,bhkd->bhqd', attn, v)
        out = out.transpose(0, 2, 1, 3).reshape(b, t, d)
        return out @ wo

    def _L0_ffn_ref(hidden_states, gate_w, gate_bias, fc1_w, fc2_w, w1, w2, shared_up_w, shared_down_w):
        import jax, jax.numpy as jnp
        import numpy as np
        H, LAT, INTER, E, G, TOPK_G, TOP_K = (256, 128, 128, 32, 4, 2, 8)
        SHARED_INTER = 512
        ROUTED_SCALE = 2.5
        B, S = (2, 128)

        def relu2(x):
            return jnp.square(jax.nn.relu(x))
        orig_shape = hidden_states.shape
        x = hidden_states.reshape(-1, H)
        T = x.shape[0]
        logits = jnp.einsum('th,eh->te', x.astype(jnp.float32), gate_w)
        scores = jax.nn.sigmoid(logits)
        sb = scores + gate_bias
        grp = sb.reshape(T, G, E // G)
        group_scores = jax.lax.top_k(grp, 2)[0].sum(-1)
        _, gidx = jax.lax.top_k(group_scores, TOPK_G)
        gmask = jax.nn.one_hot(gidx, G, dtype=sb.dtype).sum(1)
        masked = jnp.where(gmask[:, :, None] > 0, grp, -jnp.inf).reshape(T, E)
        _, topi = jax.lax.top_k(masked, TOP_K)
        wsel = jnp.take_along_axis(scores, topi, axis=1)
        wsel = wsel / wsel.sum(-1, keepdims=True) * ROUTED_SCALE
        cw = jnp.zeros((T, E), jnp.float32).at[jnp.arange(T)[:, None], topi].add(wsel)
        x_lat = x @ fc1_w.T
        h = relu2(jnp.einsum('tl,eil->eti', x_lat, w1))
        h = h * cw.T[:, :, None]
        y_lat = jnp.einsum('eti,eli->tl', h, w2)
        routed = y_lat @ fc2_w.T
        shared = relu2(x @ shared_up_w.T) @ shared_down_w.T
        return (shared + routed).reshape(orig_shape)

    def _L1_attn_ref(x, Wq, Wk, Wv, Wo, gq, gk):
        import jax, jax.numpy as jnp
        import numpy as np
        N_HEADS = 16
        HEAD_DIM = 128
        D_MODEL = 256
        EPS = 1e-05

        def _rmsnorm(x, w):
            rms = jnp.sqrt(jnp.mean(x * x, axis=-1, keepdims=True) + EPS)
            return x / rms * w
        B, T, _ = x.shape
        H, hd = (N_HEADS, HEAD_DIM)
        q = (x @ Wq.T).reshape(B, T, H, hd)
        k = (x @ Wk.T).reshape(B, T, H, hd)
        v = (x @ Wv.T).reshape(B, T, H, hd)
        q = _rmsnorm(q, gq)
        k = _rmsnorm(k, gk)
        q = q.transpose(0, 2, 1, 3)
        k = k.transpose(0, 2, 1, 3)
        v = v.transpose(0, 2, 1, 3)
        scale = hd ** (-0.5)
        scores = jnp.einsum('bhqd,bhkd->bhqk', q, k) * scale
        q_idx = jnp.arange(T)[:, None]
        k_idx = jnp.arange(T)[None, :]
        mask = k_idx > q_idx
        scores = jnp.where(mask[None, None], -jnp.inf, scores)
        attn = jax.nn.softmax(scores.astype(jnp.float32), axis=-1).astype(q.dtype)
        out = jnp.einsum('bhqk,bhkd->bhqd', attn, v)
        out = out.transpose(0, 2, 1, 3).reshape(B, T, H * hd)
        return out @ Wo.T

    def _L1_ffn_ref(x, w_router, w_gate, w_up, w_down, amplitudes, expert_scale, shared_w_gate, shared_w_up, shared_w_down):
        import jax, jax.numpy as jnp
        import numpy as np
        H = 256
        I = 128
        K = 8
        E = 128
        TOPK = 4
        EPS = 1e-08
        B, S, _ = x.shape
        T = B * S
        xt = x.reshape(T, H)
        probs = jax.nn.softmax(xt @ w_router, axis=-1)
        topk_p, topk_idx = jax.lax.top_k(probs, TOPK)
        topk_w = topk_p / (jnp.sum(topk_p, axis=-1, keepdims=True) + EPS)
        gate = (xt @ w_gate).reshape(T, K, I)
        up = (xt @ w_up).reshape(T, K, I)
        basis = jax.nn.silu(gate) * up
        p = amplitudes[..., 0] ** 2 + amplitudes[..., 1] ** 2
        mix = p / (jnp.sum(p, axis=-1, keepdims=True) + EPS)
        mix_sel = mix[topk_idx]
        mixed = jnp.einsum('tek,tki->tei', mix_sel, basis)
        down = jnp.einsum('tei,ih->teh', mixed, w_down)
        coeff = topk_w * expert_scale[topk_idx]
        out = jnp.einsum('teh,te->th', down, coeff)
        shared = jax.nn.silu(xt @ shared_w_gate) * (xt @ shared_w_up) @ shared_w_down
        out = out + shared
        return out.reshape(B, S, H)

    def _L2_attn_ref(x, Wu, bu, Wv, bv, Wg1, bg1, Wg2, bg2, conv_w, conv_b):
        import jax, jax.numpy as jnp
        import numpy as np
        from jax import lax
        B, L, D = (4, 256, 256)
        R = 256
        DH = D // 4
        xc = jnp.transpose(x, (0, 2, 1))
        t = lax.conv_general_dilated(xc, conv_w, window_strides=(1,), padding=[(1, 1)], dimension_numbers=('NCH', 'OIH', 'NCH'), feature_group_count=D)
        t_out = jnp.transpose(t + conv_b[None, :, None], (0, 2, 1))
        u = jnp.einsum('bld,rd->blr', x, Wu) + bu
        v = jnp.einsum('bld,rd->blr', x, Wv) + bv
        h = jax.nn.relu(jnp.einsum('bld,hd->blh', x, Wg1) + bg1)
        gates = jax.nn.sigmoid(jnp.einsum('blh,rh->blr', h, Wg2) + bg2)
        u_gated = u * gates
        v_gated = v * gates
        k_cumsum = jnp.cumsum(u_gated, axis=1)
        global_out = k_cumsum * v_gated
        uv_term = jnp.einsum('blr,rd->bld', global_out, Wu.T[:R, :])
        return t_out + uv_term

    def _L2_ffn_ref(x, w_gate, w_up, w_down):
        import jax, jax.numpy as jnp
        import numpy as np

        def _sparsify_2to4(h):
            B, S, I = h.shape
            g = h.reshape(B, S, I // 4, 4)
            a = jnp.abs(g)
            _, idx = jax.lax.top_k(a, 2)
            pos = jnp.arange(4)
            mask = (pos == idx[..., 0:1]) | (pos == idx[..., 1:2])
            return (g * mask.astype(g.dtype)).reshape(B, S, I)
        h = jax.nn.silu(jnp.einsum('bsh,hi->bsi', x, w_gate)) * jnp.einsum('bsh,hi->bsi', x, w_up)
        h_sparse = _sparsify_2to4(h)
        return jnp.einsum('bsi,ih->bsh', h_sparse, w_down)

    def _L3_attn_ref(x, Wq, Wk, Wv, Wo, lq1, lq2, lk1, lk2, rms_w):
        import jax, jax.numpy as jnp
        import numpy as np
        B, S, E, H, KVH = (2, 128, 256, 16, 4)
        D = E // H
        RATIO = H // KVH
        NEG = -1e+30
        EPS = 1e-08
        LAM_INIT = 0.8 - 0.6 * float(np.exp(-0.3 * 0))

        def _rope(t):
            d2 = t.shape[-1]
            theta = 1.0 / 10000.0 ** (jnp.arange(0, d2, 2, dtype=jnp.float32) / d2)
            ang = jnp.arange(t.shape[1], dtype=jnp.float32)[:, None] * theta[None, :]
            cos = jnp.cos(ang)[None, :, None, :]
            sin = jnp.sin(ang)[None, :, None, :]
            tr = t.reshape(*t.shape[:-1], d2 // 2, 2)
            re, im = (tr[..., 0], tr[..., 1])
            out = jnp.stack([re * cos - im * sin, re * sin + im * cos], axis=-1)
            return out.reshape(t.shape)
        b, s, _ = x.shape
        q = (x @ Wq).reshape(b, s, H, 2 * D)
        k = (x @ Wk).reshape(b, s, KVH, 2 * D)
        v = (x @ Wv).reshape(b, s, KVH, D)
        q = _rope(q)
        k = _rope(k)
        k = jnp.repeat(k, RATIO, axis=2)
        v = jnp.repeat(v, RATIO, axis=2)
        qd = q.reshape(b, s, H, 2, D)
        kd = k.reshape(b, s, H, 2, D)
        energy = jnp.einsum('bqhad,bkhad->bahqk', qd, kd)
        causal = jnp.triu(jnp.ones((s, s), dtype=bool), 1)
        energy = jnp.where(causal, NEG, energy)
        scores = jax.nn.softmax(energy / np.sqrt(D), axis=-1)
        lam = (jnp.exp(jnp.sum(lq1 * lk1, -1)) - jnp.exp(jnp.sum(lq2 * lk2, -1)) + LAM_INIT)[None, :, None, None]
        diff = scores[:, 0] - lam * scores[:, 1]
        diff = jnp.where(causal, NEG, diff)
        diff = jax.nn.softmax(diff, axis=-1)
        att = jnp.einsum('bhqv,bvhd->bqhd', diff, v)
        att = att * jax.lax.rsqrt(jnp.mean(att * att, axis=-1, keepdims=True) + EPS) * rms_w
        att = att * (1.0 - LAM_INIT)
        return att.reshape(b, s, E) @ Wo

    def _L3_ffn_ref(hidden_states, gate, gate_up_proj, down_proj):
        import jax, jax.numpy as jnp
        import numpy as np
        NUM_EXPERTS = 32
        TOP_K = 4
        HIDDEN = 256
        INTER = 96
        batch_size = hidden_states.shape[0]
        x = hidden_states.reshape(-1, HIDDEN)
        num_tokens = x.shape[0]
        router_logits = jnp.einsum('TD,DE->TE', x, gate)
        routing_weights = jax.nn.softmax(router_logits.astype(jnp.float32), axis=-1)
        top_k_weights, top_k_indices = jax.lax.top_k(routing_weights, TOP_K)
        top_k_weights = top_k_weights / top_k_weights.sum(axis=-1, keepdims=True)
        top_k_weights = top_k_weights.astype(x.dtype)
        router_weights = jnp.zeros((num_tokens, NUM_EXPERTS), dtype=x.dtype)
        token_indices = jnp.broadcast_to(jnp.arange(num_tokens)[:, None], top_k_indices.shape)
        router_weights = router_weights.at[token_indices, top_k_indices].set(top_k_weights)
        gate_up = jnp.einsum('TD,EDF->TEF', x, gate_up_proj)
        g, u = jnp.split(gate_up, 2, axis=-1)
        gated = u * jax.nn.silu(g)
        next_states = jnp.einsum('TEF,EFD->TED', gated, down_proj)
        next_states = (next_states * router_weights[..., None]).sum(axis=1)
        return next_states.reshape(batch_size, -1, HIDDEN)
    x = L0_attn_x
    x = _layernorm(x + _L0_attn_ref(x, L0_attn_wq, L0_attn_wk, L0_attn_wv, L0_attn_wo), axis=-1)
    x = _layernorm(x + _L0_ffn_ref(x, L0_ffn_gate_w, L0_ffn_gate_bias, L0_ffn_fc1_w, L0_ffn_fc2_w, L0_ffn_w1, L0_ffn_w2, L0_ffn_shared_up_w, L0_ffn_shared_down_w), axis=-1)
    x = _layernorm(x + _L1_attn_ref(x, L1_attn_Wq, L1_attn_Wk, L1_attn_Wv, L1_attn_Wo, L1_attn_gq, L1_attn_gk), axis=-1)
    x = _layernorm(x + _L1_ffn_ref(x, L1_ffn_w_router, L1_ffn_w_gate, L1_ffn_w_up, L1_ffn_w_down, L1_ffn_amplitudes, L1_ffn_expert_scale, L1_ffn_shared_w_gate, L1_ffn_shared_w_up, L1_ffn_shared_w_down), axis=-1)
    x = _layernorm(x + _L2_attn_ref(x, L2_attn_Wu, L2_attn_bu, L2_attn_Wv, L2_attn_bv, L2_attn_Wg1, L2_attn_bg1, L2_attn_Wg2, L2_attn_bg2, L2_attn_conv_w, L2_attn_conv_b), axis=-1)
    x = _layernorm(x + _L2_ffn_ref(x, L2_ffn_w_gate, L2_ffn_w_up, L2_ffn_w_down), axis=-1)
    x = _layernorm(x + _L3_attn_ref(x, L3_attn_Wq, L3_attn_Wk, L3_attn_Wv, L3_attn_Wo, L3_attn_lq1, L3_attn_lq2, L3_attn_lk1, L3_attn_lk2, L3_attn_rms_w), axis=-1)
    x = _layernorm(x + _L3_ffn_ref(x, L3_ffn_gate, L3_ffn_gate_up_proj, L3_ffn_down_proj), axis=-1)
    return x

_drawn_inputs = setup_inputs


def setup_inputs(seed=0):
    import zlib

    import numpy as np

    out = dict(_drawn_inputs(seed))
    spreads = {'L1_attn_gq': (1.0, 0.2),
     'L1_attn_gk': (1.0, 0.2),
     'L1_ffn_expert_scale': (1.0, 0.6),
     'L2_attn_bu': (0.0, 0.1),
     'L2_attn_bv': (0.0, 0.1),
     'L2_attn_bg1': (0.0, 0.664),
     'L2_attn_bg2': (0.0, 0.1),
     'L2_attn_conv_b': (0.0, 0.1),
     'L3_attn_rms_w': (1.0, 0.2)}
    factors = {'L0_ffn_gate_w': 8.0,
     'L0_ffn_gate_bias': 8.0,
     'L0_ffn_fc1_w': 8.0,
     'L0_ffn_fc2_w': 8.0,
     'L0_ffn_w1': 8.0,
     'L0_ffn_w2': 8.0,
     'L1_ffn_w_router': 8.0,
     'L1_ffn_w_gate': 5.084,
     'L1_ffn_w_up': 5.033,
     'L1_ffn_w_down': 5.033,
     'L1_ffn_amplitudes': 8.0,
     'L2_attn_Wg1': 3.593,
     'L3_attn_Wq': 8.0,
     'L3_attn_Wk': 8.0,
     'L3_attn_lq1': 8.0,
     'L3_attn_lq2': 8.0,
     'L3_attn_lk1': 8.0,
     'L3_attn_lk2': 8.0,
     'L3_ffn_gate': 8.0,
     'L3_ffn_gate_up_proj': 8.0,
     'L3_ffn_down_proj': 8.0}
    for name, (base, spread) in spreads.items():
        noise = np.random.default_rng([zlib.crc32(name.encode()), seed]).standard_normal(out[name].shape)
        drawn = base * np.exp(spread * noise) if base else spread * noise
        out[name] = jnp.asarray(drawn.astype(out[name].dtype))
    for name, factor in factors.items():
        out[name] = (out[name] * factor).astype(out[name].dtype)
    return out
```

```python
import math
from contextlib import ExitStack

import numpy as np

import concourse.bass as bass
from concourse import mybir

P = 128
F32 = mybir.dt.float32
BF16 = mybir.dt.bfloat16
I32 = mybir.dt.int32
ALU = mybir.AluOpType
ACT = mybir.ActivationFunctionType
AX = mybir.AxisListType

B, T, D = 8, 256, 256
TOK = B * T
NT = TOK // P
KD = D // P
TT = T // P
CH = 4
CN = CH * P
NCH = NT // CH
LN_EPS = 1e-5
NEG = -1e30
MAGIC = float(0x5F3759DF)


def bc(ap, axis, n):
    wide = ap.unsqueeze(axis)
    shape = list(wide.shape)
    shape[axis] = n
    return wide.broadcast_to(tuple(shape))


def ln_scratch(sb, n):
    return {"z": sb("ln_z", [P, n, D]), "stats": sb("ln_stats", [P, n, 6]), "mv": sb("ln_mv", [P, n, 2]),
            "ve": sb("ln_ve", [P, n]), "rs": sb("ln_rs", [P, n]), "tmp": sb("ln_tmp", [P, n]),
            "carrier": sb("ln_carrier", [P, 1])}


class Steps:

    def __init__(self, eng, sem, per_turn):
        self.eng, self.sem, self.per, self.k, self.turn = eng, sem, per_turn, 0, None

    def begin(self, turn):
        self.turn, self.k = turn, 0

    def inc(self, ins):
        ins.then_inc(self.sem, 1)
        self.k += 1
        return self.k

    def wait(self, k=None):
        self.eng.wait_ge(self.sem, self.turn * self.per + (self.k if k is None else k))

    def do(self, ins):
        self.inc(ins)
        self.wait()

    def end(self):
        assert self.k == self.per, f"a turn has {self.k} steps, not {self.per}"


def carry(nc, w):
    nc.vector.memset(w["carrier"][:, :], 0.0)


def newton_rsqrt(nc, st, v, y, t, iters=3):
    st.inc(nc.vector.tensor_scalar(y.bitcast(I32), v.bitcast(I32), -0.5, MAGIC, ALU.mult, ALU.add))
    for _ in range(iters):
        st.wait()
        st.inc(nc.vector.tensor_tensor(t, y, y, ALU.mult))
        st.wait()
        st.inc(nc.vector.scalar_tensor_tensor(t, v, -0.5, t, ALU.mult, ALU.mult))
        st.wait()
        st.inc(nc.vector.scalar_tensor_tensor(y, t, 1.5, y, ALU.add, ALU.mult))
NEWTON_STEPS = 10
LN_STEPS = NEWTON_STEPS + 5


BIG = 3e38
LOW = -2e38


def split3(nc, st, v, parts, rest):
    st.do(nc.vector.tensor_copy(parts[0], v))
    st.do(nc.vector.tensor_tensor(rest, v, parts[0], ALU.subtract))
    st.do(nc.vector.tensor_copy(parts[1], rest))
    st.do(nc.vector.tensor_tensor(rest, rest, parts[1], ALU.subtract))
    st.do(nc.vector.tensor_copy(parts[2], rest))


def layernorm_tail(nc, st, x_sb, tile0, n, y_ps, y_ready, w):
    z, stats, mv, rs, tmp = w["z"], w["stats"], w["mv"], w["rs"], w["tmp"]
    y_ready()
    st.inc(nc.vector.tensor_tensor(z[:, 0:n, :], y_ps, x_sb[:, bass.ds(tile0, n), :], ALU.add))
    st.wait()
    for t in range(n):
        last = nc.vector.bn_stats(stats[:, t, :], z[:, t, :])
    st.inc(last)
    st.wait()
    carry(nc, w)
    for t in range(n):
        last = nc.vector.bn_aggr(mv[:, t, :], stats[:, t, :])
    st.inc(last)
    st.wait()
    st.inc(nc.vector.tensor_scalar(w["ve"][:, 0:n], mv[:, 0:n, 1], LN_EPS, None, ALU.add))
    st.wait()
    newton_rsqrt(nc, st, w["ve"][:, 0:n], rs[:, 0:n], tmp[:, 0:n])
    st.wait()
    for t in range(n):
        last = nc.vector.tensor_scalar(x_sb[:, bass.ds(tile0 + t, 1), :], z[:, t, :], mv[:, t, 0:1], rs[:, t:t + 1],
                                       ALU.subtract, ALU.mult)
    st.inc(last)



def l0_attention(nc, c, x_sb, w, psum):
    HD, G, R = 16, 4, 4
    V1 = HD + 1
    NG = 8
    with ExitStack() as ctx:
        sb = lambda name, shape, dt=F32: ctx.enter_context(nc.sbuf_tensor("l0a_" + name, shape, dt))
        sem = lambda name: ctx.enter_context(nc.semaphore("l0a_" + name))
        xs = sb("xs", [P, TT, D])
        xT = sb("xT", [P, KD, T])
        qr = sb("qr", [P, R, T])
        k1 = sb("k1", [P, 2, T])
        kr = sb("kr", [P, T])
        va = sb("va", [P, TT, G, V1])
        nm = sb("nm", [P, 2, TT, 2])
        pr = sb("pr", [P, 2, 2, 3 * P])
        pt = sb("pt", [P, 2, 2, 3 * P])
        rec = sb("rec", [P, TT, G * R])
        on = sb("on", [P, TT, D])
        oT = sb("oT", [P, KD, T])
        lw = ln_scratch(sb, TT)
        S = [psum[:, 0:2, :], psum[:, 2:4, :]]
        PT = [psum[:, 4, :], psum[:, 5, :]]
        O = psum[:, 6:8, 0:G * R * V1].rearrange("p t (h e) -> p t h e", e=V1)

        x_staged = sem("x_staged")
        xT_ps = sem("xT_ps")
        xT_ready = sem("xT_ready")
        proj_ps = sem("proj_ps")
        rot_ready = sem("rot_ready")
        s_ps = sem("s_ps")
        nm_ready = sem("nm_ready")
        p_ready = sem("p_ready")
        pt_ps = sem("pt_ps")
        pt_ready = sem("pt_ready")
        av_ps = sem("av_ps")
        on_ready = sem("on_ready")
        oT_ps = sem("oT_ps")
        oT_ready = sem("oT_ready")
        y_ps = sem("y_ps")
        steps = sem("steps")

        with nc.Block() as block:
            @block.sync
            def _(sp):
                with sp.Fori(0, B) as b:
                    sp.wait_ge(xT_ps, b + 1)
                    sp.dma_start(xs[:, :, :], x_sb[:, bass.ds(b * TT, TT), :]).then_inc(x_staged, 16)

            @block.tensor
            def _(pe):
                mm = nc.tensor.matmul
                pe.sem_inc(xT_ps, 1)
                with pe.Fori(0, B) as b:
                    pe.wait_ge(x_staged, b * 16 + 16)
                    for h in range(KD):
                        for t in range(TT):
                            last = nc.tensor.transpose(PT[0][:, (h * TT + t) * P:(h * TT + t + 1) * P],
                                                       xs[:, t, h * P:(h + 1) * P], c["id"])
                    last.then_inc(xT_ps, 1)
                    pe.wait_ge(xT_ready, b + 1)
                    for r in range(R):
                        for k in range(KD):
                            last = mm(S[0][:, r // 2, (r % 2) * T:(r % 2 + 1) * T], w["q"][:, k, r * P:(r + 1) * P],
                                      xT[:, k, :], start=(k == 0), stop=(k == KD - 1))
                    last.then_inc(proj_ps, 1)
                    for j in range(2):
                        for k in range(KD):
                            last = mm(S[1][:, 0, j * T:(j + 1) * T], w["k"][:, k, j * P:(j + 1) * P],
                                      xT[:, k, :], start=(k == 0), stop=(k == KD - 1))
                    last.then_inc(proj_ps, 1)
                    for t in range(TT):
                        for k in range(KD):
                            last = mm(S[1][:, 1, t * G * HD:(t + 1) * G * HD], xT[:, k, t * P:(t + 1) * P],
                                      w["v"][:, k, :], start=(k == 0), stop=(k == KD - 1))
                    last.then_inc(proj_ps, 1)

                    def scores(n):
                        if n < 2:
                            pe.wait_ge(rot_ready, b * 3 + 3)
                        else:
                            pe.wait_ge(p_ready, b * NG + n - 1)
                        for i in range(2):
                            r, g = n // 2, n % 2 * 2 + i
                            rows = slice(32 * g, 32 * g + 32)
                            for t in range(TT):
                                dst = S[n % 2][:, i, t * P:t * P + (t + 1) * P]
                                mm(dst, qr[rows, r, t * P:(t + 1) * P], kr[rows, 0:(t + 1) * P], start=True, stop=False)
                                last = mm(S[n % 2][:, i, 2 * t * P:(2 * t + 1) * P], c["idb"], c["maskb"],
                                          start=False, stop=True)
                        last.then_inc(s_ps, 1)

                    def turn(n):
                        pe.wait_ge(p_ready, b * NG + n + 1)
                        for i in range(2):
                            if n > 0:
                                pe.wait_ge(pt_ready, b * 2 * NG + 2 * (n - 1) + i + 1)
                            for j in range(3):
                                last = nc.tensor.transpose(PT[i][:, j * P:(j + 1) * P],
                                                           pr[:, n % 2, i, j * P:(j + 1) * P], c["id"])
                            last.then_inc(pt_ps, 1)

                    def values(n):
                        for i in range(2):
                            r, g = n // 2, n % 2 * 2 + i
                            h = 4 * g + r
                            pe.wait_ge(pt_ready, b * 2 * NG + 2 * n + i + 1)
                            pp = pt[:, n % 2, i, :]
                            mm(O[:, 0, h, :], pp[:, 0:P], va[:, 0, g, :], start=True, stop=True)
                            mm(O[:, 1, h, :], pp[:, P:2 * P], va[:, 0, g, :], start=True, stop=False)
                            last = mm(O[:, 1, h, :], pp[:, 2 * P:3 * P], va[:, 1, g, :], start=False, stop=True)
                        last.then_inc(av_ps, 1)

                    for n in range(NG + 2):
                        if n < NG:
                            scores(n)
                        if 1 <= n <= NG:
                            turn(n - 1)
                        if n >= 2:
                            values(n - 2)
                    pe.wait_ge(on_ready, b + 1)
                    for h in range(KD):
                        for t in range(TT):
                            last = nc.tensor.transpose(PT[0][:, (h * TT + t) * P:(h * TT + t + 1) * P],
                                                       on[:, t, h * P:(h + 1) * P], c["id"])
                    last.then_inc(oT_ps, 1)
                    pe.wait_ge(oT_ready, b + 1)
                    for t in range(TT):
                        for k in range(KD):
                            last = mm(PT[1][:, t * D:(t + 1) * D], oT[:, k, t * P:(t + 1) * P], w["o"][:, k, :],
                                      start=(k == 0), stop=(k == KD - 1))
                    last.then_inc(y_ps, 1)

            @block.scalar
            def _(act):
                nc.scalar.preload_act_table(ACT.Exp)
                with act.Fori(0, B) as b:
                    act.wait_ge(xT_ps, b + 2)
                    nc.scalar.activation(xT[:, :, :], PT[0].rearrange("p (k t) -> p k t", k=KD), ACT.Copy).then_inc(xT_ready, 1)
                    for n in range(NG):
                        act.wait_ge(nm_ready, b * NG + n + 1)
                        if n >= 2:
                            act.wait_ge(pt_ps, b * 2 * NG + 2 * (n - 1))
                        for i in range(2):
                            for t in range(TT):
                                s = slice(t * P, t * P + (t + 1) * P)
                                last = nc.scalar.activation(pr[:, n % 2, i, s], S[n % 2][:, i, s], ACT.Exp,
                                                            bias=nm[:, n % 2, t, i:i + 1])
                        last.then_inc(p_ready, 1)
                    act.wait_ge(oT_ps, b + 1)
                    nc.scalar.activation(oT[:, :, :], PT[0].rearrange("p (k t) -> p k t", k=KD), ACT.Copy).then_inc(oT_ready, 1)

            @block.vector
            def _(dve):
                N_STEPS = LN_STEPS + 2
                st = Steps(dve, steps, N_STEPS)
                nc.vector.memset(va[:, :, :, HD:V1], 1.0)
                with dve.Fori(0, B) as b:
                    st.begin(b)
                    dve.wait_ge(proj_ps, b * 3 + 1)
                    for j in range(2):
                        last = nc.vector.tensor_tensor(qr[:, 2 * j:2 * j + 2, :],
                                                       S[0][:, j, :].rearrange("p (r t) -> p r t", r=2),
                                                       bc(c["l0_q"], 1, 2), ALU.mult)
                    last.then_inc(rot_ready, 1)
                    dve.wait_ge(proj_ps, b * 3 + 2)
                    st.inc(nc.vector.tensor_tensor(k1[:, :, :], S[1][:, 0, :].rearrange("p (r t) -> p r t", r=2),
                                                   c["l0_k"], ALU.mult))
                    st.wait()
                    nc.vector.tensor_tensor(kr[:, :], k1[:, 0, :], k1[:, 1, :], ALU.add).then_inc(rot_ready, 1)
                    dve.wait_ge(proj_ps, b * 3 + 3)
                    nc.vector.tensor_copy(va[:, :, :, 0:HD],
                                          S[1][:, 1, 0:TT * G * HD].rearrange("p (t g e) -> p t g e", t=TT, g=G)).then_inc(rot_ready, 1)

                    def maxima(n):
                        dve.wait_ge(s_ps, b * NG + n + 1)
                        if n >= 2:
                            dve.wait_ge(p_ready, b * NG + n - 1)
                        for t in range(TT):
                            last = nc.vector.tensor_reduce(nm[:, n % 2, t, :], S[n % 2][:, :, t * P:t * P + (t + 1) * P],
                                                           AX.X, ALU.max, negate=True)
                        last.then_inc(nm_ready, 1)

                    def out_of_psum(n):
                        for i in range(2):
                            dve.wait_ge(pt_ps, b * 2 * NG + 2 * n + i + 1)
                            if n >= 2:
                                dve.wait_ge(av_ps, b * NG + n - 1)
                            nc.vector.tensor_copy(pt[:, n % 2, i, :], PT[i][:, 0:3 * P]).then_inc(pt_ready, 1)

                    for n in range(NG + 1):
                        if n < NG:
                            maxima(n)
                        if n >= 1:
                            out_of_psum(n - 1)
                    dve.wait_ge(av_ps, b * NG + NG)
                    st.inc(nc.vector.reciprocal(rec[:, :, :], O[:, :, :, HD]))
                    st.wait()
                    for t in range(TT):
                        last = nc.vector.tensor_tensor(on[:, t, :].rearrange("p (h e) -> p h e", e=HD), O[:, t, :, 0:HD],
                                                       bc(rec[:, t, :], 2, HD), ALU.mult)
                    last.then_inc(on_ready, 1)
                    layernorm_tail(nc, st, x_sb, b * TT, TT, PT[1].rearrange("p (t n) -> p t n", t=TT),
                                   lambda: dve.wait_ge(y_ps, b + 1), lw)
                    st.end()



def l0_ffn(nc, c, x_sb, w, psum):
    E, G, EG, LAT, SH = 32, 4, 8, 128, 512
    with ExitStack() as ctx:
        sb = lambda name, shape, dt=F32: ctx.enter_context(nc.sbuf_tensor("l0f_" + name, shape, dt))
        sem = lambda name: ctx.enter_context(nc.semaphore("l0f_" + name))
        xs = sb("xs", [P, CH, D])
        xT = sb("xT", [P, KD, CN])
        xl = sb("xl", [LAT, CN])
        relu = sb("relu", [P, 2, CN])
        sq = sb("sq", [P, 2, CN])
        hg = sb("hg", [P, 2, CN])
        hs = sb("hs", [P, SH // P, CN])
        yl = sb("yl", [LAT, CN])
        ex = sb("ex", [P, CH, E])
        sc = sb("sc", [P, CH, E])
        cand = sb("cand", [P, CH, E])
        left = sb("left", [P, CH, E])
        top = sb("top", [P, CH * G, 8])
        garr = sb("garr", [P, CH, 14])
        gpick = sb("gpick", [P, CH, 8])
        gtop = sb("gtop", [P, CH, 8])
        gout = sb("gout", [P, CH, 10])
        gsel = sb("gsel", [P, CH, G])
        wsum = sb("wsum", [P, CH])
        rest = sb("rest", [P, CH, E])
        c3 = sb("c3", [P, CH, 3, E], BF16)
        c3T = sb("c3T", [3 * E, CN], BF16)
        lw = ln_scratch(sb, CH)
        HB = [psum[:, 0, :], psum[:, 1, :]]
        GB = [psum[:, 2, :], psum[:, 3, :]]
        YL, XL = psum[:, 4, :], psum[:, 5, :]
        Y = psum[:, 6:8, :].rearrange("p a (t n) -> p (a t) n", t=2)

        x_staged = sem("x_staged")
        xT_ps = sem("xT_ps")
        xT_ready = sem("xT_ready")
        logit_ps = sem("logit_ps")
        ex_ready = sem("ex_ready")
        xl_ps = sem("xl_ps")
        xl_ready = sem("xl_ready")
        c3_ready = sem("c3_ready")
        c3T_ps = sem("c3T_ps")
        c3T_ready = sem("c3T_ready")
        h_ps = sem("h_ps")
        sq_ready = sem("sq_ready")
        hg_ready = sem("hg_ready")
        used = sem("used")
        yl_ready = sem("yl_ready")
        y_ps = sem("y_ps")
        relu_ready = sem("relu_ready")
        steps = sem("steps")
        NH = E + SH // P

        with nc.Block() as block:
            @block.sync
            def _(sp):
                with sp.Fori(0, NCH) as b:
                    sp.wait_ge(xT_ps, b + 1)
                    sp.dma_start(xs[:, :, :], x_sb[:, bass.ds(b * CH, CH), :]).then_inc(x_staged, 16)

            @block.tensor
            def _(pe):
                mm = nc.tensor.matmul
                pe.sem_inc(xT_ps, 1)
                with pe.Fori(0, NCH) as b:
                    pe.wait_ge(x_staged, b * 16 + 16)
                    for k in range(KD):
                        for t in range(CH):
                            last = nc.tensor.transpose(HB[k][:, t * P:(t + 1) * P], xs[:, t, k * P:(k + 1) * P], c["id"])
                    last.then_inc(xT_ps, 1)
                    pe.wait_ge(xT_ready, b + 1)
                    for t in range(CH):
                        for k in range(KD):
                            last = mm(GB[0][:, t * E:(t + 1) * E], xT[:, k, t * P:(t + 1) * P], w["gate"][:, k, :],
                                      start=(k == 0), stop=(k == KD - 1))
                    last.then_inc(logit_ps, 1)
                    for k in range(KD):
                        last = mm(XL, w["fc1"][:, k, :], xT[:, k, :], start=(k == 0), stop=(k == KD - 1))
                    last.then_inc(xl_ps, 1)

                    def hidden(e):
                        if e >= 2:
                            pe.wait_ge(sq_ready, b * NH + e - 1)
                        if e < E:
                            if e == 0:
                                pe.wait_ge(xl_ready, b + 1)
                                pe.wait_ge(c3T_ready, b + 1)
                            if e >= 2:
                                pe.wait_ge(hg_ready, b * E + e - 1)
                            mm(GB[e % 2], c["sel0"][:, e * P:(e + 1) * P], c3T[:, :], start=True, stop=True)
                            mm(HB[e % 2], w["w1"][:, e, :], xl[:, :], start=True, stop=True).then_inc(h_ps, 1)
                        else:
                            m = e - E
                            for k in range(KD):
                                last = mm(HB[e % 2], w["up"][:, k, m * P:(m + 1) * P], xT[:, k, :], start=(k == 0), stop=(k == KD - 1))
                            last.then_inc(h_ps, 1)

                    def latent(e):
                        pe.wait_ge(hg_ready, b * E + e + 1)
                        mm(YL, w["w2"][:, e, :], hg[:, e % 2, :], start=(e == 0), stop=(e == E - 1)).then_inc(used, 1)

                    pe.wait_ge(c3_ready, b + 1)
                    for t in range(CH):
                        last = nc.tensor.transpose(GB[1].bitcast(BF16)[0:3 * E, t * P:(t + 1) * P],
                                                   c3[:, t, :, :].rearrange("p a e -> p (a e)"), c["idb"])
                    last.then_inc(c3T_ps, 1)
                    for e in range(NH):
                        hidden(e)
                        if 2 <= e < E + 2:
                            latent(e - 2)
                    pe.wait_ge(yl_ready, b + 1)
                    pe.wait_ge(sq_ready, b * NH + NH)
                    for t in range(CH):
                        for m in range(SH // P):
                            mm(Y[:, t, :], hs[:, m, t * P:(t + 1) * P], w["down"][:, m, :], start=(m == 0), stop=False)
                        last = mm(Y[:, t, :], yl[:, t * P:(t + 1) * P], w["fc2"][:, :], start=False, stop=True)
                    last.then_inc(y_ps, 1)

            @block.scalar
            def _(act):
                nc.scalar.preload_act_table(ACT.Exp)
                with act.Fori(0, NCH) as b:
                    act.wait_ge(xT_ps, b + 2)
                    for k in range(KD):
                        last = nc.scalar.activation(xT[:, k, :], HB[k], ACT.Copy)
                    last.then_inc(xT_ready, 1)
                    act.wait_ge(logit_ps, b + 1)
                    nc.scalar.activation(ex[:, :, :], GB[0][:, 0:CH * E].rearrange("p (t e) -> p t e", t=CH), ACT.Exp,
                                         scale=-1.0).then_inc(ex_ready, 1)
                    act.wait_ge(xl_ps, b + 1)
                    nc.scalar.activation(xl[:, :], XL, ACT.Copy).then_inc(xl_ready, 1)
                    for e in range(NH):
                        act.wait_ge(h_ps, b * NH + e + 1)
                        if 2 <= e < E:
                            act.wait_ge(hg_ready, b * E + e - 1)
                        nc.scalar.activation(relu[:, e % 2, :], HB[e % 2], ACT.Relu).then_inc(relu_ready, 1)
                        act.wait_ge(relu_ready, b * NH + e + 1)
                        dst = sq[:, e % 2, :] if e < E else hs[:, e - E, :]
                        nc.scalar.activation(dst, relu[:, e % 2, :], ACT.Square).then_inc(sq_ready, 1)

            @block.vector
            def _(dve):
                st = Steps(dve, steps, L0F_STEPS)
                nc.vector.memset(garr[:, :, 0:4], LOW)
                nc.vector.memset(garr[:, :, 8:14], BIG)
                nc.vector.memset(gpick[:, :, :], BIG)
                with dve.Fori(0, NCH) as b:
                    st.begin(b)
                    dve.wait_ge(ex_ready, b + 1)
                    st.do(nc.vector.tensor_scalar(ex[:, :, :], ex[:, :, :], 1.0, None, ALU.add))
                    st.do(nc.vector.reciprocal(sc[:, :, :], ex[:, :, :]))
                    st.do(nc.vector.tensor_tensor(cand[:, :, :], sc[:, :, :], bc(w["bias"][:, :], 1, CH), ALU.add))
                    carry(nc, lw)
                    for j in range(CH * G):
                        last = nc.vector.max(top[:, j, :], cand[:, j // G, (j % G) * EG:(j % G + 1) * EG])
                    st.do(last)
                    st.do(nc.vector.tensor_tensor(garr[:, :, 4:8], top[:, :, 0].rearrange("p (t g) -> p t g", g=G),
                                                  top[:, :, 1].rearrange("p (t g) -> p t g", g=G), ALU.add))
                    carry(nc, lw)
                    for t in range(CH):
                        last = nc.vector.max(gtop[:, t, :], garr[:, t, 0:8])
                    st.do(last)
                    st.do(nc.vector.tensor_copy(gpick[:, :, 0:2], gtop[:, :, 0:2]))
                    carry(nc, lw)
                    for t in range(CH):
                        last = nc.vector.match_replace(gout[:, t, :], gpick[:, t, :], garr[:, t, 4:14], -BIG)
                    st.do(last)
                    st.do(nc.vector.tensor_scalar(gsel[:, :, :], gout[:, :, 0:4], -BIG, None, ALU.is_equal))
                    st.do(nc.vector.tensor_scalar(gsel[:, :, :], gsel[:, :, :], -NEG, NEG, ALU.mult, ALU.add))
                    st.do(nc.vector.tensor_tensor(cand[:, :, :].rearrange("p t (g e) -> p (t g) e", g=G),
                                                  cand[:, :, :].rearrange("p t (g e) -> p (t g) e", g=G),
                                                  bc(gsel[:, :, :].rearrange("p t g -> p (t g)"), 2, EG), ALU.add))
                    carry(nc, lw)
                    for t in range(CH):
                        last = nc.vector.max(gtop[:, t, :], cand[:, t, :])
                    st.do(last)
                    carry(nc, lw)
                    for t in range(CH):
                        last = nc.vector.match_replace(left[:, t, :], gtop[:, t, :], cand[:, t, :], -BIG)
                    st.do(last)
                    st.do(nc.vector.scalar_tensor_tensor(left[:, :, :], left[:, :, :], -BIG, sc[:, :, :], ALU.is_equal, ALU.mult))
                    st.do(nc.vector.tensor_reduce(wsum[:, :], left[:, :, :], AX.X, ALU.add))
                    st.do(nc.vector.reciprocal(wsum[:, :], wsum[:, :]))
                    st.do(nc.vector.scalar_tensor_tensor(left[:, :, :], left[:, :, :], 2.5, bc(wsum[:, :], 2, E), ALU.mult, ALU.mult))
                    split3(nc, st, left[:, :, :], [c3[:, :, j, :] for j in range(3)], rest[:, :, :])
                    nc.vector.memset(lw["carrier"][:, :], 0.0).then_inc(c3_ready, 1)
                    dve.wait_ge(c3T_ps, b + 1)
                    nc.vector.tensor_copy(c3T[:, :], GB[1].bitcast(BF16)[0:3 * E, 0:CN]).then_inc(c3T_ready, 1)
                    for e in range(E):
                        dve.wait_ge(sq_ready, b * NH + e + 1)
                        if e >= 2:
                            dve.wait_ge(used, b * E + e - 1)
                        nc.vector.tensor_tensor(hg[:, e % 2, :], sq[:, e % 2, :], GB[e % 2], ALU.mult).then_inc(hg_ready, 1)
                    dve.wait_ge(used, b * E + E)
                    nc.vector.tensor_copy(yl[:, :], YL).then_inc(yl_ready, 1)
                    layernorm_tail(nc, st, x_sb, b * CH, CH, Y, lambda: dve.wait_ge(y_ps, b + 1), lw)
                    st.end()


L0F_STEPS = 17 + 5 + LN_STEPS



def l1_attention(nc, c, x_sb, w, psum):
    H, HD = 16, 128
    EPS = 1e-5
    NJ = 8
    NG = H // 2
    with ExitStack() as ctx:
        sb = lambda name, shape, dt=F32: ctx.enter_context(nc.sbuf_tensor("l1a_" + name, shape, dt))
        sem = lambda name: ctx.enter_context(nc.semaphore("l1a_" + name))
        xs = sb("xs", [P, TT, D])
        xT = sb("xT", [P, KD, T])
        qT = sb("qT", [HD, H, T])
        kT = sb("kT", [HD, H, T])
        va = sb("va", [P, TT, H * HD])
        ko = sb("ko", [P, H * T])
        kn = ko[:, :].rearrange("p (t h d) -> p (t h) d", t=TT, h=H)
        oT = ko[:, :].rearrange("p (h t) -> p h t", h=H)
        ksq = sb("ksq", [P, 2, 512])
        qsq = sb("qsq", [P, 2, 512])
        pr = sb("pr", [P, 2, 2, 3 * P])
        pt = sb("pt", [P, 2, 2, 3 * P])
        gain = sb("gain", [P, 1])
        ssk = sb("ssk", [P, TT * H])
        rk = sb("rk", [P, TT * H])
        rq = sb("rq", [P, TT, H])
        vv = sb("vv", [P, TT * H])
        tmp = sb("tmp", [P, TT * H])
        nm = sb("nm", [P, 2, TT, 2])
        nb = sb("nb", [P, 2, TT, 2])
        sums = sb("sums", [P, 2, TT, 2])
        rec = sb("rec", [P, 2, TT, 2])
        lw = ln_scratch(sb, TT)
        bank = lambda i: psum[:, i, :]
        S = [psum[:, 0:2, :], psum[:, 2:4, :]]
        PT = [bank(4), bank(5)]

        x_staged = sem("x_staged")
        xT_ps = sem("xT_ps")
        xT_ready = sem("xT_ready")
        k_ps = sem("k_ps")
        q_ps = sem("q_ps")
        v_ps = sem("v_ps")
        k_out = sem("k_out")
        q_sq = sem("q_sq")
        q_out = sem("q_out")
        v_out = sem("v_out")
        k_sum = sem("k_sum")
        ssq_ps = sem("ssq_ps")
        kn_ready = sem("kn_ready")
        kT_ps = sem("kT_ps")
        kT_ready = sem("kT_ready")
        s_ps = sem("s_ps")
        nb_ready = sem("nb_ready")
        p_exp = sem("p_exp")
        p_norm = sem("p_norm")
        pt_ps = sem("pt_ps")
        pt_ready = sem("pt_ready")
        av_ps = sem("av_ps")
        o_ready = sem("o_ready")
        y_ps = sem("y_ps")
        steps = sem("steps")

        with nc.Block() as block:
            @block.sync
            def _(sp):
                with sp.Fori(0, B) as b:
                    sp.wait_ge(xT_ps, b + 1)
                    sp.dma_start(xs[:, :, :], x_sb[:, bass.ds(b * TT, TT), :]).then_inc(x_staged, 16)

            @block.tensor
            def _(pe):
                mm = nc.tensor.matmul
                pe.sem_inc(xT_ps, 1)
                with pe.Fori(0, B) as b:
                    pe.wait_ge(x_staged, b * 16 + 16)
                    for k in range(KD):
                        for t in range(TT):
                            last = nc.tensor.transpose(PT[1][:, (k * TT + t) * P:(k * TT + t + 1) * P],
                                                       xs[:, t, k * P:(k + 1) * P], c["id"])
                    last.then_inc(xT_ps, 1)
                    pe.wait_ge(xT_ready, b + 1)

                    def square_sums(j):
                        pe.wait_ge(q_sq, b * NJ + j + 1)
                        pe.wait_ge(q_out, b * NJ + 1)
                        for i in range(2):
                            for t in range(TT):
                                h = 2 * j + i
                                last = mm(bank(4)[:, t * H + h:t * H + h + 1], qsq[:, j % 2, i * T + t * P:i * T + (t + 1) * P],
                                          c["one"], start=True, stop=True)
                        last.then_inc(ssq_ps, 1)

                    for j in range(NJ):
                        t, cols = j // 4, slice((j % 4) * 512, (j % 4 + 1) * 512)
                        if j >= 2:
                            pe.wait_ge(k_out, b * NJ + j - 1)
                        for k in range(KD):
                            last = mm(bank(j % 2), xT[:, k, t * P:(t + 1) * P], w["k"][:, k, cols], start=(k == 0), stop=(k == KD - 1))
                        last.then_inc(k_ps, 1)
                        if j >= 2:
                            pe.wait_ge(q_out, b * NJ + j - 1)
                        for i in range(2):
                            for k in range(KD):
                                last = mm(bank(2 + j % 2)[:, i * T:(i + 1) * T], w["q"][:, k, (2 * j + i) * HD:(2 * j + i + 1) * HD],
                                          xT[:, k, :], start=(k == 0), stop=(k == KD - 1))
                        last.then_inc(q_ps, 1)
                        if j >= 2:
                            pe.wait_ge(v_out, b * NJ + j - 1)
                        for k in range(KD):
                            last = mm(bank(6 + j % 2), xT[:, k, t * P:(t + 1) * P], w["v"][:, k, cols], start=(k == 0), stop=(k == KD - 1))
                        last.then_inc(v_ps, 1)
                        if j >= 1:
                            square_sums(j - 1)
                    square_sums(NJ - 1)
                    pe.wait_ge(kn_ready, b + 1)
                    pe.wait_ge(q_out, b * NJ + NJ)
                    for m in range(NG):
                        if m >= 4:
                            pe.wait_ge(kT_ready, b * NG + m - 3)
                        for i in range(2):
                            for t in range(TT):
                                last = nc.tensor.transpose(bank(m % 4)[:, i * T + t * P:i * T + (t + 1) * P],
                                                           kn[:, t * H + 2 * m + i, :], c["id"])
                        last.then_inc(kT_ps, 1)

                    def scores(n):
                        if n < 2:
                            pe.wait_ge(kT_ready, b * NG + NG)
                        else:
                            pe.wait_ge(p_exp, b * NG + n - 1)
                        for i in range(2):
                            h = 2 * n + i
                            for t in range(TT):
                                mm(S[n % 2][:, i, t * P:t * P + (t + 1) * P], qT[:, h, t * P:(t + 1) * P], kT[:, h, 0:(t + 1) * P],
                                   start=True, stop=False)
                                last = mm(S[n % 2][:, i, 2 * t * P:(2 * t + 1) * P], c["idb"], c["maskb"], start=False, stop=True)
                        last.then_inc(s_ps, 1)

                    def turn(n):
                        pe.wait_ge(p_norm, b * NG + n + 1)
                        for i in range(2):
                            if n > 0:
                                pe.wait_ge(pt_ready, b * 2 * NG + 2 * (n - 1) + i + 1)
                            for j in range(3):
                                last = nc.tensor.transpose(PT[i][:, j * P:(j + 1) * P], pr[:, n % 2, i, j * P:(j + 1) * P], c["id"])
                            last.then_inc(pt_ps, 1)

                    def values(n):
                        if n >= 2:
                            pe.wait_ge(o_ready, b * NG + n - 1)
                        for i in range(2):
                            h = 2 * n + i
                            pe.wait_ge(pt_ready, b * 2 * NG + 2 * n + i + 1)
                            pp, o = pt[:, n % 2, i, :], bank(6 + n % 2)[:, i * T:(i + 1) * T]
                            mm(o, va[:, 0, h * HD:(h + 1) * HD], pp[:, 0:2 * P], start=True, stop=False)
                            last = mm(o[:, P:2 * P], va[:, 1, h * HD:(h + 1) * HD], pp[:, 2 * P:3 * P], start=False, stop=True)
                        last.then_inc(av_ps, 1)

                    for n in range(NG + 2):
                        if n < NG:
                            scores(n)
                        if 1 <= n <= NG:
                            turn(n - 1)
                        if n >= 2:
                            values(n - 2)
                    pe.wait_ge(o_ready, b * NG + NG)
                    for t in range(TT):
                        for h in range(H):
                            last = mm(PT[0][:, t * D:(t + 1) * D], oT[:, h, t * P:(t + 1) * P], w["o"][:, h, :],
                                      start=(h == 0), stop=(h == H - 1))
                    last.then_inc(y_ps, 1)

            @block.scalar
            def _(act):
                nc.scalar.preload_act_table(ACT.Exp)
                with act.Fori(0, B) as b:
                    act.wait_ge(xT_ps, b + 2)
                    nc.scalar.activation(xT[:, :, :], PT[1].rearrange("p (k t) -> p k t", k=KD), ACT.Copy).then_inc(xT_ready, 1)
                    for j in range(NJ):
                        t, j4 = j // 4, j % 4
                        act.wait_ge(k_ps, b * NJ + j + 1)
                        if j >= 2:
                            act.wait_ge(k_sum, b * NJ + j - 1)
                        nc.scalar.activation(kn[:, t * H + 4 * j4:t * H + 4 * j4 + 4, :],
                                             bank(j % 2).rearrange("p (h d) -> p h d", h=4), ACT.Copy)
                        nc.scalar.activation(ksq[:, j % 2, :], bank(j % 2), ACT.Square).then_inc(k_out, 1)
                        act.wait_ge(q_out, b * NJ + j + 1)
                        if j >= 2:
                            act.wait_ge(ssq_ps, b * NJ + j - 1)
                        nc.scalar.activation(qsq[:, j % 2, :], qT[:, 2 * j:2 * j + 2, :].rearrange("p i t -> p (i t)"), ACT.Square).then_inc(q_sq, 1)
                    for m in range(NG):
                        act.wait_ge(kT_ps, b * NG + m + 1)
                        nc.scalar.activation(kT[:, 2 * m:2 * m + 2, :], bank(m % 4).rearrange("p (i t) -> p i t", i=2), ACT.Copy,
                                             scale=gain[:, :]).then_inc(kT_ready, 1)

                    def out(n):
                        act.wait_ge(av_ps, b * NG + n + 1)
                        nc.scalar.activation(oT[:, 2 * n:2 * n + 2, :], bank(6 + n % 2).rearrange("p (i t) -> p i t", i=2),
                                             ACT.Copy).then_inc(o_ready, 1)

                    for n in range(NG + 2):
                        if n < NG:
                            act.wait_ge(nb_ready, b * NG + n + 1)
                            if n >= 2:
                                act.wait_ge(pt_ps, b * 2 * NG + 2 * (n - 1))
                            for i in range(2):
                                for t in range(TT):
                                    s = slice(t * P, t * P + (t + 1) * P)
                                    last = nc.scalar.activation(pr[:, n % 2, i, s], S[n % 2][:, i, s], ACT.Exp,
                                                                bias=nb[:, n % 2, t, i:i + 1], scale=rq[:, t, 2 * n + i:2 * n + i + 1],
                                                                accum_out=sums[:, n % 2, t, i:i + 1])
                            last.then_inc(p_exp, 1)
                        if n >= 2:
                            out(n - 2)

            @block.vector
            def _(dve):
                st = Steps(dve, steps, L1A_STEPS)
                nc.vector.tensor_tensor(gain[:, :], w["gq"], w["gk"], ALU.mult)
                with dve.Fori(0, B) as b:
                    st.begin(b)
                    for j in range(NJ):
                        t, cols = j // 4, slice((j % 4) * 512, (j % 4 + 1) * 512)
                        dve.wait_ge(q_ps, b * NJ + j + 1)
                        nc.vector.tensor_copy(qT[:, 2 * j:2 * j + 2, :], bank(2 + j % 2).rearrange("p (i t) -> p i t", i=2)).then_inc(q_out, 1)
                        dve.wait_ge(v_ps, b * NJ + j + 1)
                        nc.vector.tensor_copy(va[:, t, cols], bank(6 + j % 2)).then_inc(v_out, 1)
                        dve.wait_ge(k_out, b * NJ + j + 1)
                        nc.vector.tensor_reduce(ssk[:, 4 * j:4 * j + 4], ksq[:, j % 2, :].rearrange("p (h d) -> p h d", h=4),
                                                AX.X, ALU.add).then_inc(k_sum, 1)
                    dve.wait_ge(k_sum, b * NJ + NJ)
                    st.do(nc.vector.tensor_scalar(vv[:, :], ssk[:, :], 1.0 / HD, EPS, ALU.mult, ALU.add))
                    newton_rsqrt(nc, st, vv[:, :], rk[:, :], tmp[:, :])
                    st.wait()
                    nc.vector.tensor_tensor(kn, kn, bc(rk[:, :], 2, HD), ALU.mult).then_inc(kn_ready, 1)
                    dve.wait_ge(ssq_ps, b * NJ + NJ)
                    st.do(nc.vector.tensor_scalar(vv[:, :], bank(4)[:, 0:TT * H], 1.0 / HD, EPS, ALU.mult, ALU.add))
                    flat = rq[:, :, :].rearrange("p t h -> p (t h)")
                    newton_rsqrt(nc, st, vv[:, :], flat, tmp[:, :])
                    st.wait()
                    st.do(nc.vector.tensor_scalar(flat, flat, float(HD) ** -0.5, None, ALU.mult))

                    def maxima(n):
                        dve.wait_ge(s_ps, b * NG + n + 1)
                        if n >= 2:
                            dve.wait_ge(p_exp, b * NG + n - 1)
                        for t in range(TT):
                            last = nc.vector.tensor_reduce(nm[:, n % 2, t, :], S[n % 2][:, :, t * P:t * P + (t + 1) * P],
                                                           AX.X, ALU.max, negate=True)
                        st.do(last)
                        nc.vector.tensor_tensor(nb[:, n % 2, :, :], nm[:, n % 2, :, :], rq[:, :, 2 * n:2 * n + 2], ALU.mult).then_inc(nb_ready, 1)

                    def normalise(n):
                        dve.wait_ge(p_exp, b * NG + n + 1)
                        st.do(nc.vector.reciprocal(rec[:, n % 2, :, :], sums[:, n % 2, :, :]))
                        for i in range(2):
                            for t in range(TT):
                                s = slice(t * P, t * P + (t + 1) * P)
                                last = nc.vector.tensor_scalar(pr[:, n % 2, i, s], pr[:, n % 2, i, s], rec[:, n % 2, t, i:i + 1], None, ALU.mult)
                        last.then_inc(p_norm, 1)

                    def out_of_psum(n):
                        for i in range(2):
                            dve.wait_ge(pt_ps, b * 2 * NG + 2 * n + i + 1)
                            if n >= 2:
                                dve.wait_ge(av_ps, b * NG + n - 1)
                            nc.vector.tensor_copy(pt[:, n % 2, i, :], PT[i][:, 0:3 * P]).then_inc(pt_ready, 1)

                    for n in range(NG + 1):
                        if n < NG:
                            maxima(n)
                        if n >= 1:
                            out_of_psum(n - 1)
                        if n < NG:
                            normalise(n)
                    layernorm_tail(nc, st, x_sb, b * TT, TT, PT[0].rearrange("p (t n) -> p t n", t=TT),
                                   lambda: dve.wait_ge(y_ps, b + 1), lw)
                    st.end()


L1A_STEPS = 1 + NEWTON_STEPS + 1 + NEWTON_STEPS + 1 + 2 * 8 + LN_STEPS



def l1_ffn(nc, c, x_sb, w, psum):
    E, K, I, TOP, SH = 128, 8, 128, 4, 2
    EPS = 1e-8
    NH = K + SH
    with ExitStack() as ctx:
        sb = lambda name, shape, dt=F32: ctx.enter_context(nc.sbuf_tensor("l1f_" + name, shape, dt))
        sem = lambda name: ctx.enter_context(nc.semaphore("l1f_" + name))
        xs = sb("xs", [P, CH, D])
        xT = sb("xT", [P, KD, CN])
        mp = sb("mp", [P, K, 2])
        mix = sb("mix", [P, K])
        msum = sb("msum", [P, 1])
        mixb = sb("mixb", [P, K, I])
        pb = sb("pb", [P, CH, E + 8 - TOP])
        nm = sb("nm", [P, CH])
        sums = sb("sums", [P, CH])
        top = sb("top", [P, CH, 8])
        pick = sb("pick", [P, CH, 8])
        left = sb("left", [P, CH, E + 8 - TOP])
        co = sb("co", [P, CH, E])
        wsum = sb("wsum", [P, CH])
        coT = sb("coT", [E, CN])
        sg = sb("sg", [P, 2, CN])
        gu = sb("gu", [P, 2, CN])
        t2 = sb("t2", [P, 2, CN])
        acc = sb("acc", [I, CN])
        hs = sb("hs", [P, SH, CN])
        lw = ln_scratch(sb, CH)
        bank = lambda i: psum[:, i, :]
        GB, UB, CB = [bank(0), bank(1)], [bank(2), bank(3)], [bank(4), bank(5)]
        Y = psum[:, 6:8, :].rearrange("p a (t n) -> p (a t) n", t=2)

        x_staged = sem("x_staged")
        xT_ps = sem("xT_ps")
        xT_ready = sem("xT_ready")
        logit_ps = sem("logit_ps")
        nm_ready = sem("nm_ready")
        ex_ready = sem("ex_ready")
        co_ready = sem("co_ready")
        coT_ps = sem("coT_ps")
        coT_ready = sem("coT_ready")
        mix_ready = sem("mix_ready")
        h_ps = sem("h_ps")
        sg_ready = sem("sg_ready")
        gu_ready = sem("gu_ready")
        t2_ready = sem("t2_ready")
        acc_ready = sem("acc_ready")
        y_ps = sem("y_ps")
        mix_steps = sem("mix_steps")
        steps = sem("steps")

        with nc.Block() as block:
            @block.sync
            def _(sp):
                with sp.Fori(0, NCH) as b:
                    sp.wait_ge(xT_ps, b + 1)
                    sp.dma_start(xs[:, :, :], x_sb[:, bass.ds(b * CH, CH), :]).then_inc(x_staged, 16)

            @block.tensor
            def _(pe):
                mm = nc.tensor.matmul
                pe.sem_inc(xT_ps, 1)
                pe.wait_ge(mix_ready, 1)
                with pe.Fori(0, NCH) as b:
                    pe.wait_ge(x_staged, b * 16 + 16)
                    for k in range(KD):
                        for t in range(CH):
                            last = nc.tensor.transpose(GB[k][:, t * P:(t + 1) * P], xs[:, t, k * P:(k + 1) * P], c["id"])
                    last.then_inc(xT_ps, 1)
                    pe.wait_ge(xT_ready, b + 1)
                    for t in range(CH):
                        for k in range(KD):
                            last = mm(UB[0][:, t * E:(t + 1) * E], xT[:, k, t * P:(t + 1) * P], w["router"][:, k, :],
                                      start=(k == 0), stop=(k == KD - 1))
                    last.then_inc(logit_ps, 1)
                    pe.wait_ge(co_ready, b + 1)
                    for t in range(CH):
                        last = nc.tensor.transpose(UB[1][:, t * P:(t + 1) * P], co[:, t, :], c["id"])
                    last.then_inc(coT_ps, 1)
                    pe.wait_ge(coT_ready, b + 1)
                    for e in range(NH):
                        if e >= 2:
                            pe.wait_ge(gu_ready, b * NH + e - 1)
                        wg, wu, m = ("gate", "up", e) if e < K else ("sgate", "sup", e - K)
                        for k in range(KD):
                            mm(GB[e % 2], w[wg][:, k, m * I:(m + 1) * I], xT[:, k, :], start=(k == 0), stop=(k == KD - 1))
                        for k in range(KD):
                            last = mm(UB[e % 2], w[wu][:, k, m * I:(m + 1) * I], xT[:, k, :], start=(k == 0), stop=(k == KD - 1))
                        if e < K:
                            if e >= 2:
                                pe.wait_ge(t2_ready, b * K + e - 1)
                            last = mm(CB[e % 2], mixb[:, e, :], coT[:, :], start=True, stop=True)
                        last.then_inc(h_ps, 1)
                    pe.wait_ge(gu_ready, b * NH + NH)
                    pe.wait_ge(acc_ready, b * (K - 1) + K - 1)
                    for t in range(CH):
                        for m in range(SH):
                            mm(Y[:, t, :], hs[:, m, t * P:(t + 1) * P], w["sdown"][:, m, :], start=(m == 0), stop=False)
                        last = mm(Y[:, t, :], acc[:, t * P:(t + 1) * P], w["down"], start=False, stop=True)
                    last.then_inc(y_ps, 1)

            @block.scalar
            def _(act):
                with act.Fori(0, NCH) as b:
                    act.wait_ge(xT_ps, b + 2)
                    for k in range(KD):
                        last = nc.scalar.activation(xT[:, k, :], GB[k], ACT.Copy)
                    last.then_inc(xT_ready, 1)
                    act.wait_ge(nm_ready, b + 1)
                    for t in range(CH):
                        last = nc.scalar.activation(pb[:, t, 0:E], UB[0][:, t * E:(t + 1) * E], ACT.Exp, bias=nm[:, t:t + 1],
                                                    accum_out=sums[:, t:t + 1])
                    last.then_inc(ex_ready, 1)
                    for e in range(NH):
                        act.wait_ge(h_ps, b * NH + e + 1)
                        if e >= 2:
                            act.wait_ge(gu_ready, b * NH + e - 1)
                        nc.scalar.activation(sg[:, e % 2, :], GB[e % 2], ACT.Silu).then_inc(sg_ready, 1)

            @block.gpsimd
            def _(pool):
                with pool.Fori(0, NCH) as b:
                    for k in range(1, K):
                        pool.wait_ge(t2_ready, b * K + k + 1)
                        if k == 1:
                            pool.wait_ge(y_ps, b + 1)
                        else:
                            pool.wait_ge(acc_ready, b * (K - 1) + k - 1)
                        nc.gpsimd.tensor_tensor(acc[:, :], t2[:, 0, :] if k == 1 else acc[:, :], t2[:, k % 2, :], ALU.add).then_inc(acc_ready, 1)

            @block.vector
            def _(dve):
                st = Steps(dve, steps, L1F_STEPS)
                dve.sem_inc(y_ps, 1)
                one = lambda ins, n: (ins.then_inc(mix_steps, 1), dve.wait_ge(mix_steps, n))
                one(nc.vector.tensor_tensor(mp[:, :, :], w["amp"], w["amp"], ALU.mult), 1)
                one(nc.vector.tensor_tensor(mix[:, :], mp[:, :, 0], mp[:, :, 1], ALU.add), 2)
                one(nc.vector.tensor_reduce(msum[:, :], mix[:, :], AX.X, ALU.add), 3)
                one(nc.vector.tensor_scalar(msum[:, :], msum[:, :], EPS, None, ALU.add), 4)
                one(nc.vector.reciprocal(msum[:, :], msum[:, :]), 5)
                one(nc.vector.tensor_scalar(mix[:, :], mix[:, :], msum[:, :], w["escale"], ALU.mult, ALU.mult), 6)
                nc.vector.tensor_copy(mixb[:, :, :], bc(mix[:, :], 2, I)).then_inc(mix_ready, 1)
                nc.vector.memset(pb[:, :, E:], BIG)
                nc.vector.memset(pick[:, :, :], BIG)
                with dve.Fori(0, NCH) as b:
                    st.begin(b)
                    dve.wait_ge(logit_ps, b + 1)
                    nc.vector.tensor_reduce(nm[:, :], UB[0].rearrange("p (t e) -> p t e", t=CH), AX.X, ALU.max, negate=True).then_inc(nm_ready, 1)
                    dve.wait_ge(ex_ready, b + 1)
                    st.do(nc.vector.reciprocal(wsum[:, :], sums[:, :]))
                    st.do(nc.vector.tensor_tensor(pb[:, :, 0:E], pb[:, :, 0:E], bc(wsum[:, :], 2, E), ALU.mult))
                    carry(nc, lw)
                    for t in range(CH):
                        last = nc.vector.max(top[:, t, :], pb[:, t, 0:E])
                    st.do(last)
                    st.do(nc.vector.tensor_copy(pick[:, :, 0:TOP], top[:, :, 0:TOP]))
                    carry(nc, lw)
                    for t in range(CH):
                        last = nc.vector.match_replace(left[:, t, :], pick[:, t, :], pb[:, t, :], -BIG)
                    st.do(last)
                    st.do(nc.vector.scalar_tensor_tensor(co[:, :, :], left[:, :, 0:E], -BIG, pb[:, :, 0:E], ALU.is_equal, ALU.mult))
                    st.do(nc.vector.tensor_reduce(wsum[:, :], co[:, :, :], AX.X, ALU.add))
                    st.do(nc.vector.tensor_scalar(wsum[:, :], wsum[:, :], EPS, None, ALU.add))
                    st.do(nc.vector.reciprocal(wsum[:, :], wsum[:, :]))
                    nc.vector.tensor_tensor(co[:, :, :], co[:, :, :], bc(wsum[:, :], 2, E), ALU.mult).then_inc(co_ready, 1)
                    dve.wait_ge(coT_ps, b + 1)
                    nc.vector.tensor_copy(coT[:, :], UB[1]).then_inc(coT_ready, 1)

                    def weigh(k):
                        dve.wait_ge(gu_ready, b * NH + k + 1)
                        if k >= 2:
                            dve.wait_ge(acc_ready, b * (K - 1) + max(k - 2, 1))
                        nc.vector.tensor_tensor(t2[:, k % 2, :], gu[:, k % 2, :], CB[k % 2], ALU.mult).then_inc(t2_ready, 1)

                    for e in range(NH):
                        dve.wait_ge(sg_ready, b * NH + e + 1)
                        dst = gu[:, e % 2, :] if e < K else hs[:, e - K, :]
                        nc.vector.tensor_tensor(dst, sg[:, e % 2, :], UB[e % 2], ALU.mult).then_inc(gu_ready, 1)
                        if 1 <= e <= K:
                            weigh(e - 1)
                    layernorm_tail(nc, st, x_sb, b * CH, CH, Y, lambda: dve.wait_ge(y_ps, b + 2), lw)
                    st.end()


L1F_STEPS = 9 + LN_STEPS



def l2_mixing(nc, c, x_sb, w, psum):
    R, DH = 256, 64
    with ExitStack() as ctx:
        sb = lambda name, shape, dt=F32: ctx.enter_context(nc.sbuf_tensor("l2a_" + name, shape, dt))
        sem = lambda name: ctx.enter_context(nc.semaphore("l2a_" + name))
        xs = sb("xs", [P, TT, D])
        xT = sb("xT", [P, KD, T + 2])
        hT = sb("hT", [DH, T])
        ga = sb("ga", [P, 2, T])
        ug = sb("ug", [P, 2, T])
        vg = sb("vg", [P, 2, T])
        cum = sb("cum", [P, 2, T])
        go = sb("go", [P, 2, T])
        tc = sb("tc", [P, KD, T])
        ones = sb("ones", [P, T])
        lw = ln_scratch(sb, TT)
        bank = lambda i: psum[:, i, :]
        two = lambda ap: ap.rearrange("p (k t) -> p k t", k=2)

        x_staged = sem("x_staged")
        xT_ps = sem("xT_ps")
        xT_ready = sem("xT_ready")
        h_ps = sem("h_ps")
        h_ready = sem("h_ready")
        uv_ps = sem("uv_ps")
        g_ps = sem("g_ps")
        ga_ready = sem("ga_ready")
        mix_ready = sem("mix_ready")
        y_ps = sem("y_ps")
        steps = sem("steps")

        with nc.Block() as block:
            @block.sync
            def _(sp):
                with sp.Fori(0, B) as b:
                    sp.wait_ge(xT_ps, b + 1)
                    sp.dma_start(xs[:, :, :], x_sb[:, bass.ds(b * TT, TT), :]).then_inc(x_staged, 16)

            @block.tensor
            def _(pe):
                mm = nc.tensor.matmul
                pe.sem_inc(xT_ps, 1)
                with pe.Fori(0, B) as b:
                    pe.wait_ge(x_staged, b * 16 + 16)
                    for k in range(KD):
                        for t in range(TT):
                            last = nc.tensor.transpose(bank(0)[:, (k * TT + t) * P:(k * TT + t + 1) * P],
                                                       xs[:, t, k * P:(k + 1) * P], c["id"])
                    last.then_inc(xT_ps, 1)
                    pe.wait_ge(xT_ready, b + 1)
                    for k in range(KD):
                        last = mm(bank(1)[0:DH, 0:T], w["g1"][:, k, :], xT[:, k, 1:T + 1], start=(k == 0), stop=(k == KD - 1))
                    last.then_inc(h_ps, 1)
                    for name, bk in (("u", 2), ("v", 3)):
                        for m in range(2):
                            for k in range(KD):
                                last = mm(bank(bk)[:, m * T:(m + 1) * T], w[name][:, k, m * P:(m + 1) * P], xT[:, k, 1:T + 1],
                                          start=(k == 0), stop=(k == KD - 1))
                    last.then_inc(uv_ps, 1)
                    pe.wait_ge(h_ready, b + 1)
                    for m in range(2):
                        last = mm(bank(4)[:, m * T:(m + 1) * T], w["g2"][0:DH, m * P:(m + 1) * P], hT[:, :], start=True, stop=True)
                    last.then_inc(g_ps, 1)
                    pe.wait_ge(mix_ready, b + 2)
                    for t in range(TT):
                        y = bank(5)[:, t * D:(t + 1) * D]
                        for k in range(2):
                            mm(y, go[:, k, t * P:(t + 1) * P], w["u"][:, k, :], start=(k == 0), stop=False)
                        for k in range(KD):
                            last = mm(y[:, k * P:(k + 1) * P], tc[:, k, t * P:(t + 1) * P], c["id"], start=False, stop=(k == KD - 1))
                    last.then_inc(y_ps, 1)

            @block.scalar
            def _(act):
                nc.scalar.preload_act_table(ACT.Sigmoid)
                with act.Fori(0, B) as b:
                    act.wait_ge(xT_ps, b + 2)
                    act.wait_ge(mix_ready, b + 1)
                    nc.scalar.activation(xT[:, :, 1:T + 1], two(bank(0)), ACT.Copy).then_inc(xT_ready, 1)
                    act.wait_ge(h_ps, b + 1)
                    nc.scalar.activation(hT[:, :], bank(1)[0:DH, 0:T], ACT.Relu, bias=w["bg1"][0:DH, :]).then_inc(h_ready, 1)
                    act.wait_ge(g_ps, b + 1)
                    for m in range(2):
                        last = nc.scalar.activation(ga[:, m, :], bank(4)[:, m * T:(m + 1) * T], ACT.Sigmoid, bias=w["bg2"][:, m:m + 1])
                    last.then_inc(ga_ready, 1)

            @block.vector
            def _(dve):
                st = Steps(dve, steps, L2A_STEPS)
                nc.vector.memset(ones[:, :], 1.0)
                nc.vector.memset(xT[:, :, 0:1], 0.0)
                nc.vector.memset(xT[:, :, T + 1:T + 2], 0.0).then_inc(mix_ready, 1)
                with dve.Fori(0, B) as b:
                    st.begin(b)
                    dve.wait_ge(xT_ready, b + 1)
                    for k in range(KD):
                        last = nc.vector.tensor_scalar(tc[:, k, :], xT[:, k, 0:T], w["conv"][:, k, 0:1], w["convb"][:, k:k + 1], ALU.mult, ALU.add)
                    st.do(last)
                    for j in (1, 2):
                        for k in range(KD):
                            last = nc.vector.scalar_tensor_tensor(tc[:, k, :], xT[:, k, j:j + T], w["conv"][:, k, j:j + 1], tc[:, k, :], ALU.mult, ALU.add)
                        st.do(last)
                    dve.wait_ge(uv_ps, b + 1)
                    dve.wait_ge(ga_ready, b + 1)
                    for m in range(2):
                        nc.vector.scalar_tensor_tensor(ug[:, m, :], bank(2)[:, m * T:(m + 1) * T], w["bu"][:, m:m + 1], ga[:, m, :], ALU.add, ALU.mult)
                        last = nc.vector.scalar_tensor_tensor(vg[:, m, :], bank(3)[:, m * T:(m + 1) * T], w["bv"][:, m:m + 1], ga[:, m, :], ALU.add, ALU.mult)
                    st.do(last)
                    for m in range(2):
                        last = nc.vector.tensor_tensor_scan(cum[:, m, :], ones[:, :], ug[:, m, :], 0.0, ALU.mult, ALU.add)
                    st.do(last)
                    nc.vector.tensor_tensor(go[:, :, :], cum[:, :, :], vg[:, :, :], ALU.mult).then_inc(mix_ready, 1)
                    layernorm_tail(nc, st, x_sb, b * TT, TT, two(bank(5)), lambda: dve.wait_ge(y_ps, b + 1), lw)
                    st.end()


L2A_STEPS = 5 + LN_STEPS



def l2_ffn(nc, c, x_sb, w, psum):
    I, SETS = 1024, 2
    NH = I // P
    with ExitStack() as ctx:
        sb = lambda name, shape, dt=F32: ctx.enter_context(nc.sbuf_tensor("l2f_" + name, shape, dt))
        sem = lambda name: ctx.enter_context(nc.semaphore("l2f_" + name))
        xs = sb("xs", [P, CH, D])
        xT = sb("xT", [P, KD, CN])
        sg = sb("sg", [P, 2, CN])
        hh = sb("hh", [P, SETS, 2, 2, CN])
        ab = sb("ab", [P, 2, 2, CN])
        big = sb("big", [P, 2, CN])
        small = sb("small", [P, 2, CN])
        win = sb("win", [P, 2, 2, CN], BF16)
        both = sb("both", [P, 3, CN], BF16)
        lw = ln_scratch(sb, CH)
        bank = lambda i: psum[:, i, :]
        Y = psum[:, 6:8, :].rearrange("p a (t n) -> p (a t) n", t=2)

        x_staged = sem("x_staged")
        xT_ps = sem("xT_ps")
        xT_ready = sem("xT_ready")
        h_ps = sem("h_ps")
        sg_ready = sem("sg_ready")
        hh_ready = sem("hh_ready")
        ab_ready = sem("ab_ready")
        kept = sem("kept")
        y_ps = sem("y_ps")
        steps = sem("steps")

        with nc.Block() as block:
            @block.sync
            def _(sp):
                with sp.Fori(0, NCH) as b:
                    sp.wait_ge(xT_ps, b + 1)
                    sp.dma_start(xs[:, :, :], x_sb[:, bass.ds(b * CH, CH), :]).then_inc(x_staged, 16)

            @block.tensor
            def _(pe):
                mm = nc.tensor.matmul
                pe.sem_inc(xT_ps, 1)
                with pe.Fori(0, NCH) as b:
                    pe.wait_ge(x_staged, b * 16 + 16)
                    for k in range(KD):
                        for t in range(CH):
                            last = nc.tensor.transpose(bank(4 + k)[:, t * P:(t + 1) * P], xs[:, t, k * P:(k + 1) * P], c["id"])
                    last.then_inc(xT_ps, 1)
                    pe.wait_ge(xT_ready, b + 1)
                    for e in range(NH):
                        if e >= 2:
                            pe.wait_ge(hh_ready, b * NH + e - 1)
                        for name, bk in (("gate", 0), ("up", 2)):
                            for k in range(KD):
                                last = mm(bank(bk + e % 2), w[name][:, k, e * P:(e + 1) * P], xT[:, k, :], start=(k == 0), stop=(k == KD - 1))
                        last.then_inc(h_ps, 1)
                    pe.wait_ge(kept, b * SETS + SETS + 1)
                    for t in range(CH):
                        for e in range(NH):
                            last = mm(Y[:, t, :], hh[:, e // 4, e % 4 // 2, e % 2, t * P:(t + 1) * P], w["down"][:, e, :],
                                      start=(e == 0), stop=(e == NH - 1))
                    last.then_inc(y_ps, 1)

            @block.scalar
            def _(act):
                nc.scalar.preload_act_table(ACT.Silu)
                with act.Fori(0, NCH) as b:
                    act.wait_ge(xT_ps, b + 2)
                    for k in range(KD):
                        last = nc.scalar.activation(xT[:, k, :], bank(4 + k), ACT.Copy)
                    last.then_inc(xT_ready, 1)

                    def magnitudes(s):
                        act.wait_ge(hh_ready, b * NH + 4 * s + 4)
                        act.wait_ge(kept, b * SETS + s + 1)
                        nc.scalar.activation(ab[:, :, :, :], hh[:, s, :, :, :], ACT.Abs).then_inc(ab_ready, 1)

                    for e in range(NH):
                        act.wait_ge(h_ps, b * NH + e + 1)
                        if e >= 2:
                            act.wait_ge(hh_ready, b * NH + e - 1)
                        nc.scalar.activation(sg[:, e % 2, :], bank(e % 2), ACT.Silu).then_inc(sg_ready, 1)
                        if e == 4:
                            magnitudes(0)
                    magnitudes(1)

            @block.vector
            def _(dve):
                st = Steps(dve, steps, L2F_STEPS)
                dve.sem_inc(kept, 1)
                with dve.Fori(0, NCH) as b:
                    st.begin(b)

                    def prune(s):
                        a0, a1 = ab[:, :, 0, :], ab[:, :, 1, :]
                        dve.wait_ge(ab_ready, b * SETS + s + 1)
                        nc.vector.tensor_tensor(big[:, :, :], a0, a1, ALU.max)
                        nc.vector.tensor_tensor(small[:, :, :], a0, a1, ALU.min)
                        nc.vector.tensor_tensor(win[:, :, 0, :], a0, a1, ALU.is_ge)
                        st.do(nc.vector.tensor_tensor(win[:, :, 1, :], a0, a1, ALU.is_lt))
                        nc.vector.tensor_tensor(both[:, 0, :], small[:, 0, :], big[:, 1, :], ALU.is_ge)
                        nc.vector.tensor_tensor(both[:, 1, :], small[:, 1, :], big[:, 0, :], ALU.is_gt)
                        st.do(nc.vector.tensor_tensor(both[:, 2, :], small[:, 0, :], big[:, 1, :], ALU.is_ge))
                        for q in range(2):
                            last = nc.vector.tensor_tensor(win[:, q, :, :], win[:, q, :, :], bc(both[:, q + 1, :], 1, 2), ALU.subtract)
                        st.do(last)
                        for q in range(2):
                            last = nc.vector.tensor_tensor(win[:, q, :, :], win[:, q, :, :], bc(both[:, q, :], 1, 2), ALU.max)
                        st.do(last)
                        nc.vector.tensor_tensor(hh[:, s, :, :, :], hh[:, s, :, :, :], win[:, :, :, :], ALU.mult).then_inc(kept, 1)

                    for e in range(NH):
                        dve.wait_ge(sg_ready, b * NH + e + 1)
                        nc.vector.tensor_tensor(hh[:, e // 4, e % 4 // 2, e % 2, :], sg[:, e % 2, :], bank(2 + e % 2), ALU.mult).then_inc(hh_ready, 1)
                        if e == 5:
                            prune(0)
                    prune(1)
                    layernorm_tail(nc, st, x_sb, b * CH, CH, Y, lambda: dve.wait_ge(y_ps, b + 1), lw)
                    st.end()


L2F_STEPS = 2 * 4 + LN_STEPS



def l3_attention(nc, c, x_sb, w, psum):
    HD, G, R, A = 16, 4, 4, 2
    H = G * R
    V1 = HD + 1
    LAM_INIT = 0.8 - 0.6 * float(np.exp(-0.3 * 0))
    EPS = 1e-8
    NG = H
    with ExitStack() as ctx:
        sb = lambda name, shape, dt=F32: ctx.enter_context(nc.sbuf_tensor("l3a_" + name, shape, dt))
        sem = lambda name: ctx.enter_context(nc.semaphore("l3a_" + name))
        xs = sb("xs", [P, TT, D])
        xT = sb("xT", [P, KD, T])
        qr = sb("qr", [P, A, R, T])
        k1 = sb("k1", [P, A, 2, T])
        kr = sb("kr", [P, A, T])
        va = sb("va", [P, TT, G, V1])
        lam = sb("lam", [P, 2, H])
        lprod = sb("lprod", [P, 2, H, HD])
        nlam = sb("nlam", [P, H])
        gain = sb("gain", [P, HD])
        nm = sb("nm", [P, 2, TT, A])
        sums = sb("sums", [P, 2, TT, A])
        rec = sb("rec", [P, 2, TT, A])
        ratio = sb("ratio", [P, 2, TT])
        pr = sb("pr", [P, 2, A, 3 * P])
        dif = sb("dif", [P, 2, 3 * P])
        nm2 = sb("nm2", [P, 2, TT])
        nb2 = sb("nb2", [P, 2, TT])
        p2 = sb("p2", [P, 2, 3 * P])
        pt = sb("pt", [P, 2, 3 * P])
        recs = sb("recs", [P, TT, H])
        on = sb("on", [P, TT, D])
        osq = sb("osq", [P, TT, D])
        vv = sb("vv", [P, TT * H])
        rs = sb("rs", [P, TT * H])
        tmp = sb("tmp", [P, TT * H])
        oT = sb("oT", [P, KD, T])
        lw = ln_scratch(sb, TT)
        S = [psum[:, 0:2, :], psum[:, 2:4, :]]
        PT = [psum[:, 4, :], psum[:, 5, :]]
        KP = [psum[:, 6, :], psum[:, 7, :]]
        O = psum[:, 6:8, 0:H * V1].rearrange("p t (h e) -> p t h e", e=V1)

        x_staged = sem("x_staged")
        xT_ps = sem("xT_ps")
        xT_ready = sem("xT_ready")
        proj_ps = sem("proj_ps")
        rot_ready = sem("rot_ready")
        lam_ready = sem("lam_ready")
        s_ps = sem("s_ps")
        nm_ready = sem("nm_ready")
        p_exp = sem("p_exp")
        nb_ready = sem("nb_ready")
        p_ready = sem("p_ready")
        pt_ps = sem("pt_ps")
        pt_ready = sem("pt_ready")
        av_ps = sem("av_ps")
        on_ready = sem("on_ready")
        oT_ps = sem("oT_ps")
        oT_ready = sem("oT_ready")
        y_ps = sem("y_ps")
        set_up = sem("set_up")
        steps = sem("steps")

        with nc.Block() as block:
            @block.sync
            def _(sp):
                with sp.Fori(0, B) as b:
                    sp.wait_ge(xT_ps, b + 1)
                    sp.dma_start(xs[:, :, :], x_sb[:, bass.ds(b * TT, TT), :]).then_inc(x_staged, 16)

            @block.tensor
            def _(pe):
                mm = nc.tensor.matmul
                pe.sem_inc(xT_ps, 1)
                with pe.Fori(0, B) as b:
                    pe.wait_ge(x_staged, b * 16 + 16)
                    for h in range(KD):
                        for t in range(TT):
                            last = nc.tensor.transpose(PT[0][:, (h * TT + t) * P:(h * TT + t + 1) * P],
                                                       xs[:, t, h * P:(h + 1) * P], c["id"])
                    last.then_inc(xT_ps, 1)
                    pe.wait_ge(xT_ready, b + 1)
                    for a in range(A):
                        for r in range(R):
                            for k in range(KD):
                                last = mm(S[a][:, r // 2, (r % 2) * T:(r % 2 + 1) * T],
                                          w["q"][:, k, (a * R + r) * P:(a * R + r + 1) * P], xT[:, k, :],
                                          start=(k == 0), stop=(k == KD - 1))
                        last.then_inc(proj_ps, 1)
                    for a in range(A):
                        for j in range(2):
                            for k in range(KD):
                                mm(KP[a][:, j * T:(j + 1) * T], w["k"][:, k, (2 * a + j) * P:(2 * a + j + 1) * P], xT[:, k, :],
                                   start=(k == 0), stop=(k == KD - 1))
                    pe.wait_ge(rot_ready, b * 3 + 1)
                    for t in range(TT):
                        for k in range(KD):
                            last = mm(PT[1][:, t * G * HD:(t + 1) * G * HD], xT[:, k, t * P:(t + 1) * P],
                                      w["v"][:, k, :], start=(k == 0), stop=(k == KD - 1))
                    last.then_inc(proj_ps, 1)

                    def scores(n):
                        if n < 2:
                            pe.wait_ge(rot_ready, b * 3 + 3)
                        else:
                            pe.wait_ge(p_exp, b * NG + n - 1)
                        r, g = n // G, n % G
                        rows = slice(32 * g, 32 * g + 32)
                        for a in range(A):
                            for t in range(TT):
                                mm(S[n % 2][:, a, t * P:t * P + (t + 1) * P], qr[rows, a, r, t * P:(t + 1) * P],
                                   kr[rows, a, 0:(t + 1) * P], start=True, stop=False)
                                last = mm(S[n % 2][:, a, 2 * t * P:(2 * t + 1) * P], c["idb"], c["maskb"], start=False, stop=True)
                        last.then_inc(s_ps, 1)

                    def turn(n):
                        pe.wait_ge(p_ready, b * NG + n + 1)
                        if n >= 2:
                            pe.wait_ge(pt_ready, b * NG + n - 1)
                        for j in range(3):
                            last = nc.tensor.transpose(PT[n % 2][:, j * P:(j + 1) * P], p2[:, n % 2, j * P:(j + 1) * P], c["id"])
                        last.then_inc(pt_ps, 1)

                    def values(n):
                        pe.wait_ge(pt_ready, b * NG + n + 1)
                        r, g = n // G, n % G
                        h = 4 * g + r
                        pp = pt[:, n % 2, :]
                        mm(O[:, 0, h, :], pp[:, 0:P], va[:, 0, g, :], start=True, stop=True)
                        mm(O[:, 1, h, :], pp[:, P:2 * P], va[:, 0, g, :], start=True, stop=False)
                        mm(O[:, 1, h, :], pp[:, 2 * P:3 * P], va[:, 1, g, :], start=False, stop=True).then_inc(av_ps, 1)

                    for n in range(NG + 3):
                        if n < NG:
                            scores(n)
                        if 2 <= n <= NG + 1:
                            turn(n - 2)
                        if n >= 3:
                            values(n - 3)
                    pe.wait_ge(on_ready, b + 1)
                    for h in range(KD):
                        for t in range(TT):
                            last = nc.tensor.transpose(PT[0][:, (h * TT + t) * P:(h * TT + t + 1) * P],
                                                       on[:, t, h * P:(h + 1) * P], c["id"])
                    last.then_inc(oT_ps, 1)
                    pe.wait_ge(oT_ready, b + 1)
                    for t in range(TT):
                        for k in range(KD):
                            last = mm(PT[1][:, t * D:(t + 1) * D], oT[:, k, t * P:(t + 1) * P], w["o"][:, k, :],
                                      start=(k == 0), stop=(k == KD - 1))
                    last.then_inc(y_ps, 1)

            @block.scalar
            def _(act):
                nc.scalar.preload_act_table(ACT.Exp)
                act.wait_ge(set_up, 2)
                nc.scalar.activation(lam[:, :, :], lam[:, :, :], ACT.Exp).then_inc(lam_ready, 1)
                with act.Fori(0, B) as b:
                    act.wait_ge(xT_ps, b + 2)
                    nc.scalar.activation(xT[:, :, :], PT[0].rearrange("p (k t) -> p k t", k=KD), ACT.Copy).then_inc(xT_ready, 1)

                    def first(n):
                        act.wait_ge(nm_ready, b * NG + n + 1)
                        if n >= 2:
                            act.wait_ge(nb_ready, b * NG + n - 1)
                        for a in range(A):
                            for t in range(TT):
                                s = slice(t * P, t * P + (t + 1) * P)
                                last = nc.scalar.activation(pr[:, n % 2, a, s], S[n % 2][:, a, s], ACT.Exp, bias=nm[:, n % 2, t, a:a + 1],
                                                            accum_out=sums[:, n % 2, t, a:a + 1])
                        last.then_inc(p_exp, 1)

                    def second(n):
                        act.wait_ge(nb_ready, b * NG + n + 1)
                        if n >= 2:
                            act.wait_ge(pt_ps, b * NG + n - 1)
                        for t in range(TT):
                            s = slice(t * P, t * P + (t + 1) * P)
                            last = nc.scalar.activation(p2[:, n % 2, s], dif[:, n % 2, s], ACT.Exp, bias=nb2[:, n % 2, t:t + 1],
                                                        scale=rec[:, n % 2, t, 0:1])
                        last.then_inc(p_ready, 1)

                    for n in range(NG + 1):
                        if n < NG:
                            first(n)
                        if n >= 1:
                            second(n - 1)
                    act.wait_ge(oT_ps, b + 1)
                    nc.scalar.activation(oT[:, :, :], PT[0].rearrange("p (k t) -> p k t", k=KD), ACT.Copy).then_inc(oT_ready, 1)

            @block.vector
            def _(dve):
                st = Steps(dve, steps, L3A_STEPS)
                for j in range(2):
                    last = nc.vector.tensor_tensor(lprod[:, j, :, :], w["lq%d" % (j + 1)], w["lk%d" % (j + 1)], ALU.mult)
                last.then_inc(set_up, 1)
                dve.wait_ge(set_up, 1)
                nc.vector.tensor_reduce(lam[:, :, :], lprod[:, :, :, :], AX.X, ALU.add).then_inc(set_up, 1)
                dve.wait_ge(lam_ready, 1)
                nc.vector.tensor_tensor(nlam[:, :], lam[:, 1, :], lam[:, 0, :], ALU.subtract).then_inc(set_up, 1)
                dve.wait_ge(set_up, 3)
                nc.vector.tensor_scalar(nlam[:, :], nlam[:, :], -LAM_INIT, None, ALU.add).then_inc(set_up, 1)
                nc.vector.tensor_scalar(gain[:, :], w["rms"], 1.0 - LAM_INIT, None, ALU.mult).then_inc(set_up, 1)
                nc.vector.memset(va[:, :, :, HD:V1], 1.0)
                dve.wait_ge(set_up, 5)
                with dve.Fori(0, B) as b:
                    st.begin(b)
                    for a in range(A):
                        dve.wait_ge(proj_ps, b * 3 + a + 1)
                        for j in range(2):
                            last = nc.vector.tensor_tensor(qr[:, a, 2 * j:2 * j + 2, :], S[a][:, j, :].rearrange("p (r t) -> p r t", r=2),
                                                           bc(c["l3_q"][:, a, :], 1, 2), ALU.mult)
                        last.then_inc(rot_ready, 1)
                    dve.wait_ge(proj_ps, b * 3 + 3)
                    for a in range(A):
                        last = nc.vector.tensor_tensor(k1[:, a, :, :], KP[a].rearrange("p (j t) -> p j t", j=2), c["l3_k"][:, a, :, :], ALU.mult)
                    st.do(last)
                    nc.vector.tensor_tensor(kr[:, :, :], k1[:, :, 0, :], k1[:, :, 1, :], ALU.add)
                    nc.vector.tensor_copy(va[:, :, :, 0:HD],
                                          PT[1][:, 0:TT * G * HD].rearrange("p (t g e) -> p t g e", t=TT, g=G)).then_inc(rot_ready, 1)

                    def maxima(n):
                        dve.wait_ge(s_ps, b * NG + n + 1)
                        if n >= 2:
                            dve.wait_ge(p_exp, b * NG + n - 1)
                        for t in range(TT):
                            last = nc.vector.tensor_reduce(nm[:, n % 2, t, :], S[n % 2][:, :, t * P:t * P + (t + 1) * P],
                                                           AX.X, ALU.max, negate=True)
                        last.then_inc(nm_ready, 1)

                    def difference(n):
                        r, g = n // G, n % G
                        h = 4 * g + r
                        i = n % 2
                        dve.wait_ge(p_exp, b * NG + n + 1)
                        if n >= 2:
                            dve.wait_ge(p_ready, b * NG + n - 1)
                        st.do(nc.vector.reciprocal(rec[:, i, :, :], sums[:, i, :, :]))
                        st.do(nc.vector.scalar_tensor_tensor(ratio[:, i, :], sums[:, i, :, 0], nlam[:, h:h + 1], rec[:, i, :, 1], ALU.mult, ALU.mult))
                        for t in range(TT):
                            s = slice(t * P, t * P + (t + 1) * P)
                            last = nc.vector.scalar_tensor_tensor(dif[:, i, s], pr[:, i, 1, s], ratio[:, i, t:t + 1], pr[:, i, 0, s], ALU.mult, ALU.add)
                        st.do(last)
                        for t in range(TT):
                            s = slice(2 * t * P, (2 * t + 1) * P)
                            last = nc.vector.tensor_tensor(dif[:, i, s], dif[:, i, s], c["mask"], ALU.add)
                        st.do(last)
                        for t in range(TT):
                            last = nc.vector.tensor_reduce(nm2[:, i, t:t + 1], dif[:, i, t * P:t * P + (t + 1) * P], AX.X, ALU.max, negate=True)
                        st.do(last)
                        nc.vector.tensor_tensor(nb2[:, i, :], nm2[:, i, :], rec[:, i, :, 0], ALU.mult).then_inc(nb_ready, 1)

                    def out_of_psum(n):
                        dve.wait_ge(pt_ps, b * NG + n + 1)
                        if n >= 2:
                            dve.wait_ge(av_ps, b * NG + n - 1)
                        nc.vector.tensor_copy(pt[:, n % 2, :], PT[n % 2][:, 0:3 * P]).then_inc(pt_ready, 1)

                    for n in range(NG + 2):
                        if n < NG:
                            maxima(n)
                        if 1 <= n <= NG:
                            difference(n - 1)
                        if n >= 2:
                            out_of_psum(n - 2)
                    dve.wait_ge(av_ps, b * NG + NG)
                    st.do(nc.vector.reciprocal(recs[:, :, :], O[:, :, :, HD]))
                    heads = lambda ap: ap.rearrange("p (h e) -> p h e", e=HD)
                    for t in range(TT):
                        last = nc.vector.tensor_tensor(heads(on[:, t, :]), O[:, t, :, 0:HD], bc(recs[:, t, :], 2, HD), ALU.mult)
                    st.do(last)
                    st.do(nc.vector.tensor_tensor(osq[:, :, :], on[:, :, :], on[:, :, :], ALU.mult))
                    flat = lambda ap: ap.rearrange("p t (h e) -> p (t h) e", e=HD)
                    st.do(nc.vector.tensor_reduce(vv[:, :], flat(osq[:, :, :]), AX.X, ALU.add))
                    st.do(nc.vector.tensor_scalar(vv[:, :], vv[:, :], 1.0 / HD, EPS, ALU.mult, ALU.add))
                    newton_rsqrt(nc, st, vv[:, :], rs[:, :], tmp[:, :])
                    st.wait()
                    st.do(nc.vector.tensor_tensor(flat(on[:, :, :]), flat(on[:, :, :]), bc(rs[:, :], 2, HD), ALU.mult))
                    nc.vector.tensor_tensor(flat(on[:, :, :]), flat(on[:, :, :]), bc(gain[:, :], 1, TT * H), ALU.mult).then_inc(on_ready, 1)
                    layernorm_tail(nc, st, x_sb, b * TT, TT, PT[1].rearrange("p (t n) -> p t n", t=TT),
                                   lambda: dve.wait_ge(y_ps, b + 1), lw)
                    st.end()


L3A_STEPS = 1 + 5 * 16 + 5 + NEWTON_STEPS + 1 + LN_STEPS



def l3_ffn(nc, c, x_sb, w, psum):
    E, I, TOP = 32, 96, 4
    NH = E * I // P
    with ExitStack() as ctx:
        sb = lambda name, shape, dt=F32: ctx.enter_context(nc.sbuf_tensor("l3f_" + name, shape, dt))
        sem = lambda name: ctx.enter_context(nc.semaphore("l3f_" + name))
        xs = sb("xs", [P, CH, D])
        xT = sb("xT", [P, KD, CN])
        pb = sb("pb", [P, CH, E + 8 - TOP])
        nm = sb("nm", [P, CH])
        sums = sb("sums", [P, CH])
        top = sb("top", [P, CH, 8])
        pick = sb("pick", [P, CH, 8])
        left = sb("left", [P, CH, E + 8 - TOP])
        wsum = sb("wsum", [P, CH])
        cw = sb("cw", [P, CH, E])
        rest = sb("rest", [P, CH, E])
        c3 = sb("c3", [P, CH, 3, E], BF16)
        c3T = sb("c3T", [3 * E, CN], BF16)
        sg = sb("sg", [P, 2, CN])
        gu = sb("gu", [P, 2, CN])
        hw = sb("hw", [P, 2, CN])
        yT = sb("yT", [P, KD, CN])
        lw = ln_scratch(sb, CH)
        bank = lambda i: psum[:, i, :]
        GB, UB, CB, YB = [bank(0), bank(1)], [bank(2), bank(3)], [bank(4), bank(5)], [bank(6), bank(7)]
        Y = psum[:, 0:2, :].rearrange("p a (t n) -> p (a t) n", t=2)

        x_staged = sem("x_staged")
        xT_ps = sem("xT_ps")
        xT_ready = sem("xT_ready")
        logit_ps = sem("logit_ps")
        nm_ready = sem("nm_ready")
        ex_ready = sem("ex_ready")
        c3_ready = sem("c3_ready")
        c3T_ps = sem("c3T_ps")
        c3T_ready = sem("c3T_ready")
        h_ps = sem("h_ps")
        sg_ready = sem("sg_ready")
        gu_ready = sem("gu_ready")
        hw_ready = sem("hw_ready")
        used = sem("used")
        yT_ready = sem("yT_ready")
        y_ps = sem("y_ps")
        steps = sem("steps")

        with nc.Block() as block:
            @block.sync
            def _(sp):
                with sp.Fori(0, NCH) as b:
                    sp.wait_ge(xT_ps, b + 1)
                    sp.dma_start(xs[:, :, :], x_sb[:, bass.ds(b * CH, CH), :]).then_inc(x_staged, 16)

            @block.tensor
            def _(pe):
                mm = nc.tensor.matmul
                pe.sem_inc(xT_ps, 1)
                with pe.Fori(0, NCH) as b:
                    pe.wait_ge(x_staged, b * 16 + 16)
                    for k in range(KD):
                        for t in range(CH):
                            last = nc.tensor.transpose(CB[k][:, t * P:(t + 1) * P], xs[:, t, k * P:(k + 1) * P], c["id"])
                    last.then_inc(xT_ps, 1)
                    pe.wait_ge(xT_ready, b + 1)
                    for t in range(CH):
                        for k in range(KD):
                            last = mm(UB[0][:, t * E:(t + 1) * E], xT[:, k, t * P:(t + 1) * P], w["router"][:, k, :],
                                      start=(k == 0), stop=(k == KD - 1))
                    last.then_inc(logit_ps, 1)
                    pe.wait_ge(c3_ready, b + 1)
                    for t in range(CH):
                        last = nc.tensor.transpose(UB[1].bitcast(BF16)[0:3 * E, t * P:(t + 1) * P],
                                                   c3[:, t, :, :].rearrange("p a e -> p (a e)"), c["idb"])
                    last.then_inc(c3T_ps, 1)
                    pe.wait_ge(c3T_ready, b + 1)

                    def hidden(e):
                        if e >= 2:
                            pe.wait_ge(gu_ready, b * NH + e - 1)
                            pe.wait_ge(hw_ready, b * NH + e - 1)
                        for name, bk in (("gate", GB), ("up", UB)):
                            for k in range(KD):
                                mm(bk[e % 2], w[name][:, k, e * P:(e + 1) * P], xT[:, k, :], start=(k == 0), stop=(k == KD - 1))
                        mm(CB[e % 2], c["sel3"][:, e * P:(e + 1) * P], c3T[:, :], start=True, stop=True).then_inc(h_ps, 1)

                    def down(e):
                        pe.wait_ge(hw_ready, b * NH + e + 1)
                        for k in range(KD):
                            last = mm(YB[k], w["down"][:, e, k * P:(k + 1) * P], hw[:, e % 2, :], start=(e == 0), stop=(e == NH - 1))
                        last.then_inc(used, 1)

                    for e in range(NH + 1):
                        if e < NH:
                            hidden(e)
                        if e >= 1:
                            down(e - 1)
                    pe.wait_ge(yT_ready, b + 1)
                    for t in range(CH):
                        for k in range(KD):
                            last = nc.tensor.transpose(Y[:, t, k * P:(k + 1) * P], yT[:, k, t * P:(t + 1) * P], c["id"])
                    last.then_inc(y_ps, 1)

            @block.scalar
            def _(act):
                with act.Fori(0, NCH) as b:
                    act.wait_ge(xT_ps, b + 2)
                    for k in range(KD):
                        last = nc.scalar.activation(xT[:, k, :], CB[k], ACT.Copy)
                    last.then_inc(xT_ready, 1)
                    act.wait_ge(nm_ready, b + 1)
                    for t in range(CH):
                        last = nc.scalar.activation(pb[:, t, 0:E], UB[0][:, t * E:(t + 1) * E], ACT.Exp, bias=nm[:, t:t + 1],
                                                    accum_out=sums[:, t:t + 1])
                    last.then_inc(ex_ready, 1)
                    for e in range(NH):
                        act.wait_ge(h_ps, b * NH + e + 1)
                        if e >= 2:
                            act.wait_ge(gu_ready, b * NH + e - 1)
                        nc.scalar.activation(sg[:, e % 2, :], GB[e % 2], ACT.Silu).then_inc(sg_ready, 1)
                    act.wait_ge(used, b * NH + NH)
                    for k in range(KD):
                        last = nc.scalar.activation(yT[:, k, :], YB[k], ACT.Copy)
                    last.then_inc(yT_ready, 1)

            @block.vector
            def _(dve):
                st = Steps(dve, steps, L3F_STEPS)
                nc.vector.memset(pb[:, :, E:], BIG)
                nc.vector.memset(pick[:, :, :], BIG)
                with dve.Fori(0, NCH) as b:
                    st.begin(b)
                    dve.wait_ge(logit_ps, b + 1)
                    nc.vector.tensor_reduce(nm[:, :], UB[0][:, 0:CH * E].rearrange("p (t e) -> p t e", t=CH), AX.X, ALU.max, negate=True).then_inc(nm_ready, 1)
                    dve.wait_ge(ex_ready, b + 1)
                    st.do(nc.vector.reciprocal(wsum[:, :], sums[:, :]))
                    st.do(nc.vector.tensor_tensor(pb[:, :, 0:E], pb[:, :, 0:E], bc(wsum[:, :], 2, E), ALU.mult))
                    carry(nc, lw)
                    for t in range(CH):
                        last = nc.vector.max(top[:, t, :], pb[:, t, 0:E])
                    st.do(last)
                    st.do(nc.vector.tensor_copy(pick[:, :, 0:TOP], top[:, :, 0:TOP]))
                    carry(nc, lw)
                    for t in range(CH):
                        last = nc.vector.match_replace(left[:, t, :], pick[:, t, :], pb[:, t, :], -BIG)
                    st.do(last)
                    st.do(nc.vector.scalar_tensor_tensor(cw[:, :, :], left[:, :, 0:E], -BIG, pb[:, :, 0:E], ALU.is_equal, ALU.mult))
                    st.do(nc.vector.tensor_reduce(wsum[:, :], cw[:, :, :], AX.X, ALU.add))
                    st.do(nc.vector.reciprocal(wsum[:, :], wsum[:, :]))
                    st.do(nc.vector.tensor_tensor(cw[:, :, :], cw[:, :, :], bc(wsum[:, :], 2, E), ALU.mult))
                    split3(nc, st, cw[:, :, :], [c3[:, :, j, :] for j in range(3)], rest[:, :, :])
                    nc.vector.memset(lw["carrier"][:, :], 0.0).then_inc(c3_ready, 1)
                    dve.wait_ge(c3T_ps, b + 1)
                    nc.vector.tensor_copy(c3T[:, :], UB[1].bitcast(BF16)[0:3 * E, 0:CN]).then_inc(c3T_ready, 1)

                    def weigh(e):
                        dve.wait_ge(gu_ready, b * NH + e + 1)
                        if e >= 2:
                            dve.wait_ge(used, b * NH + e - 1)
                        nc.vector.tensor_tensor(hw[:, e % 2, :], gu[:, e % 2, :], CB[e % 2], ALU.mult).then_inc(hw_ready, 1)

                    for e in range(NH):
                        dve.wait_ge(sg_ready, b * NH + e + 1)
                        nc.vector.tensor_tensor(gu[:, e % 2, :], sg[:, e % 2, :], UB[e % 2], ALU.mult).then_inc(gu_ready, 1)
                        weigh(e)
                    layernorm_tail(nc, st, x_sb, b * CH, CH, Y, lambda: dve.wait_ge(y_ps, b + 1), lw)
                    st.end()


L3F_STEPS = 9 + 5 + LN_STEPS



LAST_STAGE = 8
W_COLS = {
    "l0a_q": KD * 512, "l0a_k": KD * 256, "l0a_v": KD * 64, "l0a_o": KD * D,
    "l0f_w1": 32 * 128, "l0f_w2": 32 * 128, "l0f_fc1": KD * 128, "l0f_fc2": D, "l0f_gate": KD * 32, "l0f_up": KD * 512,
    "l0f_down": 4 * D, "l0f_bias": 32,
    "l1a_q": KD * 2048, "l1a_k": KD * 2048, "l1a_v": KD * 2048, "l1a_o": 16 * D, "l1a_gq": 1, "l1a_gk": 1,
    "l1f_router": KD * 128, "l1f_gate": KD * 1024, "l1f_up": KD * 1024, "l1f_down": D, "l1f_amp": 16, "l1f_escale": 1,
    "l1f_sgate": KD * 256, "l1f_sup": KD * 256, "l1f_sdown": 2 * D,
    "l2a_u": KD * 256, "l2a_v": KD * 256, "l2a_g1": KD * 64, "l2a_g2": 256, "l2a_bu": 2, "l2a_bv": 2,
    "l2a_bg1": 1, "l2a_bg2": 2, "l2a_conv": KD * 3, "l2a_convb": KD,
    "l2f_gate": KD * 1024, "l2f_up": KD * 1024, "l2f_down": 8 * D,
    "l3a_q": KD * 1024, "l3a_k": KD * 512, "l3a_v": KD * 64, "l3a_o": KD * D, "l3a_lq1": 256, "l3a_lq2": 256, "l3a_lk1": 256,
    "l3a_lk2": 256, "l3a_rms": 16,
    "l3f_router": KD * 32, "l3f_gate": KD * 3072, "l3f_up": KD * 3072, "l3f_down": 24 * D,
}
W_CUT = {"l0a_q": KD, "l0a_k": KD, "l0a_v": KD, "l0a_o": KD, "l0f_w1": 32, "l0f_w2": 32, "l0f_fc1": KD, "l0f_gate": KD,
         "l0f_up": KD, "l1a_q": KD, "l1a_k": KD, "l1a_v": KD, "l1a_o": 16,
         "l1f_router": KD, "l1f_gate": KD, "l1f_up": KD, "l1f_amp": 8, "l1f_sgate": KD, "l1f_sup": KD, "l1f_sdown": 2,
         "l2a_u": KD, "l2a_v": KD, "l2a_g1": KD, "l2a_conv": KD, "l2f_gate": KD, "l2f_up": KD, "l2f_down": 8,
         "l3a_q": KD, "l3a_k": KD, "l3a_v": KD, "l3a_o": KD, "l3a_lq1": 16, "l3a_lq2": 16, "l3a_lk1": 16, "l3a_lk2": 16,
         "l3f_router": KD, "l3f_gate": KD, "l3f_up": KD, "l3f_down": 24, "l0f_down": 4}
C_COLS = {"id": P, "l0_q": T, "l0_k": 2 * T, "one": 1, "l3_q": 2 * T, "l3_k": 4 * T, "mask": P}
CB_COLS = {"idb": P, "maskb": P, "sel0": 32 * P, "sel3": 24 * P}


STAGES = [("l0a", l0_attention), ("l0f", l0_ffn), ("l1a", l1_attention), ("l1f", l1_ffn), ("l2a", l2_mixing), ("l2f", l2_ffn),
          ("l3a", l3_attention), ("l3f", l3_ffn)]


def network(nc, x_in, cf, cb, wts, out):
    with ExitStack() as ctx:
        x_sb = ctx.enter_context(nc.sbuf_tensor("x_sb", [P, NT, D], F32))
        cf_sb = ctx.enter_context(nc.sbuf_tensor("cf_sb", [P, sum(C_COLS.values())], F32))
        cb_sb = ctx.enter_context(nc.sbuf_tensor("cb_sb", [P, sum(CB_COLS.values())], mybir.dt.uint16))
        psum = ctx.enter_context(nc.psum_tensor("psum", [P, 8, 512], F32))
        loaded = [ctx.enter_context(nc.semaphore(f"loaded{s}")) for s in range(8)]
        stored = ctx.enter_context(nc.semaphore("stored"))
        c, at = {}, 0
        for name, n in C_COLS.items():
            c[name] = cf_sb[:, at:at + n]
            at += n
        at = 0
        for name, n in CB_COLS.items():
            c[name] = cb_sb[:, at:at + n].bitcast(BF16)
            at += n
        c["l0_k"] = c["l0_k"].rearrange("p (j t) -> p j t", j=2)
        x_rows = x_in.rearrange("b (t p) d -> p (b t) d", p=P)
        o_rows = out.rearrange("b (t p) d -> p (b t) d", p=P)

        c["l3_q"] = c["l3_q"].rearrange("p (a t) -> p a t", a=2)
        c["l3_k"] = c["l3_k"].rearrange("p (a j t) -> p a j t", a=2, j=2)
        c["sel0"], c["sel3"] = c["sel0"][0:96, :], c["sel3"][0:96, :]

        def weights(scope, stage):
            raw = {n: scope.enter_context(nc.sbuf_tensor("w_" + n, [P, k], F32)) for n, k in W_COLS.items() if n.startswith(stage)}
            view = {n[4:]: t[:, :].rearrange("p (k n) -> p k n", k=W_CUT[n]) if n in W_CUT else t[:, :] for n, t in raw.items()}
            return raw, view

        def load(raw, sem, before=()):
            with nc.Block() as block:
                @block.sync
                def _(sp):
                    for dst, src in before:
                        sp.dma_start(dst, src).then_inc(sem, 16)
                    for n, t in raw.items():
                        sp.dma_start(t[:, :], wts[n]).then_inc(sem, 16)
                    sp.wait_ge(sem, 16 * (len(before) + len(raw)))

        with ExitStack() as scope:
            raw, view = weights(scope, "l0a")
            load(raw, loaded[0], [(cf_sb[:, :], cf), (cb_sb[:, :], cb), (x_sb[:, :, :], x_rows)])
            l0_attention(nc, c, x_sb, view, psum)
        for s, (stage, run) in enumerate(STAGES[1:LAST_STAGE], 1):
            with ExitStack() as scope:
                raw, view = weights(scope, stage)
                load(raw, loaded[s])
                run(nc, c, x_sb, view, psum)
        with nc.Block() as block:
            @block.sync
            def _(sp):
                sp.dma_start(o_rows, x_sb[:, :, :]).then_inc(stored, 16)
                sp.wait_ge(stored, 16)



def k_major(w):
    k, n = w.shape
    return np.ascontiguousarray(w.reshape(k // P, P, n).transpose(1, 0, 2).reshape(P, -1))


def l0_columns():
    q = [16 * (4 * g + r) + (j if j < 16 else (j - 16 + 8) % 16) for r in range(4) for g in range(4) for j in range(32)]
    k = [16 * g + (j + 8 * s) % 16 for s in range(2) for g in range(4) for j in range(32)]
    return np.array(q), np.array(k)


def rope_l0():
    f = (1.0 / 10000.0 ** (np.arange(0, 16, 2, dtype=np.float32) / np.float32(16))).astype(np.float32)
    ang = (np.arange(T, dtype=np.float32)[:, None] * f[None, :]).astype(np.float32)
    cos, sin = np.cos(ang).astype(np.float32), np.sin(ang).astype(np.float32)
    j = np.arange(P) % 16
    cp, sp = cos[:, j % 8].T, sin[:, j % 8].T * np.where(j < 8, -1, 1)[:, None].astype(np.float32)
    first = (np.arange(P) % 32 < 16)[:, None]
    return (np.where(first, cp, sp) * np.float32(0.25)).astype(np.float32), np.concatenate([cp, sp], 1).astype(np.float32)


def l3_columns():
    q = [32 * (4 * g + r) + ((16 * a + j) if j < 16 else (16 * a + j - 16) ^ 1)
         for a in range(2) for r in range(4) for g in range(4) for j in range(32)]
    k = [32 * g + ((16 * a + j % 16) ^ s) for a in range(2) for s in range(2) for g in range(4) for j in range(32)]
    return np.array(q), np.array(k)


def rope_l3():
    f = (1.0 / 10000.0 ** (np.arange(0, 32, 2, dtype=np.float32) / np.float32(32))).astype(np.float32)
    ang = (np.arange(T, dtype=np.float32)[:, None] * f[None, :]).astype(np.float32)
    cos, sin = np.cos(ang).astype(np.float32), np.sin(ang).astype(np.float32)
    qs, ks = [], []
    for a in range(2):
        dd = 16 * a + np.arange(P) % 16
        cp, sp = cos[:, dd // 2].T, sin[:, dd // 2].T * np.where(dd % 2 == 0, -1, 1)[:, None].astype(np.float32)
        qs.append(np.where((np.arange(P) % 32 < 16)[:, None], cp, sp) * np.float32(0.25))
        ks += [cp, sp]
    return np.concatenate(qs, 1).astype(np.float32), np.concatenate(ks, 1).astype(np.float32)


def tables():
    q0, k0 = rope_l0()
    q3, k3 = rope_l3()
    mask = np.where(np.arange(P)[None, :] > np.arange(P)[:, None], np.float32(NEG), np.float32(0))
    cf = np.concatenate([np.eye(P, dtype=np.float32), q0, k0, np.ones((P, 1), np.float32), q3, k3, mask], 1)
    part = np.arange(P)[:, None]
    sel0 = (part % 32 == np.arange(32 * P)[None, :] // P).astype(np.float32)
    sel3 = (part % 32 == np.arange(24 * P)[None, :] // 96).astype(np.float32)
    cb = np.concatenate([np.eye(P, dtype=np.float32), mask, sel0, sel3], 1)
    cb = (cb.view(np.uint32) >> 16).astype(np.uint16)
    return np.ascontiguousarray(cf), np.ascontiguousarray(cb)


def layouts(i):
    q0, k0 = l0_columns()
    w = {
        "l0a_q": k_major(i["L0_attn_wq"][:, q0]), "l0a_k": k_major(i["L0_attn_wk"][:, k0]),
        "l0a_v": k_major(i["L0_attn_wv"]), "l0a_o": k_major(i["L0_attn_wo"]),
    }
    w |= {
        "l0f_w1": i["L0_ffn_w1"].transpose(2, 0, 1).reshape(P, -1), "l0f_w2": i["L0_ffn_w2"].transpose(2, 0, 1).reshape(P, -1),
        "l0f_fc1": k_major(i["L0_ffn_fc1_w"].T), "l0f_fc2": i["L0_ffn_fc2_w"].T, "l0f_gate": k_major(i["L0_ffn_gate_w"].T),
        "l0f_up": k_major(i["L0_ffn_shared_up_w"].T), "l0f_down": k_major(i["L0_ffn_shared_down_w"].T),
        "l0f_bias": np.broadcast_to(i["L0_ffn_gate_bias"], (P, 32)),
    }
    w |= {
        "l1a_q": k_major(i["L1_attn_Wq"].T), "l1a_k": k_major(i["L1_attn_Wk"].T), "l1a_v": k_major(i["L1_attn_Wv"].T),
        "l1a_o": k_major(i["L1_attn_Wo"].T), "l1a_gq": i["L1_attn_gq"][:, None], "l1a_gk": i["L1_attn_gk"][:, None],
    }
    w |= {
        "l1f_router": k_major(i["L1_ffn_w_router"]), "l1f_gate": k_major(i["L1_ffn_w_gate"]), "l1f_up": k_major(i["L1_ffn_w_up"]),
        "l1f_down": i["L1_ffn_w_down"], "l1f_amp": i["L1_ffn_amplitudes"].reshape(P, -1), "l1f_escale": i["L1_ffn_expert_scale"][:, None],
        "l1f_sgate": k_major(i["L1_ffn_shared_w_gate"]), "l1f_sup": k_major(i["L1_ffn_shared_w_up"]),
        "l1f_sdown": k_major(i["L1_ffn_shared_w_down"]),
    }
    halves = lambda v: v.reshape(2, P).T
    down = lambda a: np.pad(a, ((0, P - a.shape[0]), (0, 0)))
    w |= {
        "l2a_u": k_major(i["L2_attn_Wu"].T), "l2a_v": k_major(i["L2_attn_Wv"].T), "l2a_g1": k_major(i["L2_attn_Wg1"].T),
        "l2a_g2": down(i["L2_attn_Wg2"].T), "l2a_bu": halves(i["L2_attn_bu"]),
        "l2a_bv": halves(i["L2_attn_bv"]), "l2a_bg1": down(i["L2_attn_bg1"][:, None]), "l2a_bg2": halves(i["L2_attn_bg2"]),
        "l2a_conv": k_major(i["L2_attn_conv_w"][:, 0, :]), "l2a_convb": halves(i["L2_attn_conv_b"]),
    }
    deal = (512 * np.arange(2)[:, None, None] + 4 * np.arange(P)[None, None, :] + np.arange(4)[None, :, None]).reshape(-1)
    w |= {
        "l2f_gate": k_major(i["L2_ffn_w_gate"][:, deal]), "l2f_up": k_major(i["L2_ffn_w_up"][:, deal]),
        "l2f_down": k_major(i["L2_ffn_w_down"][deal, :]),
    }
    q3, k3 = l3_columns()
    every = lambda a: np.broadcast_to(a.reshape(-1), (P, a.size))
    g3 = i["L3_ffn_gate_up_proj"].transpose(1, 0, 2)
    w |= {
        "l3a_q": k_major(i["L3_attn_Wq"][:, q3]), "l3a_k": k_major(i["L3_attn_Wk"][:, k3]), "l3a_v": k_major(i["L3_attn_Wv"]),
        "l3a_o": k_major(i["L3_attn_Wo"]), "l3a_rms": every(i["L3_attn_rms_w"]),
        **{"l3a_" + n: every(i["L3_attn_" + n]) for n in ("lq1", "lq2", "lk1", "lk2")},
        "l3f_router": k_major(i["L3_ffn_gate"]), "l3f_gate": k_major(g3[:, :, 0:96].reshape(D, -1)),
        "l3f_up": k_major(g3[:, :, 96:192].reshape(D, -1)), "l3f_down": k_major(i["L3_ffn_down_proj"].reshape(-1, D)),
    }
    return {n: np.ascontiguousarray(a) for n, a in w.items()}


def kernel(**inputs):
    import concourse.bacc as bacc
    from concourse.bass_utils import run_bass_kernel_spmd

    i = {k: np.asarray(v) for k, v in inputs.items()}
    cf, cb = tables()
    host = {"x": np.ascontiguousarray(i["L0_attn_x"]), "table_f32": cf, "table_bf16": cb, **layouts(i)}
    nc = bacc.Bacc("TRN2", target_bir_lowering=False, num_devices=1)
    arrays, aps = {}, {}
    for name, a in host.items():
        arrays[name + "_dram"] = a
        aps[name] = nc.dram_tensor(name + "_dram", a.shape, mybir.dt.from_np(a.dtype), kind="ExternalInput").ap()
    out = nc.dram_tensor("out_dram", (B, T, D), F32, kind="ExternalOutput").ap()
    network(nc, aps["x"], aps["table_f32"], aps["table_bf16"], aps, out)
    r = run_bass_kernel_spmd(nc, [arrays], core_ids=[0])
    return r.results[0]["out_dram"]
```

```python
import math
from contextlib import ExitStack

import numpy as np

import concourse.bass as bass
from concourse import mybir

P = 128
F32 = mybir.dt.float32
BF16 = mybir.dt.bfloat16
I32 = mybir.dt.int32
ALU = mybir.AluOpType
ACT = mybir.ActivationFunctionType
AX = mybir.AxisListType

B, T, D = 8, 256, 256
TOK = B * T
NT = TOK // P
KD = D // P
TT = T // P
CH = 4
CN = CH * P
NCH = NT // CH
LN_EPS = 1e-5
NEG = -1e30
MAGIC = float(0x5F3759DF)


def bc(ap, axis, n):
    wide = ap.unsqueeze(axis)
    shape = list(wide.shape)
    shape[axis] = n
    return wide.broadcast_to(tuple(shape))


def ln_scratch(sb, n):
    return {"stats": sb("ln_stats", [P, n, 6]), "mv": sb("ln_mv", [P, n, 2]), "carrier": sb("ln_carrier", [P, 1])}


class Steps:

    def __init__(self, eng, sem, per_turn):
        self.eng, self.sem, self.per, self.k, self.turn = eng, sem, per_turn, 0, None

    def begin(self, turn):
        self.turn, self.k = turn, 0

    def inc(self, ins):
        ins.then_inc(self.sem, 1)
        self.k += 1
        return self.k

    def wait(self, k=None):
        self.eng.wait_ge(self.sem, self.turn * self.per + (self.k if k is None else k))

    def do(self, ins):
        self.inc(ins)
        self.wait()

    def end(self):
        assert self.k == self.per, f"a turn has {self.k} steps, not {self.per}"


def carry(nc, w):
    nc.vector.memset(w["carrier"][:, :], 0.0)


def newton_rsqrt(nc, st, v, y, t, iters=3):
    st.inc(nc.vector.tensor_scalar(y.bitcast(I32), v.bitcast(I32), -0.5, MAGIC, ALU.mult, ALU.add))
    for _ in range(iters):
        st.wait()
        st.inc(nc.vector.tensor_tensor(t, y, y, ALU.mult))
        st.wait()
        st.inc(nc.vector.scalar_tensor_tensor(t, v, -0.5, t, ALU.mult, ALU.mult))
        st.wait()
        st.inc(nc.vector.scalar_tensor_tensor(y, t, 1.5, y, ALU.add, ALU.mult))
NEWTON_STEPS = 10
LN_STEPS = 2


BIG = 3e38
LOW = -2e38


def split3(nc, st, v, parts, rest):
    st.do(nc.vector.tensor_copy(parts[0], v))
    st.do(nc.vector.tensor_tensor(rest, v, parts[0], ALU.subtract))
    st.do(nc.vector.tensor_copy(parts[1], rest))
    st.do(nc.vector.tensor_tensor(rest, rest, parts[1], ALU.subtract))
    st.do(nc.vector.tensor_copy(parts[2], rest))


def add_and_measure(nc, st, x_sb, mv, tile0, n, y_ps, w, z_ready, z_count=None):
    nc.vector.tensor_tensor(x_sb[:, bass.ds(tile0, n), :], y_ps, x_sb[:, bass.ds(tile0, n), :], ALU.add).then_inc(z_ready, 1)
    st.eng.wait_ge(z_ready, st.turn + 1 if z_count is None else z_count)
    carry(nc, w)
    for t in range(n):
        last = nc.vector.bn_stats(w["stats"][:, t, :], x_sb[:, bass.ds(tile0 + t, 1), :].rearrange("p o d -> p (o d)"))
    st.do(last)
    carry(nc, w)
    for t in range(n):
        last = nc.vector.bn_aggr(w["mv"][:, t, :], w["stats"][:, t, :])
    st.do(last)
    nc.vector.tensor_copy(mv[:, bass.ds(tile0, n), :], w["mv"][:, :, :])


def boundary(nc, c, x_sb, mv, xT, psum, sems, at, name, issue_loads, normalise=True, transpose=True, out_rows=None):
    NG = NT // 2
    done = at * NG
    with ExitStack() as ctx:
        sb = lambda n, shape: ctx.enter_context(nc.sbuf_tensor(name + "_" + n, shape, F32))
        ve, rs, tmp = sb("ve", [P, NT]), sb("rs", [P, NT]), sb("tmp", [P, NT])
        normal, turned, copied, steps, stored = (sems[n] for n in ("normal", "turned", "copied", "steps", "stored"))

        with nc.Block() as block:
            @block.sync
            def _(sp):
                issue_loads(sp)
                if out_rows is not None:
                    for g in range(NG):
                        sp.wait_ge(normal, done - NG + g + 1)
                        sp.dma_start(out_rows[:, 2 * g:2 * g + 2, :], x_sb[:, 2 * g:2 * g + 2, :]).then_inc(stored, 16)
                    sp.wait_ge(stored, 16 * NG)

            if transpose:
                @block.tensor
                def _(pe):
                    for g in range(NG):
                        if normalise:
                            pe.wait_ge(normal, done - NG + g + 1)
                        for k in range(KD):
                            for t in range(2):
                                last = nc.tensor.transpose(psum[:, g, (2 * k + t) * P:(2 * k + t + 1) * P],
                                                           x_sb[:, 2 * g + t, k * P:(k + 1) * P], c["id"])
                        last.then_inc(turned, 1)

                @block.scalar
                def _(act):
                    for g in range(NG):
                        act.wait_ge(turned, done + g + 1)
                        nc.scalar.activation(xT[:, :, g * 2 * P:(g + 1) * 2 * P], psum[:, g, :].rearrange("p (k t) -> p k t", k=KD),
                                             ACT.Copy).then_inc(copied, 1)

            if normalise:
                @block.vector
                def _(dve):
                    st = Steps(dve, steps, 1 + NEWTON_STEPS)
                    st.begin(at - 1)
                    st.do(nc.vector.tensor_scalar(ve[:, :], mv[:, :, 1], LN_EPS, None, ALU.add))
                    newton_rsqrt(nc, st, ve[:, :], rs[:, :], tmp[:, :])
                    st.wait()
                    for t in range(NT):
                        ins = nc.vector.tensor_scalar(x_sb[:, t, :], x_sb[:, t, :], mv[:, t, 0:1], rs[:, t:t + 1], ALU.subtract, ALU.mult)
                        if t % 2 == 1:
                            ins.then_inc(normal, 1)



def l0_attention(nc, c, x_sb, mv, xT, w, psum):
    HD, G, R = 16, 4, 4
    V1 = HD + 1
    NG = 8
    with ExitStack() as ctx:
        sb = lambda name, shape, dt=F32: ctx.enter_context(nc.sbuf_tensor("l0a_" + name, shape, dt))
        sem = lambda name: ctx.enter_context(nc.semaphore("l0a_" + name))
        xc = sb("xc", [P, KD, T])
        qr = sb("qr", [P, R, T])
        k1 = sb("k1", [P, 2, T])
        kr = sb("kr", [P, G, T])
        va = sb("va", [P, TT, G, V1])
        nm = sb("nm", [P, 2, TT, 2])
        pr = sb("pr", [P, 2, 2, 3 * P])
        pt = sb("pt", [P, 2, 2, 3 * P])
        rec = sb("rec", [P, TT, G * R])
        on = sb("on", [P, TT, D])
        oT = sb("oT", [P, KD, T])
        lw = ln_scratch(sb, TT)
        S = [psum[:, 0:2, :], psum[:, 2:4, :]]
        PT = [psum[:, 4, :], psum[:, 5, :]]
        O = psum[:, 6:8, 0:G * R * V1].rearrange("p t (h e) -> p t h e", e=V1)

        x_staged = sem("x_staged")
        xc_free = sem("xc_free")
        rot_steps = sem("rot_steps")
        proj_ps = sem("proj_ps")
        rot_ready = sem("rot_ready")
        s_ps = sem("s_ps")
        nm_ready = sem("nm_ready")
        p_ready = sem("p_ready")
        pt_ps = sem("pt_ps")
        pt_ready = sem("pt_ready")
        av_ps = sem("av_ps")
        on_ready = sem("on_ready")
        oT_ps = sem("oT_ps")
        oT_ready = sem("oT_ready")
        y_ps = sem("y_ps")
        z_ready = sem("z_ready")
        steps = sem("steps")

        with nc.Block() as block:
            @block.sync
            def _(sp):
                with sp.Fori(0, B) as b:
                    sp.wait_ge(xc_free, b + 1)
                    sp.dma_start(xc[:, :, :], xT[:, :, bass.ds(b * T, T)]).then_inc(x_staged, 16)

            @block.tensor
            def _(pe):
                mm = nc.tensor.matmul
                pe.sem_inc(xc_free, 1)

                def project(b):
                    pe.wait_ge(x_staged, b * 16 + 16)
                    for r in range(R):
                        for k in range(KD):
                            last = mm(S[0][:, r // 2, (r % 2) * T:(r % 2 + 1) * T], w["q"][:, k, r * P:(r + 1) * P],
                                      xc[:, k, :], start=(k == 0), stop=(k == KD - 1))
                    last.then_inc(proj_ps, 1)
                    for j in range(2):
                        for k in range(KD):
                            last = mm(S[1][:, 0, j * T:(j + 1) * T], w["k"][:, k, j * P:(j + 1) * P],
                                      xc[:, k, :], start=(k == 0), stop=(k == KD - 1))
                    last.then_inc(proj_ps, 1)
                    for t in range(TT):
                        for k in range(KD):
                            last = mm(S[1][:, 1, t * G * HD:(t + 1) * G * HD], xc[:, k, t * P:(t + 1) * P],
                                      w["v"][:, k, :], start=(k == 0), stop=(k == KD - 1))
                    last.then_inc(proj_ps, 1)
                    pe.wait_ge(proj_ps, b * 3 + 3)
                    pe.sem_inc(xc_free, 1)

                def attend(b):
                    def scores(n):
                        if n < 2:
                            pe.wait_ge(rot_ready, b * 3 + 3)
                        else:
                            pe.wait_ge(p_ready, b * NG + n - 1)
                        for i in range(2):
                            r, g = n // 2, n % 2 * 2 + i
                            for t in range(TT):
                                dst = S[n % 2][:, i, t * P:t * P + (t + 1) * P]
                                mm(dst, qr[:, r, t * P:(t + 1) * P], kr[:, g, 0:(t + 1) * P], start=True, stop=False)
                                last = mm(S[n % 2][:, i, 2 * t * P:(2 * t + 1) * P], c["idb"], c["maskb"],
                                          start=False, stop=True)
                        last.then_inc(s_ps, 1)

                    def turn(n):
                        pe.wait_ge(p_ready, b * NG + n + 1)
                        for i in range(2):
                            if n > 0:
                                pe.wait_ge(pt_ready, b * 2 * NG + 2 * (n - 1) + i + 1)
                            for j in range(3):
                                last = nc.tensor.transpose(PT[i][:, j * P:(j + 1) * P],
                                                           pr[:, n % 2, i, j * P:(j + 1) * P], c["id"])
                            last.then_inc(pt_ps, 1)

                    def values(n):
                        for i in range(2):
                            r, g = n // 2, n % 2 * 2 + i
                            h = 4 * g + r
                            pe.wait_ge(pt_ready, b * 2 * NG + 2 * n + i + 1)
                            pp = pt[:, n % 2, i, :]
                            mm(O[:, 0, h, :], pp[:, 0:P], va[:, 0, g, :], start=True, stop=True)
                            mm(O[:, 1, h, :], pp[:, P:2 * P], va[:, 0, g, :], start=True, stop=False)
                            last = mm(O[:, 1, h, :], pp[:, 2 * P:3 * P], va[:, 1, g, :], start=False, stop=True)
                        last.then_inc(av_ps, 1)

                    for n in range(NG + 3):
                        if n < NG:
                            scores(n)
                        if 2 <= n < NG + 2:
                            turn(n - 2)
                        if n >= 3:
                            values(n - 3)

                def output(b):
                    pe.wait_ge(on_ready, b + 1)
                    for h in range(KD):
                        for t in range(TT):
                            last = nc.tensor.transpose(PT[0][:, (h * TT + t) * P:(h * TT + t + 1) * P],
                                                       on[:, t, h * P:(h + 1) * P], c["id"])
                    last.then_inc(oT_ps, 1)
                    pe.wait_ge(oT_ready, b + 1)
                    for t in range(TT):
                        for k in range(KD):
                            last = mm(PT[1][:, t * D:(t + 1) * D], oT[:, k, t * P:(t + 1) * P], w["o"][:, k, :],
                                      start=(k == 0), stop=(k == KD - 1))
                    last.then_inc(y_ps, 1)

                w["early"](pe)
                project(0)
                w["late"](pe)
                with pe.Fori(0, B - 1) as b:
                    attend(b)
                    project(b + 1)
                    output(b)
                    pe.wait_ge(z_ready, b + 1)
                attend(B - 1)
                output(B - 1)

            @block.scalar
            def _(act):
                nc.scalar.preload_act_table(ACT.Exp)
                with act.Fori(0, B) as b:
                    for n in range(NG):
                        act.wait_ge(nm_ready, b * NG + n + 1)
                        if n >= 2:
                            act.wait_ge(pt_ps, b * 2 * NG + 2 * (n - 1))
                        for i in range(2):
                            for t in range(TT):
                                s = slice(t * P, t * P + (t + 1) * P)
                                last = nc.scalar.activation(pr[:, n % 2, i, s], S[n % 2][:, i, s], ACT.Exp,
                                                            bias=nm[:, n % 2, t, i:i + 1])
                        last.then_inc(p_ready, 1)
                    act.wait_ge(oT_ps, b + 1)
                    nc.scalar.activation(oT[:, :, :], PT[0].rearrange("p (k t) -> p k t", k=KD), ACT.Copy).then_inc(oT_ready, 1)

            @block.vector
            def _(dve):
                st = Steps(dve, steps, LN_STEPS + 1)
                nc.vector.memset(va[:, :, :, HD:V1], 1.0)
                nc.vector.memset(kr[:, :, :], 0.0).then_inc(rot_steps, 1)

                def rotate(b):
                    dve.wait_ge(proj_ps, b * 3 + 1)
                    for j in range(2):
                        last = nc.vector.tensor_tensor(qr[:, 2 * j:2 * j + 2, :],
                                                       S[0][:, j, :].rearrange("p (r t) -> p r t", r=2),
                                                       bc(c["l0_q"], 1, 2), ALU.mult)
                    last.then_inc(rot_ready, 1)
                    dve.wait_ge(proj_ps, b * 3 + 2)
                    nc.vector.tensor_tensor(k1[:, :, :], S[1][:, 0, :].rearrange("p (r t) -> p r t", r=2),
                                            c["l0_k"], ALU.mult).then_inc(rot_steps, 1)
                    dve.wait_ge(rot_steps, b + 2)
                    for g in range(G):
                        rows = slice(32 * g, 32 * g + 32)
                        last = nc.vector.tensor_tensor(kr[rows, g, :], k1[rows, 0, :], k1[rows, 1, :], ALU.add)
                    last.then_inc(rot_ready, 1)
                    dve.wait_ge(proj_ps, b * 3 + 3)
                    nc.vector.tensor_copy(va[:, :, :, 0:HD],
                                          S[1][:, 1, 0:TT * G * HD].rearrange("p (t g e) -> p t g e", t=TT, g=G)).then_inc(rot_ready, 1)

                def attend(b):
                    def maxima(n):
                        dve.wait_ge(s_ps, b * NG + n + 1)
                        if n >= 2:
                            dve.wait_ge(p_ready, b * NG + n - 1)
                        for t in range(TT):
                            last = nc.vector.tensor_reduce(nm[:, n % 2, t, :], S[n % 2][:, :, t * P:t * P + (t + 1) * P],
                                                           AX.X, ALU.max, negate=True)
                        last.then_inc(nm_ready, 1)

                    def out_of_psum(n):
                        for i in range(2):
                            dve.wait_ge(pt_ps, b * 2 * NG + 2 * n + i + 1)
                            if n >= 2:
                                dve.wait_ge(av_ps, b * NG + n - 1)
                            nc.vector.tensor_copy(pt[:, n % 2, i, :], PT[i][:, 0:3 * P]).then_inc(pt_ready, 1)

                    for n in range(NG + 2):
                        if n < NG:
                            maxima(n)
                        if n >= 2:
                            out_of_psum(n - 2)
                    dve.wait_ge(av_ps, b * NG + NG)
                    st.do(nc.vector.reciprocal(rec[:, :, :], O[:, :, :, HD]))
                    for t in range(TT):
                        last = nc.vector.tensor_tensor(on[:, t, :].rearrange("p (h e) -> p h e", e=HD), O[:, t, :, 0:HD],
                                                       bc(rec[:, t, :], 2, HD), ALU.mult)
                    last.then_inc(on_ready, 1)

                def output(b):
                    dve.wait_ge(y_ps, b + 1)
                    add_and_measure(nc, st, x_sb, mv, b * TT, TT, PT[1].rearrange("p (t n) -> p t n", t=TT), lw, z_ready)
                    st.end()

                rotate(0)
                with dve.Fori(0, B - 1) as b:
                    st.begin(b)
                    attend(b)
                    rotate(b + 1)
                    output(b)
                st.begin(B - 1)
                attend(B - 1)
                output(B - 1)



def l0_ffn(nc, c, x_sb, mv, xT, w, psum):
    E, G, EG, LAT, SH = 32, 4, 8, 128, 512
    with ExitStack() as ctx:
        sb = lambda name, shape, dt=F32: ctx.enter_context(nc.sbuf_tensor("l0f_" + name, shape, dt))
        sem = lambda name: ctx.enter_context(nc.semaphore("l0f_" + name))
        xl = sb("xl", [LAT, TOK])
        relu = sb("relu", [P, 2, CN])
        sq = sb("sq", [P, 2, CN])
        hg = sb("hg", [P, 2, CN])
        hs = sb("hs", [P, SH // P, CN])
        yl = sb("yl", [LAT, CN])
        ex = sb("ex", [P, NT, E])
        sc = sb("sc", [P, NT, E])
        cand = sb("cand", [P, NT, E])
        left = sb("left", [P, NT, E])
        top = sb("top", [P, NT * G, 8])
        garr = sb("garr", [P, NT, 14])
        gpick = sb("gpick", [P, NT, 8])
        gtop = sb("gtop", [P, NT, 8])
        gout = sb("gout", [P, NT, 10])
        gsel = sb("gsel", [P, NT, G])
        wsum = sb("wsum", [P, NT])
        rest = sb("rest", [P, NT, E])
        c3 = sb("c3", [P, NT, 3, E], BF16)
        c3T = sb("c3T", [3 * E, TOK], BF16)
        lw = ln_scratch(sb, CH)
        HB = [psum[:, 0, :], psum[:, 1, :]]
        GB = [psum[:, 2, :], psum[:, 3, :]]
        YL = psum[:, 4, :]
        LOGITS = psum[:, 0, :].rearrange("p (t e) -> p t e", t=NT)
        Y = psum[:, 6:8, :].rearrange("p a (t n) -> p (a t) n", t=2)

        z_ready = sem("z_ready")
        route_steps = sem("route_steps")
        logit_ps = sem("logit_ps")
        ex_ready = sem("ex_ready")
        xl_ps = sem("xl_ps")
        xl_ready = sem("xl_ready")
        c3_ready = sem("c3_ready")
        c3T_ps = sem("c3T_ps")
        c3T_ready = sem("c3T_ready")
        h_ps = sem("h_ps")
        sq_ready = sem("sq_ready")
        hg_ready = sem("hg_ready")
        used = sem("used")
        yl_ready = sem("yl_ready")
        y_ps = sem("y_ps")
        relu_ready = sem("relu_ready")
        steps = sem("steps")
        NH = E + SH // P

        with nc.Block() as block:
            @block.tensor
            def _(pe):
                mm = nc.tensor.matmul
                w["early"](pe)
                for t in range(NT):
                    for k in range(KD):
                        last = mm(LOGITS[:, t, :], xT[:, k, t * P:(t + 1) * P], w["gate"][:, k, :], start=(k == 0), stop=(k == KD - 1))
                last.then_inc(logit_ps, 1)
                w["late"](pe)
                for j in range(NCH):
                    for k in range(KD):
                        last = mm(psum[:, 4 + j, :], w["fc1"][:, k, :], xT[:, k, j * CN:(j + 1) * CN], start=(k == 0), stop=(k == KD - 1))
                    last.then_inc(xl_ps, 1)
                pe.wait_ge(c3_ready, 1)
                for t in range(NT):
                    last = nc.tensor.transpose(psum[0:3 * E, 2 + t // 8, (t % 8) * P // 2:(t % 8 + 1) * P // 2].bitcast(BF16),
                                               c3[:, t, :, :].rearrange("p a e -> p (a e)"), c["idb"])
                last.then_inc(c3T_ps, 1)
                pe.wait_ge(c3T_ready, 1)
                pe.wait_ge(xl_ready, NCH)
                with pe.Fori(0, NCH) as b:
                    chunk = bass.ds(b * CN, CN)

                    def hidden(e):
                        if e >= 2:
                            pe.wait_ge(sq_ready, b * NH + e - 1)
                        if e < E:
                            if e >= 2:
                                pe.wait_ge(hg_ready, b * E + e - 1)
                            mm(GB[e % 2], c["sel0"][:, e * P:(e + 1) * P], c3T[:, chunk], start=True, stop=True)
                            mm(HB[e % 2], w["w1"][:, e, :], xl[:, chunk], start=True, stop=True).then_inc(h_ps, 1)
                        else:
                            m = e - E
                            for k in range(KD):
                                last = mm(HB[e % 2], w["up"][:, k, m * P:(m + 1) * P], xT[:, k, chunk], start=(k == 0), stop=(k == KD - 1))
                            last.then_inc(h_ps, 1)

                    def latent(e):
                        pe.wait_ge(hg_ready, b * E + e + 1)
                        mm(YL, w["w2"][:, e, :], hg[:, e % 2, :], start=(e == 0), stop=(e == E - 1)).then_inc(used, 1)

                    for e in range(NH):
                        hidden(e)
                        if 2 <= e < E + 2:
                            latent(e - 2)
                    pe.wait_ge(z_ready, b + 1)
                    pe.wait_ge(yl_ready, b + 1)
                    pe.wait_ge(sq_ready, b * NH + NH)
                    for t in range(CH):
                        for m in range(SH // P):
                            mm(Y[:, t, :], hs[:, m, t * P:(t + 1) * P], w["down"][:, m, :], start=(m == 0), stop=False)
                        last = mm(Y[:, t, :], yl[:, t * P:(t + 1) * P], w["fc2"][:, :], start=False, stop=True)
                    last.then_inc(y_ps, 1)

            @block.scalar
            def _(act):
                nc.scalar.preload_act_table(ACT.Exp)
                act.wait_ge(logit_ps, 1)
                nc.scalar.activation(ex[:, :, :], LOGITS, ACT.Exp, scale=-1.0).then_inc(ex_ready, 1)
                for j in range(NCH):
                    act.wait_ge(xl_ps, j + 1)
                    nc.scalar.activation(xl[:, j * CN:(j + 1) * CN], psum[:, 4 + j, :], ACT.Copy).then_inc(xl_ready, 1)
                with act.Fori(0, NCH) as b:
                    for e in range(NH):
                        act.wait_ge(h_ps, b * NH + e + 1)
                        if 2 <= e < E:
                            act.wait_ge(hg_ready, b * E + e - 1)
                        nc.scalar.activation(relu[:, e % 2, :], HB[e % 2], ACT.Relu).then_inc(relu_ready, 1)
                        act.wait_ge(relu_ready, b * NH + e + 1)
                        dst = sq[:, e % 2, :] if e < E else hs[:, e - E, :]
                        nc.scalar.activation(dst, relu[:, e % 2, :], ACT.Square).then_inc(sq_ready, 1)

            @block.vector
            def _(dve):
                nc.vector.memset(garr[:, :, 0:4], LOW)
                nc.vector.memset(garr[:, :, 8:14], BIG)
                nc.vector.memset(gpick[:, :, :], BIG)
                w["early"](dve)
                st = Steps(dve, route_steps, 0)
                st.begin(0)
                dve.wait_ge(ex_ready, 1)
                st.do(nc.vector.tensor_scalar(ex[:, :, :], ex[:, :, :], 1.0, None, ALU.add))
                st.do(nc.vector.reciprocal(sc[:, :, :], ex[:, :, :]))
                st.do(nc.vector.tensor_tensor(cand[:, :, :], sc[:, :, :], bc(w["bias"][:, :], 1, NT), ALU.add))
                for j in range(NT * G):
                    last = nc.vector.max(top[:, j, :], cand[:, j // G, (j % G) * EG:(j % G + 1) * EG])
                st.do(last)
                st.do(nc.vector.tensor_tensor(garr[:, :, 4:8], top[:, :, 0].rearrange("p (t g) -> p t g", g=G),
                                              top[:, :, 1].rearrange("p (t g) -> p t g", g=G), ALU.add))
                for t in range(NT):
                    last = nc.vector.max(gtop[:, t, :], garr[:, t, 0:8])
                st.do(last)
                st.do(nc.vector.tensor_copy(gpick[:, :, 0:2], gtop[:, :, 0:2]))
                for t in range(NT):
                    last = nc.vector.match_replace(gout[:, t, :], gpick[:, t, :], garr[:, t, 4:14], -BIG)
                st.do(last)
                st.do(nc.vector.tensor_scalar(gsel[:, :, :], gout[:, :, 0:4], -BIG, None, ALU.is_equal))
                st.do(nc.vector.tensor_scalar(gsel[:, :, :], gsel[:, :, :], -NEG, NEG, ALU.mult, ALU.add))
                st.do(nc.vector.tensor_tensor(cand[:, :, :].rearrange("p t (g e) -> p (t g) e", g=G),
                                              cand[:, :, :].rearrange("p t (g e) -> p (t g) e", g=G),
                                              bc(gsel[:, :, :].rearrange("p t g -> p (t g)"), 2, EG), ALU.add))
                for t in range(NT):
                    last = nc.vector.max(gtop[:, t, :], cand[:, t, :])
                st.do(last)
                for t in range(NT):
                    last = nc.vector.match_replace(left[:, t, :], gtop[:, t, :], cand[:, t, :], -BIG)
                st.do(last)
                st.do(nc.vector.scalar_tensor_tensor(left[:, :, :], left[:, :, :], -BIG, sc[:, :, :], ALU.is_equal, ALU.mult))
                st.do(nc.vector.tensor_reduce(wsum[:, :], left[:, :, :], AX.X, ALU.add))
                st.do(nc.vector.reciprocal(wsum[:, :], wsum[:, :]))
                st.do(nc.vector.scalar_tensor_tensor(left[:, :, :], left[:, :, :], 2.5, bc(wsum[:, :], 2, E), ALU.mult, ALU.mult))
                split3(nc, st, left[:, :, :], [c3[:, :, j, :] for j in range(3)], rest[:, :, :])
                nc.vector.memset(lw["carrier"][:, :], 0.0).then_inc(c3_ready, 1)
                dve.wait_ge(c3T_ps, 1)
                nc.vector.tensor_copy(c3T[:, :].rearrange("p (a n) -> p a n", a=2), psum[0:3 * E, 2:4, :].bitcast(BF16)).then_inc(c3T_ready, 1)
                dve.sem_inc(z_ready, 1)
                st = Steps(dve, steps, LN_STEPS)
                with dve.Fori(0, NCH) as b:
                    st.begin(b)
                    for e in range(E):
                        dve.wait_ge(sq_ready, b * NH + e + 1)
                        if e >= 2:
                            dve.wait_ge(used, b * E + e - 1)
                        nc.vector.tensor_tensor(hg[:, e % 2, :], sq[:, e % 2, :], GB[e % 2], ALU.mult).then_inc(hg_ready, 1)
                    dve.wait_ge(used, b * E + E)
                    nc.vector.tensor_copy(yl[:, :], YL).then_inc(yl_ready, 1)
                    dve.wait_ge(y_ps, b + 1)
                    add_and_measure(nc, st, x_sb, mv, b * CH, CH, Y, lw, z_ready, b + 2)
                    st.end()



def l1_attention(nc, c, x_sb, mv, xT, w, psum):
    H, HD = 16, 128
    EPS = 1e-5
    NJ = 8
    NG = H // 2
    with ExitStack() as ctx:
        sb = lambda name, shape, dt=F32: ctx.enter_context(nc.sbuf_tensor("l1a_" + name, shape, dt))
        sem = lambda name: ctx.enter_context(nc.semaphore("l1a_" + name))
        xc = sb("xc", [P, KD, T])
        qT = sb("qT", [HD, H, T])
        kT = sb("kT", [HD, H, T])
        va = sb("va", [P, TT, H * HD])
        ko = sb("ko", [P, H * T])
        kn = ko[:, :].rearrange("p (t h d) -> p (t h) d", t=TT, h=H)
        oT = ko[:, :].rearrange("p (h t) -> p h t", h=H)
        ksq = sb("ksq", [P, 2, 512])
        qsq = sb("qsq", [P, 2, 512])
        pr = sb("pr", [P, 2, 2, 3 * P])
        pt = sb("pt", [P, 2, 2, 3 * P])
        gain = sb("gain", [P, 1])
        ssk = sb("ssk", [P, TT * H])
        rk = sb("rk", [P, TT * H])
        rq = sb("rq", [P, TT, H])
        vv = sb("vv", [P, TT * H])
        tmp = sb("tmp", [P, TT * H])
        nm = sb("nm", [P, 2, TT, 2])
        nb = sb("nb", [P, 2, TT, 2])
        sums = sb("sums", [P, 2, TT, 2])
        rec = sb("rec", [P, 2, TT, 2])
        lw = ln_scratch(sb, TT)
        bank = lambda i: psum[:, i, :]
        S = [psum[:, 0:2, :], psum[:, 2:4, :]]
        PT = [bank(4), bank(5)]

        x_staged = sem("x_staged")
        xc_free = sem("xc_free")
        k_ps = sem("k_ps")
        q_ps = sem("q_ps")
        v_ps = sem("v_ps")
        k_out = sem("k_out")
        q_sq = sem("q_sq")
        q_out = sem("q_out")
        v_out = sem("v_out")
        k_sum = sem("k_sum")
        ssq_ps = sem("ssq_ps")
        kn_ready = sem("kn_ready")
        kT_ps = sem("kT_ps")
        kT_ready = sem("kT_ready")
        s_ps = sem("s_ps")
        nb_ready = sem("nb_ready")
        p_exp = sem("p_exp")
        p_norm = sem("p_norm")
        pt_ps = sem("pt_ps")
        pt_ready = sem("pt_ready")
        av_ps = sem("av_ps")
        o_ready = sem("o_ready")
        y_ps = sem("y_ps")
        z_ready = sem("z_ready")
        steps = sem("steps")

        with nc.Block() as block:
            @block.sync
            def _(sp):
                with sp.Fori(0, B) as b:
                    sp.wait_ge(xc_free, b + 1)
                    sp.dma_start(xc[:, :, :], xT[:, :, bass.ds(b * T, T)]).then_inc(x_staged, 16)

            @block.tensor
            def _(pe):
                mm = nc.tensor.matmul
                pe.sem_inc(xc_free, 1)
                w["early"](pe)
                w["late"](pe)
                with pe.Fori(0, B) as b:
                    pe.wait_ge(x_staged, b * 16 + 16)

                    def square_sums(j):
                        pe.wait_ge(q_sq, b * NJ + j + 1)
                        pe.wait_ge(q_out, b * NJ + 1)
                        for i in range(2):
                            for t in range(TT):
                                h = 2 * j + i
                                last = mm(bank(4)[:, t * H + h:t * H + h + 1], qsq[:, j % 2, i * T + t * P:i * T + (t + 1) * P],
                                          c["one"], start=True, stop=True)
                        last.then_inc(ssq_ps, 1)

                    for j in range(NJ):
                        t, cols = j // 4, slice((j % 4) * 512, (j % 4 + 1) * 512)
                        if j >= 2:
                            pe.wait_ge(k_out, b * NJ + j - 1)
                        for k in range(KD):
                            last = mm(bank(j % 2), xc[:, k, t * P:(t + 1) * P], w["k"][:, k, cols], start=(k == 0), stop=(k == KD - 1))
                        last.then_inc(k_ps, 1)

                    def turn_keys(m):
                        if m >= 2:
                            pe.wait_ge(kT_ready, b * NG + m - 1)
                        for i in range(2):
                            for t in range(TT):
                                last = nc.tensor.transpose(bank(m % 2)[:, i * T + t * P:i * T + (t + 1) * P],
                                                           kn[:, t * H + 2 * m + i, :], c["id"])
                        last.then_inc(kT_ps, 1)

                    for j in range(NJ):
                        t, cols = j // 4, slice((j % 4) * 512, (j % 4 + 1) * 512)
                        if j >= 2:
                            pe.wait_ge(q_out, b * NJ + j - 1)
                        for i in range(2):
                            for k in range(KD):
                                last = mm(bank(2 + j % 2)[:, i * T:(i + 1) * T], w["q"][:, k, (2 * j + i) * HD:(2 * j + i + 1) * HD],
                                          xc[:, k, :], start=(k == 0), stop=(k == KD - 1))
                        last.then_inc(q_ps, 1)
                        if j >= 2:
                            pe.wait_ge(v_out, b * NJ + j - 1)
                        for k in range(KD):
                            last = mm(bank(6 + j % 2), xc[:, k, t * P:(t + 1) * P], w["v"][:, k, cols], start=(k == 0), stop=(k == KD - 1))
                        last.then_inc(v_ps, 1)
                        if j >= 1:
                            square_sums(j - 1)
                        if j == 3:
                            pe.wait_ge(kn_ready, b + 1)
                        if j >= 3:
                            turn_keys(j - 3)
                    pe.wait_ge(v_ps, b * NJ + NJ)
                    pe.sem_inc(xc_free, 1)
                    square_sums(NJ - 1)
                    for m in range(NJ - 3, NG):
                        turn_keys(m)
                    pe.wait_ge(q_out, b * NJ + NJ)

                    def scores(n):
                        if n < 2:
                            pe.wait_ge(kT_ready, b * NG + NG)
                        else:
                            pe.wait_ge(p_exp, b * NG + n - 1)
                        for i in range(2):
                            h = 2 * n + i
                            for t in range(TT):
                                mm(S[n % 2][:, i, t * P:t * P + (t + 1) * P], qT[:, h, t * P:(t + 1) * P], kT[:, h, 0:(t + 1) * P],
                                   start=True, stop=False)
                                last = mm(S[n % 2][:, i, 2 * t * P:(2 * t + 1) * P], c["idb"], c["maskb"], start=False, stop=True)
                        last.then_inc(s_ps, 1)

                    def turn(n):
                        pe.wait_ge(p_norm, b * NG + n + 1)
                        for i in range(2):
                            if n > 0:
                                pe.wait_ge(pt_ready, b * 2 * NG + 2 * (n - 1) + i + 1)
                            for j in range(3):
                                last = nc.tensor.transpose(PT[i][:, j * P:(j + 1) * P], pr[:, n % 2, i, j * P:(j + 1) * P], c["id"])
                            last.then_inc(pt_ps, 1)

                    def values(n):
                        if n >= 2:
                            pe.wait_ge(o_ready, b * NG + n - 1)
                        for i in range(2):
                            h = 2 * n + i
                            pe.wait_ge(pt_ready, b * 2 * NG + 2 * n + i + 1)
                            pp, o = pt[:, n % 2, i, :], bank(6 + n % 2)[:, i * T:(i + 1) * T]
                            mm(o, va[:, 0, h * HD:(h + 1) * HD], pp[:, 0:2 * P], start=True, stop=False)
                            last = mm(o[:, P:2 * P], va[:, 1, h * HD:(h + 1) * HD], pp[:, 2 * P:3 * P], start=False, stop=True)
                        last.then_inc(av_ps, 1)

                    for n in range(NG + 3):
                        if n < NG:
                            scores(n)
                        if 2 <= n < NG + 2:
                            turn(n - 2)
                        if n >= 3:
                            values(n - 3)
                    pe.wait_ge(o_ready, b * NG + NG)
                    for t in range(TT):
                        for h in range(H):
                            last = mm(PT[0][:, t * D:(t + 1) * D], oT[:, h, t * P:(t + 1) * P], w["o"][:, h, :],
                                      start=(h == 0), stop=(h == H - 1))
                    last.then_inc(y_ps, 1)

            @block.scalar
            def _(act):
                nc.scalar.preload_act_table(ACT.Exp)
                with act.Fori(0, B) as b:
                    for j in range(NJ):
                        t, j4 = j // 4, j % 4
                        act.wait_ge(k_ps, b * NJ + j + 1)
                        if j >= 2:
                            act.wait_ge(k_sum, b * NJ + j - 1)
                        nc.scalar.activation(kn[:, t * H + 4 * j4:t * H + 4 * j4 + 4, :],
                                             bank(j % 2).rearrange("p (h d) -> p h d", h=4), ACT.Copy)
                        nc.scalar.activation(ksq[:, j % 2, :], bank(j % 2), ACT.Square).then_inc(k_out, 1)

                    def keys_out(m):
                        act.wait_ge(kT_ps, b * NG + m + 1)
                        nc.scalar.activation(kT[:, 2 * m:2 * m + 2, :], bank(m % 2).rearrange("p (i t) -> p i t", i=2), ACT.Copy,
                                             scale=gain[:, :]).then_inc(kT_ready, 1)

                    for j in range(NJ):
                        act.wait_ge(q_out, b * NJ + j + 1)
                        if j >= 2:
                            act.wait_ge(ssq_ps, b * NJ + j - 1)
                        nc.scalar.activation(qsq[:, j % 2, :], qT[:, 2 * j:2 * j + 2, :].rearrange("p i t -> p (i t)"), ACT.Square).then_inc(q_sq, 1)
                        if j >= 3:
                            keys_out(j - 3)
                    for m in range(NJ - 3, NG):
                        keys_out(m)

                    def out(n):
                        act.wait_ge(av_ps, b * NG + n + 1)
                        nc.scalar.activation(oT[:, 2 * n:2 * n + 2, :], bank(6 + n % 2).rearrange("p (i t) -> p i t", i=2),
                                             ACT.Copy).then_inc(o_ready, 1)

                    for n in range(NG + 3):
                        if n < NG:
                            act.wait_ge(nb_ready, b * NG + n + 1)
                            if n >= 2:
                                act.wait_ge(pt_ps, b * 2 * NG + 2 * (n - 1))
                            for i in range(2):
                                for t in range(TT):
                                    s = slice(t * P, t * P + (t + 1) * P)
                                    last = nc.scalar.activation(pr[:, n % 2, i, s], S[n % 2][:, i, s], ACT.Exp,
                                                                bias=nb[:, n % 2, t, i:i + 1], scale=rq[:, t, 2 * n + i:2 * n + i + 1],
                                                                accum_out=sums[:, n % 2, t, i:i + 1])
                            last.then_inc(p_exp, 1)
                        if n >= 3:
                            out(n - 3)

            @block.vector
            def _(dve):
                st = Steps(dve, steps, L1A_STEPS)
                w["early"](dve)
                nc.vector.tensor_tensor(gain[:, :], w["gq"], w["gk"], ALU.mult)
                with dve.Fori(0, B) as b:
                    st.begin(b)
                    for j in range(NJ):
                        dve.wait_ge(k_out, b * NJ + j + 1)
                        nc.vector.tensor_reduce(ssk[:, 4 * j:4 * j + 4], ksq[:, j % 2, :].rearrange("p (h d) -> p h d", h=4),
                                                AX.X, ALU.add).then_inc(k_sum, 1)

                    def queries_and_values_out(j):
                        t, cols = j // 4, slice((j % 4) * 512, (j % 4 + 1) * 512)
                        dve.wait_ge(q_ps, b * NJ + j + 1)
                        nc.vector.tensor_copy(qT[:, 2 * j:2 * j + 2, :], bank(2 + j % 2).rearrange("p (i t) -> p i t", i=2)).then_inc(q_out, 1)
                        dve.wait_ge(v_ps, b * NJ + j + 1)
                        nc.vector.tensor_copy(va[:, t, cols], bank(6 + j % 2)).then_inc(v_out, 1)

                    dve.wait_ge(k_sum, b * NJ + NJ)
                    st.do(nc.vector.tensor_scalar(vv[:, :], ssk[:, :], 1.0 / HD, EPS, ALU.mult, ALU.add))
                    newton_rsqrt(nc, st, vv[:, :], rk[:, :], tmp[:, :])
                    st.wait()
                    for j in range(NJ):
                        queries_and_values_out(j)
                        if j < 2:
                            part = slice(j * H, (j + 1) * H)
                            last = nc.vector.tensor_tensor(kn[:, part, :], kn[:, part, :], bc(rk[:, part], 2, HD), ALU.mult)
                            if j == 1:
                                last.then_inc(kn_ready, 1)
                    dve.wait_ge(ssq_ps, b * NJ + NJ)
                    st.do(nc.vector.tensor_scalar(vv[:, :], bank(4)[:, 0:TT * H], 1.0 / HD, EPS, ALU.mult, ALU.add))
                    flat = rq[:, :, :].rearrange("p t h -> p (t h)")
                    newton_rsqrt(nc, st, vv[:, :], flat, tmp[:, :])
                    st.wait()
                    st.do(nc.vector.tensor_scalar(flat, flat, float(HD) ** -0.5, None, ALU.mult))

                    def maxima(n):
                        dve.wait_ge(s_ps, b * NG + n + 1)
                        if n >= 2:
                            dve.wait_ge(p_exp, b * NG + n - 1)
                        for t in range(TT):
                            last = nc.vector.tensor_reduce(nm[:, n % 2, t, :], S[n % 2][:, :, t * P:t * P + (t + 1) * P],
                                                           AX.X, ALU.max, negate=True)
                        st.do(last)
                        nc.vector.tensor_tensor(nb[:, n % 2, :, :], nm[:, n % 2, :, :], rq[:, :, 2 * n:2 * n + 2], ALU.mult).then_inc(nb_ready, 1)

                    def normalise(n):
                        dve.wait_ge(p_exp, b * NG + n + 1)
                        st.do(nc.vector.reciprocal(rec[:, n % 2, :, :], sums[:, n % 2, :, :]))
                        for i in range(2):
                            for t in range(TT):
                                s = slice(t * P, t * P + (t + 1) * P)
                                last = nc.vector.tensor_scalar(pr[:, n % 2, i, s], pr[:, n % 2, i, s], rec[:, n % 2, t, i:i + 1], None, ALU.mult)
                        last.then_inc(p_norm, 1)

                    def out_of_psum(n):
                        for i in range(2):
                            dve.wait_ge(pt_ps, b * 2 * NG + 2 * n + i + 1)
                            if n >= 2:
                                dve.wait_ge(av_ps, b * NG + n - 1)
                            nc.vector.tensor_copy(pt[:, n % 2, i, :], PT[i][:, 0:3 * P]).then_inc(pt_ready, 1)

                    for n in range(NG + 2):
                        if n < NG:
                            maxima(n)
                        if 1 <= n <= NG:
                            normalise(n - 1)
                        if n >= 2:
                            out_of_psum(n - 2)
                    dve.wait_ge(y_ps, b + 1)
                    add_and_measure(nc, st, x_sb, mv, b * TT, TT, PT[0].rearrange("p (t n) -> p t n", t=TT), lw, z_ready)
                    st.end()


L1A_STEPS = 1 + NEWTON_STEPS + 1 + NEWTON_STEPS + 1 + 2 * 8 + LN_STEPS



def l1_ffn(nc, c, x_sb, mv, xT, w, psum):
    E, K, I, TOP, SH = 128, 8, 128, 4, 2
    EPS = 1e-8
    NH = K + SH
    with ExitStack() as ctx:
        sb = lambda name, shape, dt=F32: ctx.enter_context(nc.sbuf_tensor("l1f_" + name, shape, dt))
        sem = lambda name: ctx.enter_context(nc.semaphore("l1f_" + name))
        mp = sb("mp", [P, K, 2])
        mix = sb("mix", [P, K])
        msum = sb("msum", [P, 1])
        mixb = sb("mixb", [P, K, I])
        pb = sb("pb", [P, NT, E + 8 - TOP])
        nm = sb("nm", [P, NT])
        sums = sb("sums", [P, NT])
        top = sb("top", [P, NT, 8])
        pick = sb("pick", [P, NT, 8])
        left = sb("left", [P, NT, E + 8 - TOP])
        co = sb("co", [P, NT, E])
        wsum = sb("wsum", [P, NT])
        coT = sb("coT", [E, TOK])
        sg = sb("sg", [P, 2, CN])
        gu = sb("gu", [P, 2, CN])
        t2 = sb("t2", [P, 2, CN])
        acc = sb("acc", [I, CN])
        hs = sb("hs", [P, SH, CN])
        lw = ln_scratch(sb, CH)
        bank = lambda i: psum[:, i, :]
        GB, UB, CB = [bank(0), bank(1)], [bank(2), bank(3)], [bank(4), bank(5)]
        Y = psum[:, 6:8, :].rearrange("p a (t n) -> p (a t) n", t=2)
        LOGITS = psum[:, 0:4, :].rearrange("p a (t e) -> p (a t) e", e=E)

        route_steps = sem("route_steps")
        z_ready = sem("z_ready")
        logit_ps = sem("logit_ps")
        nm_ready = sem("nm_ready")
        ex_ready = sem("ex_ready")
        co_ready = sem("co_ready")
        coT_ps = sem("coT_ps")
        coT_ready = sem("coT_ready")
        mix_ready = sem("mix_ready")
        h_ps = sem("h_ps")
        sg_ready = sem("sg_ready")
        gu_ready = sem("gu_ready")
        t2_ready = sem("t2_ready")
        acc_ready = sem("acc_ready")
        y_ps = sem("y_ps")
        mix_steps = sem("mix_steps")
        steps = sem("steps")

        with nc.Block() as block:
            @block.tensor
            def _(pe):
                mm = nc.tensor.matmul
                w["early"](pe)
                for t in range(NT):
                    for k in range(KD):
                        last = mm(LOGITS[:, t, :], xT[:, k, t * P:(t + 1) * P], w["router"][:, k, :], start=(k == 0), stop=(k == KD - 1))
                last.then_inc(logit_ps, 1)
                pe.wait_ge(mix_ready, 1)
                pe.wait_ge(co_ready, 1)
                for t in range(NT):
                    last = nc.tensor.transpose(psum[:, 4 + t // 4, (t % 4) * P:(t % 4 + 1) * P], co[:, t, :], c["id"])
                last.then_inc(coT_ps, 1)
                pe.wait_ge(coT_ready, 1)
                w["late"](pe)
                with pe.Fori(0, NCH) as b:
                    chunk = bass.ds(b * CN, CN)
                    for e in range(NH):
                        if e >= 2:
                            pe.wait_ge(gu_ready, b * NH + e - 1)
                        wg, wu, m = ("gate", "up", e) if e < K else ("sgate", "sup", e - K)
                        for k in range(KD):
                            mm(GB[e % 2], w[wg][:, k, m * I:(m + 1) * I], xT[:, k, chunk], start=(k == 0), stop=(k == KD - 1))
                        for k in range(KD):
                            last = mm(UB[e % 2], w[wu][:, k, m * I:(m + 1) * I], xT[:, k, chunk], start=(k == 0), stop=(k == KD - 1))
                        if e < K:
                            if e >= 2:
                                pe.wait_ge(t2_ready, b * K + e - 1)
                            last = mm(CB[e % 2], mixb[:, e, :], coT[:, chunk], start=True, stop=True)
                        last.then_inc(h_ps, 1)
                    pe.wait_ge(gu_ready, b * NH + NH)
                    pe.wait_ge(acc_ready, b * (K - 1) + K - 1)
                    pe.wait_ge(z_ready, b + 1)
                    for t in range(CH):
                        for m in range(SH):
                            mm(Y[:, t, :], hs[:, m, t * P:(t + 1) * P], w["sdown"][:, m, :], start=(m == 0), stop=False)
                        last = mm(Y[:, t, :], acc[:, t * P:(t + 1) * P], w["down"], start=False, stop=True)
                    last.then_inc(y_ps, 1)

            @block.scalar
            def _(act):
                act.wait_ge(nm_ready, 1)
                for t in range(NT):
                    last = nc.scalar.activation(pb[:, t, 0:E], LOGITS[:, t, :], ACT.Exp, bias=nm[:, t:t + 1], accum_out=sums[:, t:t + 1])
                last.then_inc(ex_ready, 1)
                nc.scalar.preload_act_table(ACT.Silu)
                with act.Fori(0, NCH) as b:
                    for e in range(NH):
                        act.wait_ge(h_ps, b * NH + e + 1)
                        if e >= 2:
                            act.wait_ge(gu_ready, b * NH + e - 1)
                        nc.scalar.activation(sg[:, e % 2, :], GB[e % 2], ACT.Silu).then_inc(sg_ready, 1)

            @block.gpsimd
            def _(pool):
                with pool.Fori(0, NCH) as b:
                    for k in range(1, K):
                        pool.wait_ge(t2_ready, b * K + k + 1)
                        if k == 1:
                            pool.wait_ge(y_ps, b + 1)
                        else:
                            pool.wait_ge(acc_ready, b * (K - 1) + k - 1)
                        nc.gpsimd.tensor_tensor(acc[:, :], t2[:, 0, :] if k == 1 else acc[:, :], t2[:, k % 2, :], ALU.add).then_inc(acc_ready, 1)

            @block.vector
            def _(dve):
                w["early"](dve)
                dve.sem_inc(y_ps, 1)
                one = lambda ins, n: (ins.then_inc(mix_steps, 1), dve.wait_ge(mix_steps, n))
                one(nc.vector.tensor_tensor(mp[:, :, :], w["amp"], w["amp"], ALU.mult), 1)
                one(nc.vector.tensor_tensor(mix[:, :], mp[:, :, 0], mp[:, :, 1], ALU.add), 2)
                one(nc.vector.tensor_reduce(msum[:, :], mix[:, :], AX.X, ALU.add), 3)
                one(nc.vector.tensor_scalar(msum[:, :], msum[:, :], EPS, None, ALU.add), 4)
                one(nc.vector.reciprocal(msum[:, :], msum[:, :]), 5)
                one(nc.vector.tensor_scalar(mix[:, :], mix[:, :], msum[:, :], w["escale"], ALU.mult, ALU.mult), 6)
                nc.vector.tensor_copy(mixb[:, :, :], bc(mix[:, :], 2, I)).then_inc(mix_ready, 1)
                nc.vector.memset(pb[:, :, E:], BIG)
                nc.vector.memset(pick[:, :, :], BIG)
                st = Steps(dve, route_steps, 0)
                st.begin(0)
                dve.wait_ge(logit_ps, 1)
                nc.vector.tensor_reduce(nm[:, :], LOGITS, AX.X, ALU.max, negate=True).then_inc(nm_ready, 1)
                dve.wait_ge(ex_ready, 1)
                st.do(nc.vector.reciprocal(wsum[:, :], sums[:, :]))
                st.do(nc.vector.tensor_tensor(pb[:, :, 0:E], pb[:, :, 0:E], bc(wsum[:, :], 2, E), ALU.mult))
                for t in range(NT):
                    last = nc.vector.max(top[:, t, :], pb[:, t, 0:E])
                st.do(last)
                st.do(nc.vector.tensor_copy(pick[:, :, 0:TOP], top[:, :, 0:TOP]))
                for t in range(NT):
                    last = nc.vector.match_replace(left[:, t, :], pick[:, t, :], pb[:, t, :], -BIG)
                st.do(last)
                st.do(nc.vector.scalar_tensor_tensor(co[:, :, :], left[:, :, 0:E], -BIG, pb[:, :, 0:E], ALU.is_equal, ALU.mult))
                st.do(nc.vector.tensor_reduce(wsum[:, :], co[:, :, :], AX.X, ALU.add))
                st.do(nc.vector.tensor_scalar(wsum[:, :], wsum[:, :], EPS, None, ALU.add))
                st.do(nc.vector.reciprocal(wsum[:, :], wsum[:, :]))
                nc.vector.tensor_tensor(co[:, :, :], co[:, :, :], bc(wsum[:, :], 2, E), ALU.mult).then_inc(co_ready, 1)
                dve.wait_ge(coT_ps, 1)
                nc.vector.tensor_copy(coT[:, :].rearrange("p (a n) -> p a n", a=4), psum[:, 4:8, :]).then_inc(coT_ready, 1)
                dve.sem_inc(z_ready, 1)
                st = Steps(dve, steps, LN_STEPS)
                with dve.Fori(0, NCH) as b:
                    st.begin(b)

                    def weigh(k):
                        dve.wait_ge(gu_ready, b * NH + k + 1)
                        if k >= 2:
                            dve.wait_ge(acc_ready, b * (K - 1) + max(k - 2, 1))
                        nc.vector.tensor_tensor(t2[:, k % 2, :], gu[:, k % 2, :], CB[k % 2], ALU.mult).then_inc(t2_ready, 1)

                    for e in range(NH):
                        dve.wait_ge(sg_ready, b * NH + e + 1)
                        dst = gu[:, e % 2, :] if e < K else hs[:, e - K, :]
                        nc.vector.tensor_tensor(dst, sg[:, e % 2, :], UB[e % 2], ALU.mult).then_inc(gu_ready, 1)
                        if 1 <= e <= K:
                            weigh(e - 1)
                    dve.wait_ge(y_ps, b + 2)
                    add_and_measure(nc, st, x_sb, mv, b * CH, CH, Y, lw, z_ready, b + 2)
                    st.end()



def l2_mixing(nc, c, x_sb, mv, xT, w, psum):
    R, DH = 256, 64
    with ExitStack() as ctx:
        sb = lambda name, shape, dt=F32: ctx.enter_context(nc.sbuf_tensor("l2a_" + name, shape, dt))
        sem = lambda name: ctx.enter_context(nc.semaphore("l2a_" + name))
        hT = sb("hT", [DH, 2, T])
        ga = sb("ga", [P, 2, 2, T])
        ug = sb("ug", [P, 2, 2, T])
        vg = sb("vg", [P, 2, 2, T])
        cum = sb("cum", [P, 2, 2, T])
        go = sb("go", [P, 2, 2, T])
        tc = sb("tc", [P, 2, KD, T])
        ones = sb("ones", [P, T])
        lw = ln_scratch(sb, TT)
        bank = lambda i: psum[:, i, :]
        two = lambda ap: ap.rearrange("p (k t) -> p k t", k=2)
        HY, U, V, GG = [bank(0), bank(1)], [bank(2), bank(3)], [bank(4), bank(5)], [bank(6), bank(7)]

        h_ps = sem("h_ps")
        h_ready = sem("h_ready")
        uv_ps = sem("uv_ps")
        g_ps = sem("g_ps")
        ga_ready = sem("ga_ready")
        mix_ready = sem("mix_ready")
        y_ps = sem("y_ps")
        z_ready = sem("z_ready")
        steps = sem("steps")

        with nc.Block() as block:
            @block.tensor
            def _(pe):
                mm = nc.tensor.matmul
                w["early"](pe)
                w["late"](pe)
                pe.sem_inc(z_ready, 2)
                with pe.Fori(0, B // 2) as b:
                    for i in range(2):
                        x = lambda k: xT[:, k, bass.ds(b * 2 * T + i * T, T)]
                        pe.wait_ge(z_ready, 2 * b + i + 1)
                        for k in range(KD):
                            last = mm(HY[i][0:DH, 0:T], w["g1"][:, k, :], x(k), start=(k == 0), stop=(k == KD - 1))
                        last.then_inc(h_ps, 1)
                        for name, bk in (("u", U), ("v", V)):
                            for m in range(2):
                                for k in range(KD):
                                    last = mm(bk[i][:, m * T:(m + 1) * T], w[name][:, k, m * P:(m + 1) * P], x(k),
                                              start=(k == 0), stop=(k == KD - 1))
                        last.then_inc(uv_ps, 1)
                        pe.wait_ge(h_ready, 2 * b + i + 1)
                        for m in range(2):
                            last = mm(GG[i][:, m * T:(m + 1) * T], w["g2"][0:DH, m * P:(m + 1) * P], hT[:, i, :], start=True, stop=True)
                        last.then_inc(g_ps, 1)
                    for i in range(2):
                        pe.wait_ge(mix_ready, 2 * b + i + 1)
                        for t in range(TT):
                            y = HY[i][:, t * D:(t + 1) * D]
                            for k in range(2):
                                mm(y, go[:, i, k, t * P:(t + 1) * P], w["u"][:, k, :], start=(k == 0), stop=False)
                            for k in range(KD):
                                last = mm(y[:, k * P:(k + 1) * P], tc[:, i, k, t * P:(t + 1) * P], c["id"], start=False, stop=(k == KD - 1))
                        last.then_inc(y_ps, 1)

            @block.scalar
            def _(act):
                nc.scalar.preload_act_table(ACT.Sigmoid)
                w["late"](act)
                with act.Fori(0, B // 2) as b:
                    for i in range(2):
                        act.wait_ge(h_ps, 2 * b + i + 1)
                        nc.scalar.activation(hT[:, i, :], HY[i][0:DH, 0:T], ACT.Relu, bias=w["bg1"][0:DH, :]).then_inc(h_ready, 1)
                        act.wait_ge(g_ps, 2 * b + i + 1)
                        for m in range(2):
                            last = nc.scalar.activation(ga[:, i, m, :], GG[i][:, m * T:(m + 1) * T], ACT.Sigmoid, bias=w["bg2"][:, m:m + 1])
                        last.then_inc(ga_ready, 1)

            @block.vector
            def _(dve):
                st = Steps(dve, steps, L2A_STEPS)
                nc.vector.memset(ones[:, :], 1.0)
                w["early"](dve)
                w["late"](dve)
                with dve.Fori(0, B // 2) as b:
                    st.begin(b)
                    for i in range(2):
                        dve.wait_ge(h_ps, 2 * b + i + 1)
                        x = lambda k, at, n: xT[:, k, bass.ds(b * 2 * T + i * T + at, n)]
                        for k in range(KD):
                            last = nc.vector.tensor_scalar(tc[:, i, k, :], x(k, 0, T), w["conv"][:, k, 1:2], w["convb"][:, k:k + 1], ALU.mult, ALU.add)
                        st.do(last)
                        for k in range(KD):
                            last = nc.vector.scalar_tensor_tensor(tc[:, i, k, 1:T], x(k, 0, T - 1), w["conv"][:, k, 0:1], tc[:, i, k, 1:T], ALU.mult, ALU.add)
                        st.do(last)
                        for k in range(KD):
                            last = nc.vector.scalar_tensor_tensor(tc[:, i, k, 0:T - 1], x(k, 1, T - 1), w["conv"][:, k, 2:3], tc[:, i, k, 0:T - 1], ALU.mult, ALU.add)
                        st.do(last)
                        dve.wait_ge(uv_ps, 2 * b + i + 1)
                        dve.wait_ge(ga_ready, 2 * b + i + 1)
                        for m in range(2):
                            nc.vector.scalar_tensor_tensor(ug[:, i, m, :], U[i][:, m * T:(m + 1) * T], w["bu"][:, m:m + 1], ga[:, i, m, :], ALU.add, ALU.mult)
                            last = nc.vector.scalar_tensor_tensor(vg[:, i, m, :], V[i][:, m * T:(m + 1) * T], w["bv"][:, m:m + 1], ga[:, i, m, :], ALU.add, ALU.mult)
                        st.do(last)
                        for m in range(2):
                            last = nc.vector.tensor_tensor_scan(cum[:, i, m, :], ones[:, :], ug[:, i, m, :], 0.0, ALU.mult, ALU.add)
                        st.do(last)
                        nc.vector.tensor_tensor(go[:, i, :, :], cum[:, i, :, :], vg[:, i, :, :], ALU.mult).then_inc(mix_ready, 1)
                    for i in range(2):
                        dve.wait_ge(y_ps, 2 * b + i + 1)
                        add_and_measure(nc, st, x_sb, mv, b * 2 * TT + i * TT, TT, two(HY[i]), lw, z_ready, 2 * b + i + 3)
                    st.end()


L2A_STEPS = 2 * (5 + LN_STEPS)



def l2_ffn(nc, c, x_sb, mv, xT, w, psum):
    I, SETS = 1024, 2
    NH = I // P
    with ExitStack() as ctx:
        sb = lambda name, shape, dt=F32: ctx.enter_context(nc.sbuf_tensor("l2f_" + name, shape, dt))
        sem = lambda name: ctx.enter_context(nc.semaphore("l2f_" + name))
        sg = sb("sg", [P, 2, CN])
        hh = sb("hh", [P, SETS, 2, 2, CN])
        ab = sb("ab", [P, 2, 2, CN])
        big = sb("big", [P, 2, CN])
        small = sb("small", [P, 2, CN])
        win = sb("win", [P, 2, 2, CN], BF16)
        both = sb("both", [P, 3, CN], BF16)
        zero = sb("zero", [P, P], BF16)
        lw = ln_scratch(sb, CH)
        bank = lambda i: psum[:, i, :]
        Y = psum[:, 6:8, :].rearrange("p a (t n) -> p (a t) n", t=2)

        h_ps = sem("h_ps")
        sg_ready = sem("sg_ready")
        hh_ready = sem("hh_ready")
        ab_ready = sem("ab_ready")
        kept = sem("kept")
        y_ps = sem("y_ps")
        z_ready = sem("z_ready")
        steps = sem("steps")
        zero_ready = sem("zero_ready")

        with nc.Block() as block:
            @block.tensor
            def _(pe):
                mm = nc.tensor.matmul
                pe.wait_ge(zero_ready, 1)

                def clear_output():
                    for a in (6, 7):
                        mm(bank(a), zero[:, :], c["finite"], start=True, stop=False)

                w["early"](pe)
                pe.sem_inc(z_ready, 1)
                w["late"](pe)
                with pe.Fori(0, NCH) as b:
                    for e in range(NH):
                        if e >= 2:
                            pe.wait_ge(hh_ready, b * NH + e - 1)
                        for name, bk in (("gate", 0), ("up", 2)):
                            for k in range(KD):
                                last = mm(bank(bk + e % 2), w[name][:, k, e * P:(e + 1) * P], xT[:, k, bass.ds(b * CN, CN)],
                                          start=(k == 0), stop=(k == KD - 1))
                        last.then_inc(h_ps, 1)
                    pe.wait_ge(z_ready, b + 1)
                    clear_output()
                    for s in range(SETS):
                        pe.wait_ge(kept, b * SETS + s + 2)
                        for t in range(CH):
                            for e in range(4 * s, 4 * s + 4):
                                last = mm(Y[:, t, :], hh[:, s, e % 4 // 2, e % 2, t * P:(t + 1) * P], w["down"][:, e, :],
                                          start=False, stop=(e == NH - 1 and t % 2 == 1))
                    last.then_inc(y_ps, 1)

            @block.scalar
            def _(act):
                nc.scalar.preload_act_table(ACT.Silu)
                with act.Fori(0, NCH) as b:
                    def magnitudes(s):
                        act.wait_ge(hh_ready, b * NH + 4 * s + 4)
                        act.wait_ge(kept, b * SETS + s + 1)
                        nc.scalar.activation(ab[:, :, :, :], hh[:, s, :, :, :], ACT.Abs).then_inc(ab_ready, 1)

                    for e in range(NH):
                        act.wait_ge(h_ps, b * NH + e + 1)
                        if e >= 2:
                            act.wait_ge(hh_ready, b * NH + e - 1)
                        nc.scalar.activation(sg[:, e % 2, :], bank(e % 2), ACT.Silu).then_inc(sg_ready, 1)
                        if e == 4:
                            magnitudes(0)
                    magnitudes(1)

            @block.vector
            def _(dve):
                nc.vector.memset(zero[:, :], 0.0).then_inc(zero_ready, 1)
                st = Steps(dve, steps, L2F_STEPS)
                dve.sem_inc(kept, 1)
                with dve.Fori(0, NCH) as b:
                    st.begin(b)

                    def prune(s):
                        a0, a1 = ab[:, :, 0, :], ab[:, :, 1, :]
                        dve.wait_ge(ab_ready, b * SETS + s + 1)
                        nc.vector.tensor_tensor(big[:, :, :], a0, a1, ALU.max)
                        nc.vector.tensor_tensor(small[:, :, :], a0, a1, ALU.min)
                        nc.vector.tensor_tensor(win[:, :, 0, :], a0, a1, ALU.is_ge)
                        st.do(nc.vector.tensor_tensor(win[:, :, 1, :], a0, a1, ALU.is_lt))
                        nc.vector.tensor_tensor(both[:, 0, :], small[:, 0, :], big[:, 1, :], ALU.is_ge)
                        nc.vector.tensor_tensor(both[:, 1, :], small[:, 1, :], big[:, 0, :], ALU.is_gt)
                        st.do(nc.vector.tensor_tensor(both[:, 2, :], small[:, 0, :], big[:, 1, :], ALU.is_ge))
                        for q in range(2):
                            last = nc.vector.tensor_tensor(win[:, q, :, :], win[:, q, :, :], bc(both[:, q + 1, :], 1, 2), ALU.subtract)
                        st.do(last)
                        for q in range(2):
                            last = nc.vector.tensor_tensor(win[:, q, :, :], win[:, q, :, :], bc(both[:, q, :], 1, 2), ALU.max)
                        st.do(last)
                        nc.vector.tensor_tensor(hh[:, s, :, :, :], hh[:, s, :, :, :], win[:, :, :, :], ALU.mult).then_inc(kept, 1)

                    for e in range(NH):
                        dve.wait_ge(sg_ready, b * NH + e + 1)
                        nc.vector.tensor_tensor(hh[:, e // 4, e % 4 // 2, e % 2, :], sg[:, e % 2, :], bank(2 + e % 2), ALU.mult).then_inc(hh_ready, 1)
                        if e == 5:
                            prune(0)
                    prune(1)
                    dve.wait_ge(y_ps, b + 1)
                    add_and_measure(nc, st, x_sb, mv, b * CH, CH, Y, lw, z_ready, b + 2)
                    st.end()


L2F_STEPS = 2 * 4 + LN_STEPS



def l3_attention(nc, c, x_sb, mv, xT, w, psum):
    HD, G, R, A = 16, 4, 4, 2
    H = G * R
    V1 = HD + 1
    LAM_INIT = 0.8 - 0.6 * float(np.exp(-0.3 * 0))
    EPS = 1e-8
    NG = H // 2
    with ExitStack() as ctx:
        sb = lambda name, shape, dt=F32: ctx.enter_context(nc.sbuf_tensor("l3a_" + name, shape, dt))
        sem = lambda name: ctx.enter_context(nc.semaphore("l3a_" + name))
        xc = sb("xc", [P, KD, T])
        qr = sb("qr", [P, A, R, T])
        k1 = sb("k1", [P, A, 2, T])
        kr = sb("kr", [P, G, A, T])
        va = sb("va", [P, TT, G, V1])
        lam = sb("lam", [P, 2, H])
        lprod = sb("lprod", [P, 2, H, HD])
        nlam = sb("nlam", [P, H])
        gain = sb("gain", [P, HD])
        nm = sb("nm", [P, 2, TT, A])
        sums = sb("sums", [P, 2, A, 2, TT])
        rec = sb("rec", [P, 2, A, 2, TT])
        ratio = sb("ratio", [P, 2, 2, TT])
        pr = sb("pr", [P, 2, A, 2, 3 * P])
        dif = sb("dif", [P, 2, 2, 3 * P])
        nm2 = sb("nm2", [P, 2, 2, TT])
        nb2 = sb("nb2", [P, 2, 2, TT])
        p2 = sb("p2", [P, 2, 2, 3 * P])
        pt = sb("pt", [P, 2, 2, 3 * P])
        recs = sb("recs", [P, TT, H])
        on = sb("on", [P, TT, D])
        osq = sb("osq", [P, TT, D])
        vv = sb("vv", [P, TT * H])
        rs = sb("rs", [P, TT * H])
        tmp = sb("tmp", [P, TT * H])
        oT = sb("oT", [P, KD, T])
        lw = ln_scratch(sb, TT)
        S = [psum[:, 0:2, :], psum[:, 2:4, :]]
        PT = [psum[:, 4, :], psum[:, 5, :]]
        KP = [psum[:, 6, :], psum[:, 7, :]]
        O = psum[:, 6:8, 0:H * V1].rearrange("p t (h e) -> p t h e", e=V1)

        x_staged = sem("x_staged")
        xc_free = sem("xc_free")
        rot_steps = sem("rot_steps")
        proj_ps = sem("proj_ps")
        rot_ready = sem("rot_ready")
        lam_ready = sem("lam_ready")
        s_ps = sem("s_ps")
        nm_ready = sem("nm_ready")
        p_exp = sem("p_exp")
        nb_ready = sem("nb_ready")
        p_ready = sem("p_ready")
        pt_ps = sem("pt_ps")
        pt_ready = sem("pt_ready")
        av_ps = sem("av_ps")
        o_free = sem("o_free")
        on_ready = sem("on_ready")
        oT_ps = sem("oT_ps")
        oT_ready = sem("oT_ready")
        y_ps = sem("y_ps")
        z_ready = sem("z_ready")
        set_up = sem("set_up")
        steps = sem("steps")

        with nc.Block() as block:
            @block.sync
            def _(sp):
                with sp.Fori(0, B) as b:
                    sp.wait_ge(xc_free, b + 1)
                    sp.dma_start(xc[:, :, :], xT[:, :, bass.ds(b * T, T)]).then_inc(x_staged, 16)

            @block.tensor
            def _(pe):
                mm = nc.tensor.matmul
                pe.sem_inc(xc_free, 1)

                def project(b):
                    pe.wait_ge(x_staged, b * 16 + 16)
                    for a in range(A):
                        for r in range(R):
                            for k in range(KD):
                                last = mm(S[a][:, r // 2, (r % 2) * T:(r % 2 + 1) * T],
                                          w["q"][:, k, (a * R + r) * P:(a * R + r + 1) * P], xc[:, k, :],
                                          start=(k == 0), stop=(k == KD - 1))
                        last.then_inc(proj_ps, 1)
                    for a in range(A):
                        for j in range(2):
                            for k in range(KD):
                                mm(KP[a][:, j * T:(j + 1) * T], w["k"][:, k, (2 * a + j) * P:(2 * a + j + 1) * P], xc[:, k, :],
                                   start=(k == 0), stop=(k == KD - 1))
                    for t in range(TT):
                        for k in range(KD):
                            last = mm(PT[1][:, t * G * HD:(t + 1) * G * HD], xc[:, k, t * P:(t + 1) * P],
                                      w["v"][:, k, :], start=(k == 0), stop=(k == KD - 1))
                    last.then_inc(proj_ps, 1)
                    pe.wait_ge(proj_ps, b * 3 + 3)
                    pe.sem_inc(xc_free, 1)

                def attend(b):
                    def scores(n):
                        if n < 2:
                            pe.wait_ge(rot_ready, b * 3 + 3)
                        else:
                            pe.wait_ge(p_exp, b * H + n - 1)
                        r, g = n // G, n % G
                        for a in range(A):
                            for t in range(TT):
                                mm(S[n % 2][:, a, t * P:t * P + (t + 1) * P], qr[:, a, r, t * P:(t + 1) * P],
                                   kr[:, g, a, 0:(t + 1) * P], start=True, stop=False)
                                last = mm(S[n % 2][:, a, 2 * t * P:(2 * t + 1) * P], c["idb"], c["maskb"], start=False, stop=True)
                        last.then_inc(s_ps, 1)

                    def turn(m):
                        pe.wait_ge(p_ready, b * NG + m + 1)
                        for j in range(2):
                            if m >= 1:
                                pe.wait_ge(pt_ready, b * H + 2 * (m - 1) + j + 1)
                            for i in range(3):
                                last = nc.tensor.transpose(PT[j][:, i * P:(i + 1) * P], p2[:, m % 2, j, i * P:(i + 1) * P], c["id"])
                            last.then_inc(pt_ps, 1)

                    def values(m):
                        for j in range(2):
                            n = 2 * m + j
                            pe.wait_ge(pt_ready, b * H + n + 1)
                            r, g = n // G, n % G
                            h = 4 * g + r
                            pp = pt[:, m % 2, j, :]
                            mm(O[:, 0, h, :], pp[:, 0:P], va[:, 0, g, :], start=True, stop=True)
                            mm(O[:, 1, h, :], pp[:, P:2 * P], va[:, 0, g, :], start=True, stop=False)
                            last = mm(O[:, 1, h, :], pp[:, 2 * P:3 * P], va[:, 1, g, :], start=False, stop=True)
                        last.then_inc(av_ps, 1)

                    for m in range(NG + 3):
                        if m < NG:
                            scores(2 * m)
                            scores(2 * m + 1)
                        if 2 <= m < NG + 2:
                            turn(m - 2)
                        if m >= 3:
                            values(m - 3)

                def output(b):
                    for h in range(KD):
                        for t in range(TT):
                            last = nc.tensor.transpose(PT[0][:, (h * TT + t) * P:(h * TT + t + 1) * P],
                                                       on[:, t, h * P:(h + 1) * P], c["id"])
                    last.then_inc(oT_ps, 1)
                    pe.wait_ge(oT_ready, b + 1)
                    for t in range(TT):
                        for k in range(KD):
                            last = mm(PT[1][:, t * D:(t + 1) * D], oT[:, k, t * P:(t + 1) * P], w["o"][:, k, :],
                                      start=(k == 0), stop=(k == KD - 1))
                    last.then_inc(y_ps, 1)

                w["early"](pe)
                project(0)
                w["late"](pe)
                with pe.Fori(0, B - 1) as b:
                    attend(b)
                    pe.wait_ge(o_free, b + 1)
                    project(b + 1)
                    pe.wait_ge(on_ready, b + 1)
                    pe.wait_ge(rot_ready, b * 3 + 6)
                    output(b)
                    pe.wait_ge(z_ready, b + 1)
                attend(B - 1)
                pe.wait_ge(on_ready, B)
                output(B - 1)

            @block.scalar
            def _(act):
                nc.scalar.preload_act_table(ACT.Exp)
                act.wait_ge(set_up, 2)
                nc.scalar.activation(lam[:, :, :], lam[:, :, :], ACT.Exp).then_inc(lam_ready, 1)
                with act.Fori(0, B) as b:
                    def first(n):
                        m, j = n // 2, n % 2
                        act.wait_ge(nm_ready, b * H + n + 1)
                        if m >= 2:
                            act.wait_ge(nb_ready, b * NG + m - 1)
                        for a in range(A):
                            for t in range(TT):
                                s = slice(t * P, t * P + (t + 1) * P)
                                last = nc.scalar.activation(pr[:, m % 2, a, j, s], S[j][:, a, s], ACT.Exp, bias=nm[:, j, t, a:a + 1],
                                                            accum_out=sums[:, m % 2, a, j, t:t + 1])
                        last.then_inc(p_exp, 1)

                    def second(m):
                        act.wait_ge(nb_ready, b * NG + m + 1)
                        if m >= 2:
                            act.wait_ge(pt_ps, b * H + 2 * (m - 1))
                        for j in range(2):
                            for t in range(TT):
                                s = slice(t * P, t * P + (t + 1) * P)
                                last = nc.scalar.activation(p2[:, m % 2, j, s], dif[:, m % 2, j, s], ACT.Exp, bias=nb2[:, m % 2, j, t:t + 1],
                                                            scale=rec[:, m % 2, 0, j, t:t + 1])
                        last.then_inc(p_ready, 1)

                    def out_of_psum(m):
                        for j in range(2):
                            act.wait_ge(pt_ps, b * H + 2 * m + j + 1)
                            if m >= 2:
                                act.wait_ge(av_ps, b * NG + m - 1)
                            nc.scalar.activation(pt[:, m % 2, j, :], PT[j][:, 0:3 * P], ACT.Copy).then_inc(pt_ready, 1)

                    for m in range(NG + 2):
                        if m < NG:
                            first(2 * m)
                            first(2 * m + 1)
                        if 1 <= m <= NG:
                            second(m - 1)
                        if m >= 2:
                            out_of_psum(m - 2)
                    act.wait_ge(oT_ps, b + 1)
                    nc.scalar.activation(oT[:, :, :], PT[0].rearrange("p (k t) -> p k t", k=KD), ACT.Copy).then_inc(oT_ready, 1)

            @block.vector
            def _(dve):
                st = Steps(dve, steps, L3A_STEPS)
                w["early"](dve)
                w["late"](dve)
                for j in range(2):
                    last = nc.vector.tensor_tensor(lprod[:, j, :, :], w["lq%d" % (j + 1)], w["lk%d" % (j + 1)], ALU.mult)
                last.then_inc(set_up, 1)
                dve.wait_ge(set_up, 1)
                nc.vector.tensor_reduce(lam[:, :, :], lprod[:, :, :, :], AX.X, ALU.add).then_inc(set_up, 1)
                dve.wait_ge(lam_ready, 1)
                nc.vector.tensor_tensor(nlam[:, :], lam[:, 1, :], lam[:, 0, :], ALU.subtract).then_inc(set_up, 1)
                dve.wait_ge(set_up, 3)
                nc.vector.tensor_scalar(nlam[:, :], nlam[:, :], -LAM_INIT, None, ALU.add).then_inc(set_up, 1)
                nc.vector.tensor_scalar(gain[:, :], w["rms"], 1.0 - LAM_INIT, None, ALU.mult).then_inc(set_up, 1)
                nc.vector.memset(va[:, :, :, HD:V1], 1.0)
                nc.vector.memset(kr[:, :, :, :], 0.0).then_inc(rot_steps, 1)
                dve.wait_ge(set_up, 5)

                def rotate(b):
                    for a in range(A):
                        dve.wait_ge(proj_ps, b * 3 + a + 1)
                        for j in range(2):
                            last = nc.vector.tensor_tensor(qr[:, a, 2 * j:2 * j + 2, :], S[a][:, j, :].rearrange("p (r t) -> p r t", r=2),
                                                           bc(c["l3_q"][:, a, :], 1, 2), ALU.mult)
                        last.then_inc(rot_ready, 1)
                    dve.wait_ge(proj_ps, b * 3 + 3)
                    for a in range(A):
                        last = nc.vector.tensor_tensor(k1[:, a, :, :], KP[a].rearrange("p (j t) -> p j t", j=2), c["l3_k"][:, a, :, :], ALU.mult)
                    last.then_inc(rot_steps, 1)
                    dve.wait_ge(rot_steps, b + 2)
                    for g in range(G):
                        rows = slice(32 * g, 32 * g + 32)
                        nc.vector.tensor_tensor(kr[rows, g, :, :], k1[rows, :, 0, :], k1[rows, :, 1, :], ALU.add)
                    nc.vector.tensor_copy(va[:, :, :, 0:HD],
                                          PT[1][:, 0:TT * G * HD].rearrange("p (t g e) -> p t g e", t=TT, g=G)).then_inc(rot_ready, 1)

                def attend(b):
                    def maxima(n):
                        dve.wait_ge(s_ps, b * H + n + 1)
                        if n >= 2:
                            dve.wait_ge(p_exp, b * H + n - 1)
                        for t in range(TT):
                            last = nc.vector.tensor_reduce(nm[:, n % 2, t, :], S[n % 2][:, :, t * P:t * P + (t + 1) * P],
                                                           AX.X, ALU.max, negate=True)
                        last.then_inc(nm_ready, 1)

                    def difference(m):
                        i = m % 2
                        dve.wait_ge(p_exp, b * H + 2 * m + 2)
                        if m >= 2:
                            dve.wait_ge(p_ready, b * NG + m - 1)
                        st.do(nc.vector.reciprocal(rec[:, i, :, :, :], sums[:, i, :, :, :]))
                        for j in range(2):
                            n = 2 * m + j
                            h = 4 * (n % G) + n // G
                            last = nc.vector.scalar_tensor_tensor(ratio[:, i, j, :], sums[:, i, 0, j, :], nlam[:, h:h + 1], rec[:, i, 1, j, :], ALU.mult, ALU.mult)
                        st.do(last)
                        for j in range(2):
                            for t in range(TT):
                                s = slice(t * P, t * P + (t + 1) * P)
                                last = nc.vector.scalar_tensor_tensor(dif[:, i, j, s], pr[:, i, 1, j, s], ratio[:, i, j, t:t + 1], pr[:, i, 0, j, s], ALU.mult, ALU.add)
                        st.do(last)
                        diagonal = dif[:, i, :, :].rearrange("p j (c k) -> p j c k", c=3)[:, :, 0:3:2, :]
                        st.do(nc.vector.tensor_tensor(diagonal, diagonal, bc(bc(c["mask"], 1, 2), 1, 2), ALU.add))
                        for t in range(TT):
                            last = nc.vector.tensor_reduce(nm2[:, i, :, t], dif[:, i, :, t * P:t * P + (t + 1) * P], AX.X, ALU.max, negate=True)
                        st.do(last)
                        nc.vector.tensor_tensor(nb2[:, i, :, :], nm2[:, i, :, :], rec[:, i, 0, :, :], ALU.mult).then_inc(nb_ready, 1)

                    for m in range(NG + 1):
                        if m < NG:
                            maxima(2 * m)
                            maxima(2 * m + 1)
                        if m >= 1:
                            difference(m - 1)
                    dve.wait_ge(av_ps, b * NG + NG)
                    st.do(nc.vector.reciprocal(recs[:, :, :], O[:, :, :, HD]))
                    heads = lambda ap: ap.rearrange("p (h e) -> p h e", e=HD)
                    for t in range(TT):
                        last = nc.vector.tensor_tensor(heads(on[:, t, :]), O[:, t, :, 0:HD], bc(recs[:, t, :], 2, HD), ALU.mult)
                    last.then_inc(o_free, 1)
                    dve.wait_ge(o_free, b + 1)

                def norm(b):
                    st.do(nc.vector.tensor_tensor(osq[:, :, :], on[:, :, :], on[:, :, :], ALU.mult))
                    flat = lambda ap: ap.rearrange("p t (h e) -> p (t h) e", e=HD)
                    st.do(nc.vector.tensor_reduce(vv[:, :], flat(osq[:, :, :]), AX.X, ALU.add))
                    st.do(nc.vector.tensor_scalar(vv[:, :], vv[:, :], 1.0 / HD, EPS, ALU.mult, ALU.add))
                    newton_rsqrt(nc, st, vv[:, :], rs[:, :], tmp[:, :])
                    st.wait()
                    st.do(nc.vector.tensor_tensor(flat(on[:, :, :]), flat(on[:, :, :]), bc(rs[:, :], 2, HD), ALU.mult))
                    nc.vector.tensor_tensor(flat(on[:, :, :]), flat(on[:, :, :]), bc(gain[:, :], 1, TT * H), ALU.mult).then_inc(on_ready, 1)

                def output(b):
                    dve.wait_ge(y_ps, b + 1)
                    add_and_measure(nc, st, x_sb, mv, b * TT, TT, PT[1].rearrange("p (t n) -> p t n", t=TT), lw, z_ready)
                    st.end()

                rotate(0)
                with dve.Fori(0, B - 1) as b:
                    st.begin(b)
                    attend(b)
                    norm(b)
                    rotate(b + 1)
                    output(b)
                st.begin(B - 1)
                attend(B - 1)
                norm(B - 1)
                output(B - 1)


L3A_STEPS = 5 * 8 + 5 + NEWTON_STEPS + LN_STEPS



def l3_ffn(nc, c, x_sb, mv, xT, w, psum):
    E, I, TOP = 32, 96, 4
    NH = E * I // P
    with ExitStack() as ctx:
        sb = lambda name, shape, dt=F32: ctx.enter_context(nc.sbuf_tensor("l3f_" + name, shape, dt))
        sem = lambda name: ctx.enter_context(nc.semaphore("l3f_" + name))
        pb = sb("pb", [P, NT, E + 8 - TOP])
        nm = sb("nm", [P, NT])
        sums = sb("sums", [P, NT])
        top = sb("top", [P, NT, 8])
        pick = sb("pick", [P, NT, 8])
        left = sb("left", [P, NT, E + 8 - TOP])
        wsum = sb("wsum", [P, NT])
        cw = sb("cw", [P, NT, E])
        rest = sb("rest", [P, NT, E])
        c3 = sb("c3", [P, NT, 3, E], BF16)
        c3T = sb("c3T", [3 * E, TOK], BF16)
        sg = sb("sg", [P, 2, CN])
        gu = sb("gu", [P, 2, CN])
        hw = sb("hw", [P, 2, CN])
        zero = sb("zero", [P, P], BF16)
        lw = ln_scratch(sb, CH)
        bank = lambda i: psum[:, i, :]
        GB, UB, CB = [bank(0), bank(1)], [bank(2), bank(3)], [bank(4), bank(5)]
        Y = psum[:, 6:8, :].rearrange("p a (t n) -> p (a t) n", t=2)
        LOGITS = bank(0).rearrange("p (t e) -> p t e", t=NT)

        logit_ps = sem("logit_ps")
        nm_ready = sem("nm_ready")
        ex_ready = sem("ex_ready")
        c3_ready = sem("c3_ready")
        c3T_ps = sem("c3T_ps")
        c3T_ready = sem("c3T_ready")
        h_ps = sem("h_ps")
        sg_ready = sem("sg_ready")
        gu_ready = sem("gu_ready")
        hw_ready = sem("hw_ready")
        used = sem("used")
        z_ready = sem("z_ready")
        steps = sem("steps")
        zero_ready = sem("zero_ready")
        route_steps = sem("route_steps")

        with nc.Block() as block:
            @block.tensor
            def _(pe):
                mm = nc.tensor.matmul
                pe.wait_ge(zero_ready, 1)

                def clear_output():
                    for a in (6, 7):
                        mm(bank(a), zero[:, :], c["finite"], start=True, stop=False)

                w["early"](pe)
                for t in range(NT):
                    for k in range(KD):
                        last = mm(LOGITS[:, t, :], xT[:, k, t * P:(t + 1) * P], w["router"][:, k, :], start=(k == 0), stop=(k == KD - 1))
                last.then_inc(logit_ps, 1)
                pe.wait_ge(c3_ready, 1)
                for t in range(NT):
                    last = nc.tensor.transpose(psum[0:3 * E, 2 + t // 8, (t % 8) * P // 2:(t % 8 + 1) * P // 2].bitcast(BF16),
                                               c3[:, t, :, :].rearrange("p a e -> p (a e)"), c["idb"])
                last.then_inc(c3T_ps, 1)
                pe.wait_ge(c3T_ready, 1)
                w["late"](pe)
                with pe.Fori(0, NCH) as b:
                    chunk = bass.ds(b * CN, CN)

                    def hidden(e):
                        if e >= 2:
                            pe.wait_ge(gu_ready, b * NH + e - 1)
                            pe.wait_ge(hw_ready, b * NH + e - 1)
                        for name, bk in (("gate", GB), ("up", UB)):
                            for k in range(KD):
                                mm(bk[e % 2], w[name][:, k, e * P:(e + 1) * P], xT[:, k, chunk], start=(k == 0), stop=(k == KD - 1))
                        mm(CB[e % 2], c["sel3"][:, e * P:(e + 1) * P], c3T[:, chunk], start=True, stop=True).then_inc(h_ps, 1)

                    def down(e):
                        pe.wait_ge(hw_ready, b * NH + e + 1)
                        if e == 0:
                            pe.wait_ge(z_ready, b + 1)
                            clear_output()
                        for t in range(CH):
                            last = mm(Y[:, t, :], hw[:, e % 2, t * P:(t + 1) * P], w["down"][:, e, :], start=False,
                                      stop=(e == NH - 1 and t % 2 == 1))
                        last.then_inc(used, 1)

                    for e in range(NH + 1):
                        if e < NH:
                            hidden(e)
                        if e >= 1:
                            down(e - 1)

            @block.scalar
            def _(act):
                act.wait_ge(nm_ready, 1)
                for t in range(NT):
                    last = nc.scalar.activation(pb[:, t, 0:E], LOGITS[:, t, :], ACT.Exp, bias=nm[:, t:t + 1], accum_out=sums[:, t:t + 1])
                last.then_inc(ex_ready, 1)
                nc.scalar.preload_act_table(ACT.Silu)
                with act.Fori(0, NCH) as b:
                    for e in range(NH):
                        act.wait_ge(h_ps, b * NH + e + 1)
                        if e >= 2:
                            act.wait_ge(gu_ready, b * NH + e - 1)
                        nc.scalar.activation(sg[:, e % 2, :], GB[e % 2], ACT.Silu).then_inc(sg_ready, 1)

            @block.vector
            def _(dve):
                nc.vector.memset(zero[:, :], 0.0).then_inc(zero_ready, 1)
                nc.vector.memset(pb[:, :, E:], BIG)
                nc.vector.memset(pick[:, :, :], BIG)
                st = Steps(dve, route_steps, 0)
                st.begin(0)
                dve.wait_ge(logit_ps, 1)
                nc.vector.tensor_reduce(nm[:, :], LOGITS, AX.X, ALU.max, negate=True).then_inc(nm_ready, 1)
                dve.wait_ge(ex_ready, 1)
                st.do(nc.vector.reciprocal(wsum[:, :], sums[:, :]))
                st.do(nc.vector.tensor_tensor(pb[:, :, 0:E], pb[:, :, 0:E], bc(wsum[:, :], 2, E), ALU.mult))
                for t in range(NT):
                    last = nc.vector.max(top[:, t, :], pb[:, t, 0:E])
                st.do(last)
                st.do(nc.vector.tensor_copy(pick[:, :, 0:TOP], top[:, :, 0:TOP]))
                for t in range(NT):
                    last = nc.vector.match_replace(left[:, t, :], pick[:, t, :], pb[:, t, :], -BIG)
                st.do(last)
                st.do(nc.vector.scalar_tensor_tensor(cw[:, :, :], left[:, :, 0:E], -BIG, pb[:, :, 0:E], ALU.is_equal, ALU.mult))
                st.do(nc.vector.tensor_reduce(wsum[:, :], cw[:, :, :], AX.X, ALU.add))
                st.do(nc.vector.reciprocal(wsum[:, :], wsum[:, :]))
                st.do(nc.vector.tensor_tensor(cw[:, :, :], cw[:, :, :], bc(wsum[:, :], 2, E), ALU.mult))
                split3(nc, st, cw[:, :, :], [c3[:, :, j, :] for j in range(3)], rest[:, :, :])
                nc.vector.memset(lw["carrier"][:, :], 0.0).then_inc(c3_ready, 1)
                dve.wait_ge(c3T_ps, 1)
                nc.vector.tensor_copy(c3T[:, :].rearrange("p (a n) -> p a n", a=2), psum[0:3 * E, 2:4, :].bitcast(BF16)).then_inc(c3T_ready, 1)
                dve.sem_inc(z_ready, 1)
                st = Steps(dve, steps, LN_STEPS)
                with dve.Fori(0, NCH) as b:
                    st.begin(b)

                    def weigh(e):
                        dve.wait_ge(gu_ready, b * NH + e + 1)
                        if e >= 2:
                            dve.wait_ge(used, b * NH + e - 1)
                        nc.vector.tensor_tensor(hw[:, e % 2, :], gu[:, e % 2, :], CB[e % 2], ALU.mult).then_inc(hw_ready, 1)

                    for e in range(NH):
                        dve.wait_ge(sg_ready, b * NH + e + 1)
                        nc.vector.tensor_tensor(gu[:, e % 2, :], sg[:, e % 2, :], UB[e % 2], ALU.mult).then_inc(gu_ready, 1)
                        weigh(e)
                    dve.wait_ge(used, b * NH + NH)
                    add_and_measure(nc, st, x_sb, mv, b * CH, CH, Y, lw, z_ready, b + 2)
                    st.end()



LAST_STAGE = 8
W_COLS = {
    "l0a_q": KD * 512, "l0a_k": KD * 256, "l0a_v": KD * 64, "l0a_o": KD * D,
    "l0f_w1": 32 * 128, "l0f_w2": 32 * 128, "l0f_fc1": KD * 128, "l0f_fc2": D, "l0f_gate": KD * 32, "l0f_up": KD * 512,
    "l0f_down": 4 * D, "l0f_bias": 32,
    "l1a_q": KD * 2048, "l1a_k": KD * 2048, "l1a_v": KD * 2048, "l1a_o": 16 * D, "l1a_gq": 1, "l1a_gk": 1,
    "l1f_router": KD * 128, "l1f_gate": KD * 1024, "l1f_up": KD * 1024, "l1f_down": D, "l1f_amp": 16, "l1f_escale": 1,
    "l1f_sgate": KD * 256, "l1f_sup": KD * 256, "l1f_sdown": 2 * D,
    "l2a_u": KD * 256, "l2a_v": KD * 256, "l2a_g1": KD * 64, "l2a_g2": 256, "l2a_bu": 2, "l2a_bv": 2,
    "l2a_bg1": 1, "l2a_bg2": 2, "l2a_conv": KD * 3, "l2a_convb": KD,
    "l2f_gate": KD * 1024, "l2f_up": KD * 1024, "l2f_down": 8 * D,
    "l3a_q": KD * 1024, "l3a_k": KD * 512, "l3a_v": KD * 64, "l3a_o": KD * D, "l3a_lq1": 256, "l3a_lq2": 256, "l3a_lk1": 256,
    "l3a_lk2": 256, "l3a_rms": 16,
    "l3f_router": KD * 32, "l3f_gate": KD * 3072, "l3f_up": KD * 3072, "l3f_down": 24 * D,
}
W_CUT = {"l0a_q": KD, "l0a_k": KD, "l0a_v": KD, "l0a_o": KD, "l0f_w1": 32, "l0f_w2": 32, "l0f_fc1": KD, "l0f_gate": KD,
         "l0f_up": KD, "l1a_q": KD, "l1a_k": KD, "l1a_v": KD, "l1a_o": 16,
         "l1f_router": KD, "l1f_gate": KD, "l1f_up": KD, "l1f_amp": 8, "l1f_sgate": KD, "l1f_sup": KD, "l1f_sdown": 2,
         "l2a_u": KD, "l2a_v": KD, "l2a_g1": KD, "l2a_conv": KD, "l2f_gate": KD, "l2f_up": KD, "l2f_down": 8,
         "l3a_q": KD, "l3a_k": KD, "l3a_v": KD, "l3a_o": KD, "l3a_lq1": 16, "l3a_lq2": 16, "l3a_lk1": 16, "l3a_lk2": 16,
         "l3f_router": KD, "l3f_gate": KD, "l3f_up": KD, "l3f_down": 24, "l0f_down": 4}
C_COLS = {"id": P, "l0_q": T, "l0_k": 2 * T, "one": 1, "l3_q": 2 * T, "l3_k": 4 * T, "mask": P}
CB_COLS = {"idb": P, "maskb": P, "sel0": 32 * P, "sel3": 24 * P}


EARLY = ("l0a_q", "l0a_k", "l0a_v", "l0f_gate", "l0f_bias", "l1a_k", "l1a_gq", "l1a_gk", "l1f_router", "l1f_amp", "l1f_escale",
         "l2a_g1", "l2a_u", "l2a_v", "l2a_conv", "l2a_convb", "l2f_gate", "l2f_up", "l3a_q", "l3a_k", "l3a_v", "l3f_router")
STAGES = [("l0a", l0_attention), ("l0f", l0_ffn), ("l1a", l1_attention), ("l1f", l1_ffn), ("l2a", l2_mixing), ("l2f", l2_ffn),
          ("l3a", l3_attention), ("l3f", l3_ffn)]


def network(nc, x_in, cf, cb, wts, out):
    with ExitStack() as ctx:
        x_sb = ctx.enter_context(nc.sbuf_tensor("x_sb", [P, NT, D], F32))
        cf_sb = ctx.enter_context(nc.sbuf_tensor("cf_sb", [P, sum(C_COLS.values())], F32))
        cb_sb = ctx.enter_context(nc.sbuf_tensor("cb_sb", [P, sum(CB_COLS.values())], mybir.dt.uint16))
        psum = ctx.enter_context(nc.psum_tensor("psum", [P, 8, 512], F32))
        mv = ctx.enter_context(nc.sbuf_tensor("mv", [P, NT, 2], F32))
        xT = ctx.enter_context(nc.sbuf_tensor("xT", [P, KD, TOK], F32))
        tables_in = ctx.enter_context(nc.semaphore("tables_in"))
        early = ctx.enter_context(nc.semaphore("early"))
        late = ctx.enter_context(nc.semaphore("late"))
        shared = {n: ctx.enter_context(nc.semaphore("boundary_" + n)) for n in ("normal", "turned", "copied", "steps", "stored")}
        c, at = {}, 0
        for name, n in C_COLS.items():
            c[name] = cf_sb[:, at:at + n]
            at += n
        at = 0
        for name, n in CB_COLS.items():
            c[name] = cb_sb[:, at:at + n].bitcast(BF16)
            at += n
        c["finite"] = c["sel0"][:, 0:512]
        c["l0_k"] = c["l0_k"].rearrange("p (j t) -> p j t", j=2)
        x_rows = x_in.rearrange("b (t p) d -> p (b t) d", p=P)
        o_rows = out.rearrange("b (t p) d -> p (b t) d", p=P)

        c["l3_q"] = c["l3_q"].rearrange("p (a t) -> p a t", a=2)
        c["l3_k"] = c["l3_k"].rearrange("p (a j t) -> p a j t", a=2, j=2)
        c["sel0"], c["sel3"] = c["sel0"][0:96, :], c["sel3"][0:96, :]

        def weights(scope, stage):
            raw = {n: scope.enter_context(nc.sbuf_tensor("w_" + n, [P, k], F32)) for n, k in W_COLS.items() if n.startswith(stage)}
            view = {n[4:]: t[:, :].rearrange("p (k n) -> p k n", k=W_CUT[n]) if n in W_CUT else t[:, :] for n, t in raw.items()}
            return raw, view

        def load_now(sp, pairs, sem):
            for dst, src in pairs:
                sp.dma_start(dst, src).then_inc(sem, 16)
            sp.wait_ge(sem, 16 * len(pairs))

        with nc.Block() as block:
            @block.sync
            def _(sp):
                load_now(sp, [(x_sb[:, :, :], x_rows), (cf_sb[:, :], cf), (cb_sb[:, :], cb)], tables_in)
        n_early = n_late = 0
        for s, (stage, run) in enumerate(STAGES[:LAST_STAGE]):
            with ExitStack() as scope:
                raw, view = weights(scope, stage)
                first = [n for n in raw if n in EARLY]
                rest = [n for n in raw if n not in EARLY]
                n_early, n_late = n_early + len(first), n_late + len(rest)

                def issue(sp, raw=raw, first=first, rest=rest):
                    for names, sem in ((first, early), (rest, late)):
                        for n in names:
                            sp.dma_start(raw[n][:, :], wts[n]).then_inc(sem, 16)

                boundary(nc, c, x_sb, mv, xT, psum, shared, s, "to_" + stage, issue, normalise=(s > 0))
                view["early"] = lambda eng, n=n_early: eng.wait_ge(early, 16 * n)
                view["late"] = lambda eng, n=n_late: eng.wait_ge(late, 16 * n)
                run(nc, c, x_sb, mv, xT, view, psum)
        boundary(nc, c, x_sb, mv, xT, psum, shared, LAST_STAGE, "end", lambda sp: None, transpose=False, out_rows=o_rows)



def k_major(w):
    k, n = w.shape
    return np.ascontiguousarray(w.reshape(k // P, P, n).transpose(1, 0, 2).reshape(P, -1))


def l0_columns():
    q = [16 * (4 * g + r) + (j if j < 16 else (j - 16 + 8) % 16) for r in range(4) for g in range(4) for j in range(32)]
    k = [16 * g + (j + 8 * s) % 16 for s in range(2) for g in range(4) for j in range(32)]
    return np.array(q), np.array(k)


def rope_l0():
    f = (1.0 / 10000.0 ** (np.arange(0, 16, 2, dtype=np.float32) / np.float32(16))).astype(np.float32)
    ang = (np.arange(T, dtype=np.float32)[:, None] * f[None, :]).astype(np.float32)
    cos, sin = np.cos(ang).astype(np.float32), np.sin(ang).astype(np.float32)
    j = np.arange(P) % 16
    cp, sp = cos[:, j % 8].T, sin[:, j % 8].T * np.where(j < 8, -1, 1)[:, None].astype(np.float32)
    first = (np.arange(P) % 32 < 16)[:, None]
    return (np.where(first, cp, sp) * np.float32(0.25)).astype(np.float32), np.concatenate([cp, sp], 1).astype(np.float32)


def l3_columns():
    q = [32 * (4 * g + r) + ((16 * a + j) if j < 16 else (16 * a + j - 16) ^ 1)
         for a in range(2) for r in range(4) for g in range(4) for j in range(32)]
    k = [32 * g + ((16 * a + j % 16) ^ s) for a in range(2) for s in range(2) for g in range(4) for j in range(32)]
    return np.array(q), np.array(k)


def rope_l3():
    f = (1.0 / 10000.0 ** (np.arange(0, 32, 2, dtype=np.float32) / np.float32(32))).astype(np.float32)
    ang = (np.arange(T, dtype=np.float32)[:, None] * f[None, :]).astype(np.float32)
    cos, sin = np.cos(ang).astype(np.float32), np.sin(ang).astype(np.float32)
    qs, ks = [], []
    for a in range(2):
        dd = 16 * a + np.arange(P) % 16
        cp, sp = cos[:, dd // 2].T, sin[:, dd // 2].T * np.where(dd % 2 == 0, -1, 1)[:, None].astype(np.float32)
        qs.append(np.where((np.arange(P) % 32 < 16)[:, None], cp, sp) * np.float32(0.25))
        ks += [cp, sp]
    return np.concatenate(qs, 1).astype(np.float32), np.concatenate(ks, 1).astype(np.float32)


def tables():
    q0, k0 = rope_l0()
    q3, k3 = rope_l3()
    mask = np.where(np.arange(P)[None, :] > np.arange(P)[:, None], np.float32(NEG), np.float32(0))
    cf = np.concatenate([np.eye(P, dtype=np.float32), q0, k0, np.ones((P, 1), np.float32), q3, k3, mask], 1)
    part = np.arange(P)[:, None]
    sel0 = (part % 32 == np.arange(32 * P)[None, :] // P).astype(np.float32)
    sel3 = (part % 32 == np.arange(24 * P)[None, :] // 96).astype(np.float32)
    cb = np.concatenate([np.eye(P, dtype=np.float32), mask, sel0, sel3], 1)
    cb = (cb.view(np.uint32) >> 16).astype(np.uint16)
    return np.ascontiguousarray(cf), np.ascontiguousarray(cb)


def layouts(i):
    q0, k0 = l0_columns()
    w = {
        "l0a_q": k_major(i["L0_attn_wq"][:, q0]), "l0a_k": k_major(i["L0_attn_wk"][:, k0]),
        "l0a_v": k_major(i["L0_attn_wv"]), "l0a_o": k_major(i["L0_attn_wo"]),
    }
    w |= {
        "l0f_w1": i["L0_ffn_w1"].transpose(2, 0, 1).reshape(P, -1), "l0f_w2": i["L0_ffn_w2"].transpose(2, 0, 1).reshape(P, -1),
        "l0f_fc1": k_major(i["L0_ffn_fc1_w"].T), "l0f_fc2": i["L0_ffn_fc2_w"].T, "l0f_gate": k_major(i["L0_ffn_gate_w"].T),
        "l0f_up": k_major(i["L0_ffn_shared_up_w"].T), "l0f_down": k_major(i["L0_ffn_shared_down_w"].T),
        "l0f_bias": np.broadcast_to(i["L0_ffn_gate_bias"], (P, 32)),
    }
    w |= {
        "l1a_q": k_major(i["L1_attn_Wq"].T), "l1a_k": k_major(i["L1_attn_Wk"].T), "l1a_v": k_major(i["L1_attn_Wv"].T),
        "l1a_o": k_major(i["L1_attn_Wo"].T), "l1a_gq": i["L1_attn_gq"][:, None], "l1a_gk": i["L1_attn_gk"][:, None],
    }
    w |= {
        "l1f_router": k_major(i["L1_ffn_w_router"]), "l1f_gate": k_major(i["L1_ffn_w_gate"]), "l1f_up": k_major(i["L1_ffn_w_up"]),
        "l1f_down": i["L1_ffn_w_down"], "l1f_amp": i["L1_ffn_amplitudes"].reshape(P, -1), "l1f_escale": i["L1_ffn_expert_scale"][:, None],
        "l1f_sgate": k_major(i["L1_ffn_shared_w_gate"]), "l1f_sup": k_major(i["L1_ffn_shared_w_up"]),
        "l1f_sdown": k_major(i["L1_ffn_shared_w_down"]),
    }
    halves = lambda v: v.reshape(2, P).T
    down = lambda a: np.pad(a, ((0, P - a.shape[0]), (0, 0)))
    w |= {
        "l2a_u": k_major(i["L2_attn_Wu"].T), "l2a_v": k_major(i["L2_attn_Wv"].T), "l2a_g1": k_major(i["L2_attn_Wg1"].T),
        "l2a_g2": down(i["L2_attn_Wg2"].T), "l2a_bu": halves(i["L2_attn_bu"]),
        "l2a_bv": halves(i["L2_attn_bv"]), "l2a_bg1": down(i["L2_attn_bg1"][:, None]), "l2a_bg2": halves(i["L2_attn_bg2"]),
        "l2a_conv": k_major(i["L2_attn_conv_w"][:, 0, :]), "l2a_convb": halves(i["L2_attn_conv_b"]),
    }
    deal = (512 * np.arange(2)[:, None, None] + 4 * np.arange(P)[None, None, :] + np.arange(4)[None, :, None]).reshape(-1)
    w |= {
        "l2f_gate": k_major(i["L2_ffn_w_gate"][:, deal]), "l2f_up": k_major(i["L2_ffn_w_up"][:, deal]),
        "l2f_down": k_major(i["L2_ffn_w_down"][deal, :]),
    }
    q3, k3 = l3_columns()
    every = lambda a: np.broadcast_to(a.reshape(-1), (P, a.size))
    g3 = i["L3_ffn_gate_up_proj"].transpose(1, 0, 2)
    w |= {
        "l3a_q": k_major(i["L3_attn_Wq"][:, q3]), "l3a_k": k_major(i["L3_attn_Wk"][:, k3]), "l3a_v": k_major(i["L3_attn_Wv"]),
        "l3a_o": k_major(i["L3_attn_Wo"]), "l3a_rms": every(i["L3_attn_rms_w"]),
        **{"l3a_" + n: every(i["L3_attn_" + n]) for n in ("lq1", "lq2", "lk1", "lk2")},
        "l3f_router": k_major(i["L3_ffn_gate"]), "l3f_gate": k_major(g3[:, :, 0:96].reshape(D, -1)),
        "l3f_up": k_major(g3[:, :, 96:192].reshape(D, -1)), "l3f_down": k_major(i["L3_ffn_down_proj"].reshape(-1, D)),
    }
    return {n: np.ascontiguousarray(a) for n, a in w.items()}


def kernel(**inputs):
    import concourse.bacc as bacc
    from concourse.bass_utils import run_bass_kernel_spmd

    i = {k: np.asarray(v) for k, v in inputs.items()}
    cf, cb = tables()
    host = {"x": np.ascontiguousarray(i["L0_attn_x"]), "table_f32": cf, "table_bf16": cb, **layouts(i)}
    nc = bacc.Bacc("TRN2", target_bir_lowering=False, num_devices=1)
    arrays, aps = {}, {}
    for name, a in host.items():
        arrays[name + "_dram"] = a
        aps[name] = nc.dram_tensor(name + "_dram", a.shape, mybir.dt.from_np(a.dtype), kind="ExternalInput").ap()
    out = nc.dram_tensor("out_dram", (B, T, D), F32, kind="ExternalOutput").ap()
    network(nc, aps["x"], aps["table_f32"], aps["table_bf16"], aps, out)
    r = run_bass_kernel_spmd(nc, [arrays], core_ids=[0])
    return r.results[0]["out_dram"]
```

```python
import math
from contextlib import ExitStack

import numpy as np

import concourse.bass as bass
from concourse import mybir

P = 128
F32 = mybir.dt.float32
BF16 = mybir.dt.bfloat16
F32R = mybir.dt.float32r
I32 = mybir.dt.int32
ALU = mybir.AluOpType
ACT = mybir.ActivationFunctionType
AX = mybir.AxisListType

B, T, D = 8, 256, 256
TOK = B * T
NT = TOK // P
KD = D // P
TT = T // P
CH = 4
CN = CH * P
NCH = NT // CH
LN_EPS = 1e-5
NEG = -1e30
MAGIC = float(0x5F3759DF)


def bc(ap, axis, n):
    wide = ap.unsqueeze(axis)
    shape = list(wide.shape)
    shape[axis] = n
    return wide.broadcast_to(tuple(shape))


def ln_scratch(sb, n):
    return {"stats": sb("ln_stats", [P, n, 6]), "mv": sb("ln_mv", [P, n, 2]), "carrier": sb("ln_carrier", [P, 1])}


class Steps:

    def __init__(self, eng, sem, per_turn):
        self.eng, self.sem, self.per, self.k, self.turn = eng, sem, per_turn, 0, None

    def begin(self, turn):
        self.turn, self.k = turn, 0

    def inc(self, ins):
        ins.then_inc(self.sem, 1)
        self.k += 1
        return self.k

    def wait(self, k=None):
        self.eng.wait_ge(self.sem, self.turn * self.per + (self.k if k is None else k))

    def do(self, ins):
        self.inc(ins)
        self.wait()

    def pad(self):
        self.eng.sem_inc(self.sem, self.per - self.k)

    def end(self):
        assert self.k == self.per, f"a turn has {self.k} steps, not {self.per}"


def carry(nc, w):
    nc.vector.memset(w["carrier"][:, :], 0.0)


def newton_rsqrt(nc, st, v, y, t, iters=3):
    st.inc(nc.vector.tensor_scalar(y.bitcast(I32), v.bitcast(I32), -0.5, MAGIC, ALU.mult, ALU.add))
    for _ in range(iters):
        st.wait()
        st.inc(nc.vector.tensor_tensor(t, y, y, ALU.mult))
        st.wait()
        st.inc(nc.vector.scalar_tensor_tensor(t, v, -0.5, t, ALU.mult, ALU.mult))
        st.wait()
        st.inc(nc.vector.scalar_tensor_tensor(y, t, 1.5, y, ALU.add, ALU.mult))
NEWTON_STEPS = 10
LN_STEPS = 2


BIG = 3e38
LOW = -2e38


def split3(nc, st, v, parts, rest):
    st.do(nc.vector.tensor_copy(parts[0], v))
    st.do(nc.vector.tensor_tensor(rest, v, parts[0], ALU.subtract))
    st.do(nc.vector.tensor_copy(parts[1], rest))
    st.do(nc.vector.tensor_tensor(rest, rest, parts[1], ALU.subtract))
    st.do(nc.vector.tensor_copy(parts[2], rest))


def add_output(nc, x_sb, tile0, n, y_ps, z_ready):
    nc.vector.tensor_tensor(x_sb[:, bass.ds(tile0, n), :], y_ps, x_sb[:, bass.ds(tile0, n), :], ALU.add).then_inc(z_ready, 1)


def measure(nc, st, x_sb, mv, tile0, n, w):
    carry(nc, w)
    for t in range(n):
        last = nc.vector.bn_stats(w["stats"][:, t, :], x_sb[:, bass.ds(tile0 + t, 1), :].rearrange("p o d -> p (o d)"))
    st.do(last)
    carry(nc, w)
    for t in range(n):
        last = nc.vector.bn_aggr(w["mv"][:, t, :], w["stats"][:, t, :])
    st.do(last)
    nc.vector.tensor_copy(mv[:, bass.ds(tile0, n), :], w["mv"][:, :, :])


def add_and_measure(nc, st, x_sb, mv, tile0, n, y_ps, w, z_ready, z_count=None):
    add_output(nc, x_sb, tile0, n, y_ps, z_ready)
    st.eng.wait_ge(z_ready, st.turn + 1 if z_count is None else z_count)
    measure(nc, st, x_sb, mv, tile0, n, w)


def boundary(nc, c, x_sb, mv, xT, psum, sems, at, name, issue_loads, normalise=True, transpose=True, out_rows=None):
    NG = NT // 2
    done = at * NG
    with ExitStack() as ctx:
        sb = lambda n, shape: ctx.enter_context(nc.sbuf_tensor(name + "_" + n, shape, F32))
        ve, rs, tmp = sb("ve", [P, NT]), sb("rs", [P, NT]), sb("tmp", [P, NT])
        normal, turned, steps, stored = (sems[n] for n in ("normal", "turned", "steps", "stored"))

        with nc.Block() as block:
            @block.sync
            def _(sp):
                issue_loads(sp)
                if out_rows is not None:
                    for g in range(NG):
                        sp.wait_ge(normal, done - NG + g + 1)
                        sp.dma_start(out_rows[:, 2 * g:2 * g + 2, :], x_sb[:, 2 * g:2 * g + 2, :]).then_inc(stored, 16)
                    sp.wait_ge(stored, 16 * (3 + NG))

            if transpose:
                @block.tensor
                def _(pe):
                    for g in range(NG):
                        if normalise:
                            pe.wait_ge(normal, done - NG + g + 1)
                        for k in range(KD):
                            for t in range(2):
                                last = nc.tensor.transpose(psum[:, g, (2 * k + t) * P:(2 * k + t + 1) * P],
                                                           x_sb[:, 2 * g + t, k * P:(k + 1) * P], c["id"])
                        last.then_inc(turned, 1)

                @block.scalar
                def _(act):
                    for g in range(NG):
                        act.wait_ge(turned, done + g + 1)
                        nc.scalar.activation(xT[:, :, g * 2 * P:(g + 1) * 2 * P], psum[:, g, :].rearrange("p (k t) -> p k t", k=KD),
                                             ACT.Copy)

            if normalise:
                @block.vector
                def _(dve):
                    st = Steps(dve, steps, 1 + NEWTON_STEPS)
                    st.begin(at - 1)
                    st.do(nc.vector.tensor_scalar(ve[:, :], mv[:, :, 1], LN_EPS, None, ALU.add))
                    newton_rsqrt(nc, st, ve[:, :], rs[:, :], tmp[:, :])
                    st.wait()
                    for t in range(NT):
                        ins = nc.vector.tensor_scalar(x_sb[:, t, :], x_sb[:, t, :], mv[:, t, 0:1], rs[:, t:t + 1], ALU.subtract, ALU.mult)
                        if t % 2 == 1:
                            ins.then_inc(normal, 1)



def l0_attention(nc, c, x_sb, mv, xT, w, psum):
    HD, G, R = 16, 4, 4
    V1 = HD + 1
    NG = 8
    with ExitStack() as ctx:
        sb = lambda name, shape, dt=F32: ctx.enter_context(nc.sbuf_tensor("l0a_" + name, shape, dt))
        sem = lambda name: ctx.enter_context(nc.semaphore("l0a_" + name))
        xc = sb("xc", [P, KD, T])
        qr = sb("qr", [P, R, T])
        k1 = sb("k1", [P, 2, T])
        kr = sb("kr", [P, G, T])
        va = sb("va", [P, TT, G, V1])
        nm = sb("nm", [P, 2, TT, 2])
        pr = sb("pr", [P, 2, 2, 3 * P])
        pt = sb("pt", [P, 2, 2, 3 * P])
        rec = sb("rec", [P, TT, G * R])
        on = sb("on", [P, TT, D])
        oT = sb("oT", [P, KD, T])
        lw = ln_scratch(sb, TT)
        S = [psum[:, 0:2, :], psum[:, 2:4, :]]
        PT = [psum[:, 4, :], psum[:, 5, :]]
        O = psum[:, 6:8, 0:G * R * V1].rearrange("p t (h e) -> p t h e", e=V1)

        x_staged = sem("x_staged")
        xc_free = sem("xc_free")
        rot_steps = sem("rot_steps")
        proj_ps = sem("proj_ps")
        rot_ready = sem("rot_ready")
        s_ps = sem("s_ps")
        nm_ready = sem("nm_ready")
        p_ready = sem("p_ready")
        pt_ps = sem("pt_ps")
        pt_ready = sem("pt_ready")
        av_ps = sem("av_ps")
        on_ready = sem("on_ready")
        oT_ps = sem("oT_ps")
        oT_ready = sem("oT_ready")
        y_ps = sem("y_ps")
        z_ready = sem("z_ready")
        steps = sem("steps")

        with nc.Block() as block:
            @block.sync
            def _(sp):
                sp.dma_start(xc[:, :, :], xT[:, :, 0:T]).then_inc(x_staged, 16)
                w["prefetch"](sp)
                with sp.Fori(0, B - 1) as b:
                    sp.wait_ge(xc_free, b + 1)
                    sp.dma_start(xc[:, :, :], xT[:, :, bass.ds(b * T + T, T)]).then_inc(x_staged, 16)

            @block.tensor
            def _(pe):
                mm = nc.tensor.matmul

                def project(b):
                    pe.wait_ge(x_staged, b * 16 + 16)
                    for r in range(R):
                        for k in range(KD):
                            last = mm(S[0][:, r // 2, (r % 2) * T:(r % 2 + 1) * T], w["q"][:, k, r * P:(r + 1) * P],
                                      xc[:, k, :], start=(k == 0), stop=(k == KD - 1))
                    last.then_inc(proj_ps, 1)
                    for j in range(2):
                        for k in range(KD):
                            last = mm(S[1][:, 0, j * T:(j + 1) * T], w["k"][:, k, j * P:(j + 1) * P],
                                      xc[:, k, :], start=(k == 0), stop=(k == KD - 1))
                    last.then_inc(proj_ps, 1)
                    for t in range(TT):
                        for k in range(KD):
                            last = mm(S[1][:, 1, t * G * HD:(t + 1) * G * HD], xc[:, k, t * P:(t + 1) * P],
                                      w["v"][:, k, :], start=(k == 0), stop=(k == KD - 1))
                    last.then_inc(proj_ps, 1)
                    pe.wait_ge(proj_ps, b * 3 + 3)
                    pe.sem_inc(xc_free, 1)

                def scores(b, n):
                    if n < 2:
                        pe.wait_ge(rot_ready, b * 3 + 2 + n)
                    else:
                        pe.wait_ge(p_ready, b * NG + n - 1)
                    for i in range(2):
                        r, g = n // 2, n % 2 * 2 + i
                        for t in range(TT):
                            dst = S[n % 2][:, i, t * P:t * P + (t + 1) * P]
                            mm(dst, qr[:, r, t * P:(t + 1) * P], kr[:, g, 0:(t + 1) * P], start=True, stop=False)
                            last = mm(S[n % 2][:, i, 2 * t * P:(2 * t + 1) * P], c["idb"], c["maskb"],
                                      start=False, stop=True)
                    last.then_inc(s_ps, 1)

                def turn(b, n):
                    pe.wait_ge(p_ready, b * NG + n + 1)
                    for i in range(2):
                        if n > 0:
                            pe.wait_ge(pt_ready, b * 2 * NG + 2 * (n - 1) + i + 1)
                        for j in range(3):
                            last = nc.tensor.transpose(PT[i][:, j * P:(j + 1) * P],
                                                       pr[:, n % 2, i, j * P:(j + 1) * P], c["id"])
                        last.then_inc(pt_ps, 1)

                def values(b, n):
                    for i in range(2):
                        r, g = n // 2, n % 2 * 2 + i
                        h = 4 * g + r
                        pe.wait_ge(pt_ready, b * 2 * NG + 2 * n + i + 1)
                        pp = pt[:, n % 2, i, :]
                        mm(O[:, 0, h, :], pp[:, 0:P], va[:, 0, g, :], start=True, stop=True)
                        mm(O[:, 1, h, :], pp[:, P:2 * P], va[:, 0, g, :], start=True, stop=False)
                        last = mm(O[:, 1, h, :], pp[:, 2 * P:3 * P], va[:, 1, g, :], start=False, stop=True)
                    last.then_inc(av_ps, 1)

                def turn_output(b):
                    pe.wait_ge(on_ready, b + 1)
                    for h in range(KD):
                        for t in range(TT):
                            last = nc.tensor.transpose(PT[0][:, (h * TT + t) * P:(h * TT + t + 1) * P],
                                                       on[:, t, h * P:(h + 1) * P], c["id"])
                    last.then_inc(oT_ps, 1)

                def project_output(b):
                    pe.wait_ge(oT_ready, b + 1)
                    for t in range(TT):
                        for k in range(KD):
                            last = mm(PT[1][:, t * D:(t + 1) * D], oT[:, k, t * P:(t + 1) * P], w["o"][:, k, :],
                                      start=(k == 0), stop=(k == KD - 1))
                    last.then_inc(y_ps, 1)

                def rest(b, more):
                    for n in range(2, NG):
                        scores(b, n)
                        if n == 2:
                            pe.wait_ge(z_ready, b + 1)
                        turn(b, n - 2)
                        if n >= 3:
                            values(b, n - 3)
                    turn(b, NG - 2)
                    values(b, NG - 3)
                    turn(b, NG - 1)
                    if more:
                        project(b + 1)
                    values(b, NG - 2)
                    values(b, NG - 1)

                w["early"](pe)
                pe.sem_inc(z_ready, 1)
                project(0)
                w["late"](pe)
                scores(0, 0)
                scores(0, 1)
                with pe.Fori(0, B - 1) as b:
                    rest(b, True)
                    scores(b + 1, 0)
                    turn_output(b)
                    scores(b + 1, 1)
                    project_output(b)
                rest(B - 1, False)
                turn_output(B - 1)
                project_output(B - 1)

            @block.scalar
            def _(act):
                nc.scalar.preload_act_table(ACT.Exp)

                def exponentials(b, n):
                    act.wait_ge(nm_ready, b * NG + n + 1)
                    if n >= 2:
                        act.wait_ge(pt_ps, b * 2 * NG + 2 * (n - 1))
                    for i in range(2):
                        for t in range(TT):
                            s = slice(t * P, t * P + (t + 1) * P)
                            last = nc.scalar.activation(pr[:, n % 2, i, s], S[n % 2][:, i, s], ACT.Exp,
                                                        bias=nm[:, n % 2, t, i:i + 1])
                    last.then_inc(p_ready, 1)

                def rest(b):
                    for n in range(2, NG):
                        exponentials(b, n)

                def output(b):
                    act.wait_ge(oT_ps, b + 1)
                    nc.scalar.activation(oT[:, :, :], PT[0].rearrange("p (k t) -> p k t", k=KD), ACT.Copy).then_inc(oT_ready, 1)

                exponentials(0, 0)
                exponentials(0, 1)
                with act.Fori(0, B - 1) as b:
                    rest(b)
                    exponentials(b + 1, 0)
                    output(b)
                    exponentials(b + 1, 1)
                rest(B - 1)
                output(B - 1)

            @block.vector
            def _(dve):
                st = Steps(dve, steps, LN_STEPS + 1)
                nc.vector.memset(va[:, :, :, HD:V1], 1.0)
                nc.vector.memset(kr[:, :, :], 0.0).then_inc(rot_steps, 1)

                def rotate(b):
                    dve.wait_ge(proj_ps, b * 3 + 1)
                    for j in range(2):
                        last = nc.vector.tensor_tensor(qr[:, 2 * j:2 * j + 2, :],
                                                       S[0][:, j, :].rearrange("p (r t) -> p r t", r=2),
                                                       bc(c["l0_q"], 1, 2), ALU.mult)
                    last.then_inc(rot_ready, 1)
                    dve.wait_ge(proj_ps, b * 3 + 2)
                    nc.vector.tensor_tensor(k1[:, :, :], S[1][:, 0, :].rearrange("p (r t) -> p r t", r=2),
                                            c["l0_k"], ALU.mult).then_inc(rot_steps, 1)
                    dve.wait_ge(rot_steps, b + 2)
                    for g in range(G):
                        rows = slice(32 * g, 32 * g + 32)
                        last = nc.vector.tensor_tensor(kr[rows, g, :], k1[rows, 0, :], k1[rows, 1, :], ALU.add)
                    last.then_inc(rot_ready, 1)

                def values_in(b):
                    dve.wait_ge(proj_ps, b * 3 + 3)
                    nc.vector.tensor_copy(va[:, :, :, 0:HD],
                                          S[1][:, 1, 0:TT * G * HD].rearrange("p (t g e) -> p t g e", t=TT, g=G)).then_inc(rot_ready, 1)

                def maxima(b, n):
                    dve.wait_ge(s_ps, b * NG + n + 1)
                    if n >= 2:
                        dve.wait_ge(p_ready, b * NG + n - 1)
                    for t in range(TT):
                        last = nc.vector.tensor_reduce(nm[:, n % 2, t, :], S[n % 2][:, :, t * P:t * P + (t + 1) * P],
                                                       AX.X, ALU.max, negate=True)
                    last.then_inc(nm_ready, 1)

                def out_of_psum(b, n):
                    for i in range(2):
                        dve.wait_ge(pt_ps, b * 2 * NG + 2 * n + i + 1)
                        if n >= 2:
                            dve.wait_ge(av_ps, b * NG + n - 1)
                        nc.vector.tensor_copy(pt[:, n % 2, i, :], PT[i][:, 0:3 * P]).then_inc(pt_ready, 1)

                def rest(b, more):
                    for n in range(2, NG):
                        maxima(b, n)
                        out_of_psum(b, n - 2)
                    out_of_psum(b, NG - 2)
                    out_of_psum(b, NG - 1)
                    if more:
                        rotate(b + 1)
                    dve.wait_ge(av_ps, b * NG + NG)
                    st.do(nc.vector.reciprocal(rec[:, :, :], O[:, :, :, HD]))
                    for t in range(TT):
                        last = nc.vector.tensor_tensor(on[:, t, :].rearrange("p (h e) -> p h e", e=HD), O[:, t, :, 0:HD],
                                                       bc(rec[:, t, :], 2, HD), ALU.mult)
                    last.then_inc(on_ready, 1)
                    if more:
                        values_in(b + 1)

                def head(b):
                    for n in range(2):
                        maxima(b, n)

                def output(b):
                    dve.wait_ge(y_ps, b + 1)
                    add_and_measure(nc, st, x_sb, mv, b * TT, TT, PT[1].rearrange("p (t n) -> p t n", t=TT), lw, z_ready, b + 2)
                    st.end()

                rotate(0)
                values_in(0)
                head(0)
                with dve.Fori(0, B - 1) as b:
                    st.begin(b)
                    rest(b, True)
                    head(b + 1)
                    output(b)
                st.begin(B - 1)
                rest(B - 1, False)
                output(B - 1)



def l0_ffn(nc, c, x_sb, mv, xT, w, psum):
    E, G, EG, LAT, SH = 32, 4, 8, 128, 512
    with ExitStack() as ctx:
        sb = lambda name, shape, dt=F32: ctx.enter_context(nc.sbuf_tensor("l0f_" + name, shape, dt))
        sem = lambda name: ctx.enter_context(nc.semaphore("l0f_" + name))
        xl = sb("xl", [LAT, TOK])
        relu = sb("relu", [P, 2, CN])
        sq = sb("sq", [P, 2, CN])
        hg = sb("hg", [P, 2, CN])
        hs = sb("hs", [P, SH // P, CN])
        yl = sb("yl", [LAT, CN])
        wsum = sb("wsum", [P, NT])
        tokens = lambda ap: ap.rearrange("p (t e) -> p t e", t=NT)
        ex, sc = tokens(relu[:, 0, :]), tokens(relu[:, 1, :])
        cand, left = tokens(sq[:, 0, :]), tokens(sq[:, 1, :])
        rest = tokens(hg[:, 0, :])
        top = hg[:, 1, :].rearrange("p (j e) -> p j e", e=8)
        hs_flat = hs[:, :, :].rearrange("p m n -> p (m n)")
        c3 = hs_flat[:, 0:NT * 3 * E // 2].bitcast(BF16).rearrange("p (t a e) -> p t a e", t=NT, a=3)
        small, place = {}, 2 * CN
        for name, n in (("garr", 14), ("gpick", 8), ("gtop", 8), ("gout", 10), ("gsel", G)):
            small[name] = tokens(hs_flat[:, place:place + NT * n])
            place += NT * n
        garr, gpick, gtop, gout, gsel = small.values()
        c3T = sb("c3T", [3 * E, TOK], BF16)
        lw = ln_scratch(sb, CH)
        HB = [psum[:, 0, :], psum[:, 1, :], psum[:, 5, :]]
        GB = [psum[:, 2, :], psum[:, 3, :]]
        YL = psum[:, 4, :]
        LOGITS = psum[:, 0, :].rearrange("p (t e) -> p t e", t=NT)
        Y = psum[:, 6:8, :].rearrange("p a (t n) -> p (a t) n", t=2)

        z_ready = sem("z_ready")
        route_steps = sem("route_steps")
        logit_ps = sem("logit_ps")
        ex_ready = sem("ex_ready")
        xl_ps = sem("xl_ps")
        xl_ready = sem("xl_ready")
        c3_ready = sem("c3_ready")
        c3T_ps = sem("c3T_ps")
        c3T_ready = sem("c3T_ready")
        h_ps = sem("h_ps")
        g_ps = sem("g_ps")
        sq_ready = sem("sq_ready")
        hg_ready = sem("hg_ready")
        used = sem("used")
        yl_ready = sem("yl_ready")
        y_ps = sem("y_ps")
        relu_ready = sem("relu_ready")
        steps = sem("steps")
        NH = E + SH // P

        with nc.Block() as block:
            @block.tensor
            def _(pe):
                mm = nc.tensor.matmul
                w["early"](pe)
                for t in range(NT):
                    for k in range(KD):
                        last = mm(LOGITS[:, t, :], xT[:, k, t * P:(t + 1) * P], w["gate"][:, k, :], start=(k == 0), stop=(k == KD - 1))
                last.then_inc(logit_ps, 1)
                w["late"](pe)
                for j in range(NCH):
                    for k in range(KD):
                        last = mm(psum[:, 4 + j, :], w["fc1"][:, k, :], xT[:, k, j * CN:(j + 1) * CN], start=(k == 0), stop=(k == KD - 1))
                    last.then_inc(xl_ps, 1)
                pe.wait_ge(c3_ready, 1)
                for t in range(NT):
                    last = nc.tensor.transpose(psum[0:3 * E, 2 + t // 8, (t % 8) * P // 2:(t % 8 + 1) * P // 2].bitcast(BF16),
                                               c3[:, t, :, :].rearrange("p a e -> p (a e)"), c["idb"])
                last.then_inc(c3T_ps, 1)
                pe.wait_ge(c3T_ready, 1)
                pe.wait_ge(xl_ready, NCH)
                with pe.Fori(0, NCH) as b:
                    chunk = bass.ds(b * CN, CN)

                    def hidden(e):
                        if e >= 3:
                            pe.wait_ge(sq_ready, b * NH + e - 2)
                        if e < E:
                            mm(HB[e % 3], w["w1"][:, e, :], xl[:, chunk], start=True, stop=True).then_inc(h_ps, 1)
                            if e >= 2:
                                pe.wait_ge(hg_ready, b * E + e - 1)
                            mm(GB[e % 2], c["sel0"][:, e * P:(e + 1) * P], c3T[:, chunk], start=True, stop=True).then_inc(g_ps, 1)
                        else:
                            m = e - E
                            for k in range(KD):
                                last = mm(HB[e % 3], w["up"][:, k, m * P:(m + 1) * P], xT[:, k, chunk], start=(k == 0), stop=(k == KD - 1))
                            last.then_inc(h_ps, 1)

                    def latent(e):
                        pe.wait_ge(hg_ready, b * E + e + 1)
                        mm(YL, w["w2"][:, e, :], hg[:, e % 2, :], start=(e == 0), stop=(e == E - 1)).then_inc(used, 1)

                    for e in range(NH):
                        hidden(e)
                        if 2 <= e < E + 2:
                            latent(e - 2)
                    pe.wait_ge(z_ready, b + 1)
                    pe.wait_ge(yl_ready, b + 1)
                    pe.wait_ge(sq_ready, b * NH + NH)
                    for t in range(CH):
                        for m in range(SH // P):
                            mm(Y[:, t, :], hs[:, m, t * P:(t + 1) * P], w["down"][:, m, :], start=(m == 0), stop=False)
                        last = mm(Y[:, t, :], yl[:, t * P:(t + 1) * P], w["fc2"][:, :], start=False, stop=True)
                    last.then_inc(y_ps, 1)

            @block.scalar
            def _(act):
                nc.scalar.preload_act_table(ACT.Exp)
                act.wait_ge(logit_ps, 1)
                nc.scalar.activation(ex[:, :, :], LOGITS, ACT.Exp, scale=-1.0).then_inc(ex_ready, 1)
                for j in range(NCH):
                    act.wait_ge(xl_ps, j + 1)
                    nc.scalar.activation(xl[:, j * CN:(j + 1) * CN], psum[:, 4 + j, :], ACT.Copy).then_inc(xl_ready, 1)
                with act.Fori(0, NCH) as b:
                    for e in range(NH):
                        act.wait_ge(h_ps, b * NH + e + 1)
                        if 2 <= e < E:
                            act.wait_ge(hg_ready, b * E + e - 1)
                        nc.scalar.activation(relu[:, e % 2, :], HB[e % 3], ACT.Relu).then_inc(relu_ready, 1)
                        act.wait_ge(relu_ready, b * NH + e + 1)
                        dst = sq[:, e % 2, :] if e < E else hs[:, e - E, :]
                        nc.scalar.activation(dst, relu[:, e % 2, :], ACT.Square).then_inc(sq_ready, 1)

            @block.vector
            def _(dve):
                nc.vector.memset(garr[:, :, 0:4], LOW)
                nc.vector.memset(garr[:, :, 8:14], BIG)
                nc.vector.memset(gpick[:, :, :], BIG)
                w["early"](dve)
                st = Steps(dve, route_steps, 0)
                st.begin(0)
                dve.wait_ge(ex_ready, 1)
                st.do(nc.vector.tensor_scalar(ex[:, :, :], ex[:, :, :], 1.0, None, ALU.add))
                st.do(nc.vector.reciprocal(sc[:, :, :], ex[:, :, :]))
                st.do(nc.vector.tensor_tensor(cand[:, :, :], sc[:, :, :], bc(w["bias"][:, :], 1, NT), ALU.add))
                for j in range(NT * G):
                    last = nc.vector.max(top[:, j, :], cand[:, j // G, (j % G) * EG:(j % G + 1) * EG])
                st.do(last)
                st.do(nc.vector.tensor_tensor(garr[:, :, 4:8], top[:, :, 0].rearrange("p (t g) -> p t g", g=G),
                                              top[:, :, 1].rearrange("p (t g) -> p t g", g=G), ALU.add))
                for t in range(NT):
                    last = nc.vector.max(gtop[:, t, :], garr[:, t, 0:8])
                st.do(last)
                st.do(nc.vector.tensor_copy(gpick[:, :, 0:2], gtop[:, :, 0:2]))
                for t in range(NT):
                    last = nc.vector.match_replace(gout[:, t, :], gpick[:, t, :], garr[:, t, 4:14], -BIG)
                st.do(last)
                st.do(nc.vector.tensor_scalar(gsel[:, :, :], gout[:, :, 0:4], -BIG, None, ALU.is_equal))
                st.do(nc.vector.tensor_scalar(gsel[:, :, :], gsel[:, :, :], -NEG, NEG, ALU.mult, ALU.add))
                st.do(nc.vector.tensor_tensor(cand[:, :, :].rearrange("p t (g e) -> p (t g) e", g=G),
                                              cand[:, :, :].rearrange("p t (g e) -> p (t g) e", g=G),
                                              bc(gsel[:, :, :].rearrange("p t g -> p (t g)"), 2, EG), ALU.add))
                for t in range(NT):
                    last = nc.vector.max(gtop[:, t, :], cand[:, t, :])
                st.do(last)
                for t in range(NT):
                    last = nc.vector.match_replace(left[:, t, :], gtop[:, t, :], cand[:, t, :], -BIG)
                st.do(last)
                st.do(nc.vector.scalar_tensor_tensor(left[:, :, :], left[:, :, :], -BIG, sc[:, :, :], ALU.is_equal, ALU.mult))
                st.do(nc.vector.tensor_reduce(wsum[:, :], left[:, :, :], AX.X, ALU.add))
                st.do(nc.vector.reciprocal(wsum[:, :], wsum[:, :]))
                st.do(nc.vector.scalar_tensor_tensor(left[:, :, :], left[:, :, :], 2.5, bc(wsum[:, :], 2, E), ALU.mult, ALU.mult))
                split3(nc, st, left[:, :, :], [c3[:, :, j, :] for j in range(3)], rest[:, :, :])
                nc.vector.memset(lw["carrier"][:, :], 0.0).then_inc(c3_ready, 1)
                dve.wait_ge(c3T_ps, 1)
                nc.vector.tensor_copy(c3T[:, :].rearrange("p (a n) -> p a n", a=2), psum[0:3 * E, 2:4, :].bitcast(BF16)).then_inc(c3T_ready, 1)
                dve.sem_inc(z_ready, 1)
                st = Steps(dve, steps, LN_STEPS)
                with dve.Fori(0, NCH) as b:
                    st.begin(b)
                    for e in range(E):
                        dve.wait_ge(g_ps, b * E + e + 1)
                        dve.wait_ge(sq_ready, b * NH + e + 1)
                        if e >= 2:
                            dve.wait_ge(used, b * E + e - 1)
                        nc.vector.tensor_tensor(hg[:, e % 2, :], sq[:, e % 2, :], GB[e % 2], ALU.mult).then_inc(hg_ready, 1)
                    dve.wait_ge(used, b * E + E)
                    nc.vector.tensor_copy(yl[:, :], YL).then_inc(yl_ready, 1)
                    dve.wait_ge(y_ps, b + 1)
                    add_and_measure(nc, st, x_sb, mv, b * CH, CH, Y, lw, z_ready, b + 2)
                    st.end()



def l1_attention(nc, c, x_sb, mv, xT, w, psum):
    H, HD = 16, 128
    EPS = 1e-5
    NJ = 8
    NG = H // 2
    with ExitStack() as ctx:
        sb = lambda name, shape, dt=F32: ctx.enter_context(nc.sbuf_tensor("l1a_" + name, shape, dt))
        sem = lambda name: ctx.enter_context(nc.semaphore("l1a_" + name))
        xc = sb("xc", [P, KD, T])
        qT = sb("qT", [HD, H, T])
        kT = sb("kT", [HD, H, T])
        va = sb("va", [P, TT, H * HD])
        ko = sb("ko", [P, H * T])
        kn = ko[:, :].rearrange("p (t h d) -> p (t h) d", t=TT, h=H)
        oT = ko[:, :].rearrange("p (h t) -> p h t", h=H)
        ksq = sb("ksq", [P, 2, 512])
        qsq = sb("qsq", [P, 2, 512])
        pr = sb("pr", [P, 2, 2, 3 * P])
        pt = sb("pt", [P, 2, 2, 3 * P])
        gain = sb("gain", [P, 1])
        ssk = sb("ssk", [P, TT * H])
        rk = sb("rk", [P, TT * H])
        rq = sb("rq", [P, TT, H])
        vv = sb("vv", [P, TT * H])
        tmp = sb("tmp", [P, TT * H])
        nm = sb("nm", [P, 2, TT, 2])
        nb = sb("nb", [P, 2, TT, 2])
        sums = sb("sums", [P, 2, TT, 2])
        rec = sb("rec", [P, 2, TT, 2])
        lw = ln_scratch(sb, TT)
        bank = lambda i: psum[:, i, :]
        S = [psum[:, 0:2, :], psum[:, 2:4, :]]
        PT = [bank(4), bank(5)]

        x_staged = sem("x_staged")
        xc_free = sem("xc_free")
        k_ps = sem("k_ps")
        q_ps = sem("q_ps")
        v_ps = sem("v_ps")
        k_out = sem("k_out")
        q_sq = sem("q_sq")
        q_out = sem("q_out")
        v_out = sem("v_out")
        k_sum = sem("k_sum")
        ssq_ps = sem("ssq_ps")
        kn_ready = sem("kn_ready")
        kT_ps = sem("kT_ps")
        kT_ready = sem("kT_ready")
        s_ps = sem("s_ps")
        nb_ready = sem("nb_ready")
        p_exp = sem("p_exp")
        p_norm = sem("p_norm")
        pt_ps = sem("pt_ps")
        pt_ready = sem("pt_ready")
        av_ps = sem("av_ps")
        o_ready = sem("o_ready")
        y_ps = sem("y_ps")
        z_ready = sem("z_ready")
        steps = sem("steps")

        with nc.Block() as block:
            @block.sync
            def _(sp):
                with sp.Fori(0, B) as b:
                    sp.wait_ge(xc_free, b + 1)
                    sp.dma_start(xc[:, :, :], xT[:, :, bass.ds(b * T, T)]).then_inc(x_staged, 16)

            @block.tensor
            def _(pe):
                mm = nc.tensor.matmul
                pe.sem_inc(xc_free, 1)
                w["early"](pe)
                w["late"](pe)
                with pe.Fori(0, B) as b:
                    pe.wait_ge(x_staged, b * 16 + 16)

                    def square_sums(j):
                        pe.wait_ge(q_sq, b * NJ + j + 1)
                        pe.wait_ge(q_out, b * NJ + 1)
                        for i in range(2):
                            for t in range(TT):
                                h = 2 * j + i
                                last = mm(bank(4)[:, t * H + h:t * H + h + 1], qsq[:, j % 2, i * T + t * P:i * T + (t + 1) * P],
                                          c["one"], start=True, stop=True)
                        last.then_inc(ssq_ps, 1)

                    for j in range(NJ):
                        t, cols = j // 4, slice((j % 4) * 512, (j % 4 + 1) * 512)
                        if j >= 2:
                            pe.wait_ge(k_out, b * NJ + j - 1)
                        for k in range(KD):
                            last = mm(bank(j % 2), xc[:, k, t * P:(t + 1) * P], w["k"][:, k, cols], start=(k == 0), stop=(k == KD - 1))
                        last.then_inc(k_ps, 1)

                    def turn_keys(m):
                        if m >= 2:
                            pe.wait_ge(kT_ready, b * NG + m - 1)
                        for i in range(2):
                            for t in range(TT):
                                last = nc.tensor.transpose(bank(m % 2)[:, i * T + t * P:i * T + (t + 1) * P],
                                                           kn[:, t * H + 2 * m + i, :], c["id"])
                        last.then_inc(kT_ps, 1)

                    for j in range(NJ):
                        t, cols = j // 4, slice((j % 4) * 512, (j % 4 + 1) * 512)
                        if j >= 2:
                            pe.wait_ge(q_out, b * NJ + j - 1)
                        for i in range(2):
                            for k in range(KD):
                                last = mm(bank(2 + j % 2)[:, i * T:(i + 1) * T], w["q"][:, k, (2 * j + i) * HD:(2 * j + i + 1) * HD],
                                          xc[:, k, :], start=(k == 0), stop=(k == KD - 1))
                        last.then_inc(q_ps, 1)
                        if j >= 2:
                            pe.wait_ge(v_out, b * NJ + j - 1)
                        for k in range(KD):
                            last = mm(bank(6 + j % 2), xc[:, k, t * P:(t + 1) * P], w["v"][:, k, cols], start=(k == 0), stop=(k == KD - 1))
                        last.then_inc(v_ps, 1)
                        if j >= 1:
                            square_sums(j - 1)
                        if j == 3:
                            pe.wait_ge(kn_ready, b + 1)
                        if j >= 3:
                            turn_keys(j - 3)
                    pe.wait_ge(v_ps, b * NJ + NJ)
                    pe.sem_inc(xc_free, 1)
                    square_sums(NJ - 1)
                    for m in range(NJ - 3, NG):
                        turn_keys(m)
                    pe.wait_ge(q_out, b * NJ + NJ)

                    def scores(n):
                        if n < 2:
                            pe.wait_ge(kT_ready, b * NG + NG)
                        else:
                            pe.wait_ge(p_exp, b * NG + n - 1)
                        for i in range(2):
                            h = 2 * n + i
                            for t in range(TT):
                                mm(S[n % 2][:, i, t * P:t * P + (t + 1) * P], qT[:, h, t * P:(t + 1) * P], kT[:, h, 0:(t + 1) * P],
                                   start=True, stop=False)
                                last = mm(S[n % 2][:, i, 2 * t * P:(2 * t + 1) * P], c["idb"], c["maskb"], start=False, stop=True)
                        last.then_inc(s_ps, 1)

                    def turn(n):
                        pe.wait_ge(p_norm, b * NG + n + 1)
                        for i in range(2):
                            if n > 0:
                                pe.wait_ge(pt_ready, b * 2 * NG + 2 * (n - 1) + i + 1)
                            for j in range(3):
                                last = nc.tensor.transpose(PT[i][:, j * P:(j + 1) * P], pr[:, n % 2, i, j * P:(j + 1) * P], c["id"])
                            last.then_inc(pt_ps, 1)

                    def values(n):
                        if n >= 2:
                            pe.wait_ge(o_ready, b * NG + n - 1)
                        for i in range(2):
                            h = 2 * n + i
                            pe.wait_ge(pt_ready, b * 2 * NG + 2 * n + i + 1)
                            pp, o = pt[:, n % 2, i, :], bank(6 + n % 2)[:, i * T:(i + 1) * T]
                            mm(o, va[:, 0, h * HD:(h + 1) * HD], pp[:, 0:2 * P], start=True, stop=False)
                            last = mm(o[:, P:2 * P], va[:, 1, h * HD:(h + 1) * HD], pp[:, 2 * P:3 * P], start=False, stop=True)
                        last.then_inc(av_ps, 1)

                    for n in range(NG + 3):
                        if n < NG:
                            scores(n)
                        if 2 <= n < NG + 2:
                            turn(n - 2)
                        if n >= 3:
                            values(n - 3)
                    pe.wait_ge(o_ready, b * NG + NG)
                    for t in range(TT):
                        for h in range(H):
                            last = mm(PT[0][:, t * D:(t + 1) * D], oT[:, h, t * P:(t + 1) * P], w["o"][:, h, :],
                                      start=(h == 0), stop=(h == H - 1))
                    last.then_inc(y_ps, 1)

            @block.scalar
            def _(act):
                nc.scalar.preload_act_table(ACT.Exp)
                with act.Fori(0, B) as b:
                    for j in range(NJ):
                        t, j4 = j // 4, j % 4
                        act.wait_ge(k_ps, b * NJ + j + 1)
                        if j >= 2:
                            act.wait_ge(k_sum, b * NJ + j - 1)
                        nc.scalar.activation(kn[:, t * H + 4 * j4:t * H + 4 * j4 + 4, :],
                                             bank(j % 2).rearrange("p (h d) -> p h d", h=4), ACT.Copy)
                        nc.scalar.activation(ksq[:, j % 2, :], bank(j % 2), ACT.Square).then_inc(k_out, 1)

                    def keys_out(m):
                        act.wait_ge(kT_ps, b * NG + m + 1)
                        nc.scalar.activation(kT[:, 2 * m:2 * m + 2, :], bank(m % 2).rearrange("p (i t) -> p i t", i=2), ACT.Copy,
                                             scale=gain[:, :]).then_inc(kT_ready, 1)

                    for j in range(NJ):
                        act.wait_ge(q_out, b * NJ + j + 1)
                        if j >= 2:
                            act.wait_ge(ssq_ps, b * NJ + j - 1)
                        nc.scalar.activation(qsq[:, j % 2, :], qT[:, 2 * j:2 * j + 2, :].rearrange("p i t -> p (i t)"), ACT.Square).then_inc(q_sq, 1)
                        if j >= 3:
                            keys_out(j - 3)
                    for m in range(NJ - 3, NG):
                        keys_out(m)

                    def out(n):
                        act.wait_ge(av_ps, b * NG + n + 1)
                        nc.scalar.activation(oT[:, 2 * n:2 * n + 2, :], bank(6 + n % 2).rearrange("p (i t) -> p i t", i=2),
                                             ACT.Copy).then_inc(o_ready, 1)

                    for n in range(NG + 3):
                        if n < NG:
                            act.wait_ge(nb_ready, b * NG + n + 1)
                            if n >= 2:
                                act.wait_ge(pt_ps, b * 2 * NG + 2 * (n - 1))
                            for i in range(2):
                                for t in range(TT):
                                    s = slice(t * P, t * P + (t + 1) * P)
                                    last = nc.scalar.activation(pr[:, n % 2, i, s], S[n % 2][:, i, s], ACT.Exp,
                                                                bias=nb[:, n % 2, t, i:i + 1], scale=rq[:, t, 2 * n + i:2 * n + i + 1],
                                                                accum_out=sums[:, n % 2, t, i:i + 1])
                            last.then_inc(p_exp, 1)
                        if n >= 3:
                            out(n - 3)

            @block.vector
            def _(dve):
                st = Steps(dve, steps, L1A_STEPS)
                w["early"](dve)
                nc.vector.tensor_tensor(gain[:, :], w["gq"], w["gk"], ALU.mult)
                with dve.Fori(0, B) as b:
                    st.begin(b)
                    for j in range(NJ):
                        dve.wait_ge(k_out, b * NJ + j + 1)
                        nc.vector.tensor_reduce(ssk[:, 4 * j:4 * j + 4], ksq[:, j % 2, :].rearrange("p (h d) -> p h d", h=4),
                                                AX.X, ALU.add).then_inc(k_sum, 1)

                    def queries_and_values_out(j):
                        t, cols = j // 4, slice((j % 4) * 512, (j % 4 + 1) * 512)
                        dve.wait_ge(q_ps, b * NJ + j + 1)
                        nc.vector.tensor_copy(qT[:, 2 * j:2 * j + 2, :], bank(2 + j % 2).rearrange("p (i t) -> p i t", i=2)).then_inc(q_out, 1)
                        dve.wait_ge(v_ps, b * NJ + j + 1)
                        nc.vector.tensor_copy(va[:, t, cols], bank(6 + j % 2)).then_inc(v_out, 1)

                    dve.wait_ge(k_sum, b * NJ + NJ)
                    st.do(nc.vector.tensor_scalar(vv[:, :], ssk[:, :], 1.0 / HD, EPS, ALU.mult, ALU.add))
                    newton_rsqrt(nc, st, vv[:, :], rk[:, :], tmp[:, :])
                    st.wait()
                    for j in range(NJ):
                        queries_and_values_out(j)
                        if j < 2:
                            part = slice(j * H, (j + 1) * H)
                            last = nc.vector.tensor_tensor(kn[:, part, :], kn[:, part, :], bc(rk[:, part], 2, HD), ALU.mult)
                            if j == 1:
                                last.then_inc(kn_ready, 1)
                    dve.wait_ge(ssq_ps, b * NJ + NJ)
                    st.do(nc.vector.tensor_scalar(vv[:, :], bank(4)[:, 0:TT * H], 1.0 / HD, EPS, ALU.mult, ALU.add))
                    flat = rq[:, :, :].rearrange("p t h -> p (t h)")
                    newton_rsqrt(nc, st, vv[:, :], flat, tmp[:, :])
                    st.wait()
                    st.do(nc.vector.tensor_scalar(flat, flat, float(HD) ** -0.5, None, ALU.mult))

                    def maxima(n):
                        dve.wait_ge(s_ps, b * NG + n + 1)
                        if n >= 2:
                            dve.wait_ge(p_exp, b * NG + n - 1)
                        for t in range(TT):
                            last = nc.vector.tensor_reduce(nm[:, n % 2, t, :], S[n % 2][:, :, t * P:t * P + (t + 1) * P],
                                                           AX.X, ALU.max, negate=True)
                        st.do(last)
                        nc.vector.tensor_tensor(nb[:, n % 2, :, :], nm[:, n % 2, :, :], rq[:, :, 2 * n:2 * n + 2], ALU.mult).then_inc(nb_ready, 1)

                    def normalise(n):
                        dve.wait_ge(p_exp, b * NG + n + 1)
                        st.do(nc.vector.reciprocal(rec[:, n % 2, :, :], sums[:, n % 2, :, :]))
                        for i in range(2):
                            for t in range(TT):
                                s = slice(t * P, t * P + (t + 1) * P)
                                last = nc.vector.tensor_scalar(pr[:, n % 2, i, s], pr[:, n % 2, i, s], rec[:, n % 2, t, i:i + 1], None, ALU.mult)
                        last.then_inc(p_norm, 1)

                    def out_of_psum(n):
                        for i in range(2):
                            dve.wait_ge(pt_ps, b * 2 * NG + 2 * n + i + 1)
                            if n >= 2:
                                dve.wait_ge(av_ps, b * NG + n - 1)
                            nc.vector.tensor_copy(pt[:, n % 2, i, :], PT[i][:, 0:3 * P]).then_inc(pt_ready, 1)

                    for n in range(NG + 2):
                        if n < NG:
                            maxima(n)
                        if 1 <= n <= NG:
                            normalise(n - 1)
                        if n >= 2:
                            out_of_psum(n - 2)
                    dve.wait_ge(y_ps, b + 1)
                    add_and_measure(nc, st, x_sb, mv, b * TT, TT, PT[0].rearrange("p (t n) -> p t n", t=TT), lw, z_ready)
                    st.end()


L1A_STEPS = 1 + NEWTON_STEPS + 1 + NEWTON_STEPS + 1 + 2 * 8 + LN_STEPS



def l1_ffn(nc, c, x_sb, mv, xT, w, psum):
    E, K, I, TOP, SH = 128, 8, 128, 4, 2
    EPS = 1e-8
    NH = K + SH
    with ExitStack() as ctx:
        sb = lambda name, shape, dt=F32: ctx.enter_context(nc.sbuf_tensor("l1f_" + name, shape, dt))
        sem = lambda name: ctx.enter_context(nc.semaphore("l1f_" + name))
        mp = sb("mp", [P, K, 2])
        mix = sb("mix", [P, K])
        msum = sb("msum", [P, 1])
        mixb = sb("mixb", [P, K, I])
        pb = sb("pb", [P, NT, E + 8 - TOP])
        nm = sb("nm", [P, NT])
        sums = sb("sums", [P, NT])
        top = sb("top", [P, NT, 8])
        pick = sb("pick", [P, NT, 8])
        left = sb("left", [P, NT, E + 8 - TOP])
        co = sb("co", [P, NT, E])
        wsum = sb("wsum", [P, NT])
        coT = sb("coT", [E, TOK])
        x_hi = sb("x_hi", [P, KD, TOK], F32R)
        x_lo = xT[:, :, :].bitcast(F32R)
        w_hi = sb("w_hi", [P, 2, 2 * KD, P], F32R)
        w_lo = sb("w_lo", [P, 2, 2 * KD, P], F32R)
        sg = sb("sg", [P, 2, CN])
        gu = sb("gu", [P, 2, CN])
        t2 = sb("t2", [P, 2, CN])
        acc = sb("acc", [I, CN])
        hs = sb("hs", [P, SH, CN])
        lw = ln_scratch(sb, CH)
        bank = lambda i: psum[:, i, :]
        GB, UB, CB = [bank(0), bank(1)], [bank(2), bank(3)], [bank(4), bank(5)]
        Y = psum[:, 6:8, :].rearrange("p a (t n) -> p (a t) n", t=2)
        LOGITS = psum[:, 0:4, :].rearrange("p a (t e) -> p (a t) e", e=E)

        route_steps = sem("route_steps")
        z_ready = sem("z_ready")
        logit_ps = sem("logit_ps")
        nm_ready = sem("nm_ready")
        ex_ready = sem("ex_ready")
        co_ready = sem("co_ready")
        coT_ps = sem("coT_ps")
        coT_ready = sem("coT_ready")
        mix_ready = sem("mix_ready")
        h_ps = sem("h_ps")
        sg_ready = sem("sg_ready")
        gu_ready = sem("gu_ready")
        t2_ready = sem("t2_ready")
        acc_ready = sem("acc_ready")
        y_ps = sem("y_ps")
        xhi_ready, xlo_ready, whi_ready, wlo_ready = c["split_sems"]
        steps = sem("steps")

        with nc.Block() as block:
            @block.tensor
            def _(pe):
                mm = nc.tensor.matmul
                w["early"](pe)
                for t in range(NT):
                    for k in range(KD):
                        last = mm(LOGITS[:, t, :], xT[:, k, t * P:(t + 1) * P], w["router"][:, k, :], start=(k == 0), stop=(k == KD - 1))
                    if t % 4 == 3:
                        last.then_inc(logit_ps, 1)
                pe.wait_ge(mix_ready, 1)
                pe.wait_ge(co_ready, 1)
                for t in range(NT):
                    last = nc.tensor.transpose(psum[:, 4 + t // 4, (t % 4) * P:(t % 4 + 1) * P], co[:, t, :], c["id"])
                last.then_inc(coT_ps, 1)
                pe.wait_ge(coT_ready, 1)
                w["late"](pe)
                pe.wait_ge(xlo_ready, NCH)
                with pe.Fori(0, NCH) as b:
                    chunk = bass.ds(b * CN, CN)
                    for e in range(NH):
                        if e >= 2:
                            pe.wait_ge(gu_ready, b * NH + e - 1)
                        pe.wait_ge(wlo_ready, b * NH + e + 1)
                        for first, bk in ((0, GB), (KD, UB)):
                            for k in range(KD):
                                hi, lo = w_hi[:, e % 2, first + k, :], w_lo[:, e % 2, first + k, :]
                                mm(bk[e % 2], hi, x_hi[:, k, chunk], start=(k == 0), stop=False)
                                mm(bk[e % 2], hi, x_lo[:, k, chunk], start=False, stop=False)
                                last = mm(bk[e % 2], lo, x_hi[:, k, chunk], start=False, stop=(k == KD - 1))
                        if e < K:
                            if e >= 2:
                                pe.wait_ge(t2_ready, b * K + e - 1)
                            last = mm(CB[e % 2], mixb[:, e, :], coT[:, chunk], start=True, stop=True)
                        last.then_inc(h_ps, 1)
                    pe.wait_ge(gu_ready, b * NH + NH)
                    pe.wait_ge(acc_ready, b * (K - 1) + K - 1)
                    pe.wait_ge(z_ready, b + 1)
                    for t in range(CH):
                        for m in range(SH):
                            mm(Y[:, t, :], hs[:, m, t * P:(t + 1) * P], w["sdown"][:, m, :], start=(m == 0), stop=False)
                        last = mm(Y[:, t, :], acc[:, t * P:(t + 1) * P], w["down"], start=False, stop=True)
                    last.then_inc(y_ps, 1)

            @block.scalar
            def _(act):
                for j in range(NCH):
                    nc.scalar.activation(x_hi[:, :, j * CN:(j + 1) * CN], xT[:, :, j * CN:(j + 1) * CN], ACT.Copy).then_inc(xhi_ready, 1)

                def weights_hi(e):
                    nc.scalar.activation(w_hi[:, e % 2, :, :], w["all"][:, e, :].rearrange("p (k n) -> p k n", n=P), ACT.Copy).then_inc(whi_ready, 1)

                for t in range(NT):
                    if t % 4 == 0:
                        act.wait_ge(nm_ready, t // 4 + 1)
                    last = nc.scalar.activation(pb[:, t, 0:E], LOGITS[:, t, :], ACT.Exp, bias=nm[:, t:t + 1], accum_out=sums[:, t:t + 1])
                last.then_inc(ex_ready, 1)
                nc.scalar.preload_act_table(ACT.Silu)
                w["late"](act)
                weights_hi(0)
                weights_hi(1)
                with act.Fori(0, NCH) as b:
                    for e in range(NH):
                        act.wait_ge(h_ps, b * NH + e + 1)
                        if e >= 2:
                            act.wait_ge(gu_ready, b * NH + e - 1)
                        nc.scalar.activation(sg[:, e % 2, :], GB[e % 2], ACT.Silu).then_inc(sg_ready, 1)
                        weights_hi((e + 2) % NH)

            @block.gpsimd
            def _(pool):
                with pool.Fori(0, NCH) as b:
                    for k in range(1, K):
                        pool.wait_ge(t2_ready, b * K + k + 1)
                        if k == 1:
                            pool.wait_ge(y_ps, b + 1)
                        else:
                            pool.wait_ge(acc_ready, b * (K - 1) + k - 1)
                        nc.gpsimd.tensor_tensor(acc[:, :], t2[:, 0, :] if k == 1 else acc[:, :], t2[:, k % 2, :], ALU.add).then_inc(acc_ready, 1)

            @block.vector
            def _(dve):
                w["early"](dve)
                dve.sem_inc(y_ps, 1)
                one = lambda ins, n: (ins.then_inc(route_steps, 1), dve.wait_ge(route_steps, n))
                one(nc.vector.tensor_tensor(mp[:, :, :], w["amp"], w["amp"], ALU.mult), 1)
                one(nc.vector.tensor_tensor(mix[:, :], mp[:, :, 0], mp[:, :, 1], ALU.add), 2)
                one(nc.vector.tensor_reduce(msum[:, :], mix[:, :], AX.X, ALU.add), 3)
                one(nc.vector.tensor_scalar(msum[:, :], msum[:, :], EPS, None, ALU.add), 4)
                one(nc.vector.reciprocal(msum[:, :], msum[:, :]), 5)
                one(nc.vector.tensor_scalar(mix[:, :], mix[:, :], msum[:, :], w["escale"], ALU.mult, ALU.mult), 6)
                nc.vector.tensor_copy(mixb[:, :, :], bc(mix[:, :], 2, I)).then_inc(mix_ready, 1)
                nc.vector.memset(pb[:, :, E:], BIG)
                nc.vector.memset(pick[:, :, :], BIG)
                st = Steps(dve, route_steps, 0)
                st.begin(0)
                st.k = 6
                for j in range(NT // 4):
                    dve.wait_ge(logit_ps, j + 1)
                    nc.vector.tensor_reduce(nm[:, 4 * j:4 * j + 4], LOGITS[:, 4 * j:4 * j + 4, :], AX.X, ALU.max, negate=True).then_inc(nm_ready, 1)
                for j in range(NCH):
                    cols = slice(j * CN, (j + 1) * CN)
                    dve.wait_ge(xhi_ready, j + 1)
                    nc.vector.tensor_tensor(x_lo[:, :, cols], xT[:, :, cols], x_hi[:, :, cols].bitcast(F32), ALU.subtract).then_inc(xlo_ready, 1)
                dve.wait_ge(ex_ready, 1)
                st.do(nc.vector.reciprocal(wsum[:, :], sums[:, :]))
                st.do(nc.vector.tensor_tensor(pb[:, :, 0:E], pb[:, :, 0:E], bc(wsum[:, :], 2, E), ALU.mult))
                for t in range(NT):
                    last = nc.vector.max(top[:, t, :], pb[:, t, 0:E])
                st.do(last)
                st.do(nc.vector.tensor_copy(pick[:, :, 0:TOP], top[:, :, 0:TOP]))
                for t in range(NT):
                    last = nc.vector.match_replace(left[:, t, :], pick[:, t, :], pb[:, t, :], -BIG)
                st.do(last)
                st.do(nc.vector.scalar_tensor_tensor(co[:, :, :], left[:, :, 0:E], -BIG, pb[:, :, 0:E], ALU.is_equal, ALU.mult))
                st.do(nc.vector.tensor_reduce(wsum[:, :], co[:, :, :], AX.X, ALU.add))
                st.do(nc.vector.tensor_scalar(wsum[:, :], wsum[:, :], EPS, None, ALU.add))
                st.do(nc.vector.reciprocal(wsum[:, :], wsum[:, :]))
                nc.vector.tensor_tensor(co[:, :, :], co[:, :, :], bc(wsum[:, :], 2, E), ALU.mult).then_inc(co_ready, 1)
                dve.wait_ge(coT_ps, 1)
                nc.vector.tensor_copy(coT[:, :].rearrange("p (a n) -> p a n", a=4), psum[:, 4:8, :]).then_inc(coT_ready, 1)
                dve.sem_inc(z_ready, 1)

                def weights_lo(e, count):
                    dve.wait_ge(whi_ready, count + 1)
                    nc.vector.tensor_tensor(w_lo[:, e % 2, :, :], w["all"][:, e, :].rearrange("p (k n) -> p k n", n=P),
                                            w_hi[:, e % 2, :, :].bitcast(F32), ALU.subtract).then_inc(wlo_ready, 1)

                w["late"](dve)
                weights_lo(0, 0)
                weights_lo(1, 1)
                st = Steps(dve, steps, LN_STEPS)
                with dve.Fori(0, NCH) as b:
                    st.begin(b)

                    def weigh(k):
                        dve.wait_ge(gu_ready, b * NH + k + 1)
                        if k >= 2:
                            dve.wait_ge(acc_ready, b * (K - 1) + max(k - 2, 1))
                        nc.vector.tensor_tensor(t2[:, k % 2, :], gu[:, k % 2, :], CB[k % 2], ALU.mult).then_inc(t2_ready, 1)

                    for e in range(NH):
                        dve.wait_ge(sg_ready, b * NH + e + 1)
                        dst = gu[:, e % 2, :] if e < K else hs[:, e - K, :]
                        nc.vector.tensor_tensor(dst, sg[:, e % 2, :], UB[e % 2], ALU.mult).then_inc(gu_ready, 1)
                        if 1 <= e <= K:
                            weigh(e - 1)
                        weights_lo((e + 2) % NH, b * NH + e + 2)
                    dve.wait_ge(y_ps, b + 2)
                    add_and_measure(nc, st, x_sb, mv, b * CH, CH, Y, lw, z_ready, b + 2)
                    st.end()



def l2_mixing(nc, c, x_sb, mv, xT, w, psum):
    R, DH = 256, 64
    with ExitStack() as ctx:
        sb = lambda name, shape, dt=F32: ctx.enter_context(nc.sbuf_tensor("l2a_" + name, shape, dt))
        sem = lambda name: ctx.enter_context(nc.semaphore("l2a_" + name))
        hT = sb("hT", [DH, 2, T])
        ga = sb("ga", [P, 2, 2, T])
        ug = sb("ug", [P, 2, 2, T])
        vg = sb("vg", [P, 2, 2, T])
        cum = sb("cum", [P, 2, 2, T])
        go = sb("go", [P, 2, 2, T])
        tc = sb("tc", [P, 2, KD, T])
        ones = sb("ones", [P, T])
        lw = ln_scratch(sb, TT)
        bank = lambda i: psum[:, i, :]
        two = lambda ap: ap.rearrange("p (k t) -> p k t", k=2)
        HY, U, V, GG = [bank(0), bank(1)], [bank(2), bank(3)], [bank(4), bank(5)], [bank(6), bank(7)]

        h_ps = sem("h_ps")
        h_ready = sem("h_ready")
        uv_ps = sem("uv_ps")
        g_ps = sem("g_ps")
        ga_ready = sem("ga_ready")
        mix_ready = sem("mix_ready")
        y_ps = sem("y_ps")
        z_ready = sem("z_ready")
        steps = sem("steps")

        with nc.Block() as block:
            @block.tensor
            def _(pe):
                mm = nc.tensor.matmul
                w["early"](pe)
                w["late"](pe)
                pe.sem_inc(z_ready, 2)
                with pe.Fori(0, B // 2) as b:
                    for i in range(2):
                        x = lambda k: xT[:, k, bass.ds(b * 2 * T + i * T, T)]
                        pe.wait_ge(z_ready, 2 * b + i + 1)
                        for k in range(KD):
                            last = mm(HY[i][0:DH, 0:T], w["g1"][:, k, :], x(k), start=(k == 0), stop=(k == KD - 1))
                        last.then_inc(h_ps, 1)
                        for name, bk in (("u", U), ("v", V)):
                            for m in range(2):
                                for k in range(KD):
                                    last = mm(bk[i][:, m * T:(m + 1) * T], w[name][:, k, m * P:(m + 1) * P], x(k),
                                              start=(k == 0), stop=(k == KD - 1))
                        last.then_inc(uv_ps, 1)
                        pe.wait_ge(h_ready, 2 * b + i + 1)
                        for m in range(2):
                            last = mm(GG[i][:, m * T:(m + 1) * T], w["g2"][0:DH, m * P:(m + 1) * P], hT[:, i, :], start=True, stop=True)
                        last.then_inc(g_ps, 1)
                    for i in range(2):
                        pe.wait_ge(mix_ready, 2 * b + i + 1)
                        for t in range(TT):
                            y = HY[i][:, t * D:(t + 1) * D]
                            for k in range(2):
                                mm(y, go[:, i, k, t * P:(t + 1) * P], w["u"][:, k, :], start=(k == 0), stop=False)
                            for k in range(KD):
                                last = mm(y[:, k * P:(k + 1) * P], tc[:, i, k, t * P:(t + 1) * P], c["id"], start=False, stop=(k == KD - 1))
                        last.then_inc(y_ps, 1)

            @block.scalar
            def _(act):
                nc.scalar.preload_act_table(ACT.Sigmoid)
                w["late"](act)
                with act.Fori(0, B // 2) as b:
                    for i in range(2):
                        act.wait_ge(h_ps, 2 * b + i + 1)
                        nc.scalar.activation(hT[:, i, :], HY[i][0:DH, 0:T], ACT.Relu, bias=w["bg1"][0:DH, :]).then_inc(h_ready, 1)
                        act.wait_ge(g_ps, 2 * b + i + 1)
                        for m in range(2):
                            last = nc.scalar.activation(ga[:, i, m, :], GG[i][:, m * T:(m + 1) * T], ACT.Sigmoid, bias=w["bg2"][:, m:m + 1])
                        last.then_inc(ga_ready, 1)

            @block.vector
            def _(dve):
                st = Steps(dve, steps, L2A_STEPS)
                nc.vector.memset(ones[:, :], 1.0)
                w["early"](dve)
                w["late"](dve)
                with dve.Fori(0, B // 2) as b:
                    st.begin(b)
                    for i in range(2):
                        dve.wait_ge(h_ps, 2 * b + i + 1)
                        x = lambda k, at, n: xT[:, k, bass.ds(b * 2 * T + i * T + at, n)]
                        for k in range(KD):
                            last = nc.vector.tensor_scalar(tc[:, i, k, :], x(k, 0, T), w["conv"][:, k, 1:2], w["convb"][:, k:k + 1], ALU.mult, ALU.add)
                        st.do(last)
                        for k in range(KD):
                            last = nc.vector.scalar_tensor_tensor(tc[:, i, k, 1:T], x(k, 0, T - 1), w["conv"][:, k, 0:1], tc[:, i, k, 1:T], ALU.mult, ALU.add)
                        st.do(last)
                        for k in range(KD):
                            last = nc.vector.scalar_tensor_tensor(tc[:, i, k, 0:T - 1], x(k, 1, T - 1), w["conv"][:, k, 2:3], tc[:, i, k, 0:T - 1], ALU.mult, ALU.add)
                        st.do(last)
                        dve.wait_ge(uv_ps, 2 * b + i + 1)
                        dve.wait_ge(ga_ready, 2 * b + i + 1)
                        for m in range(2):
                            nc.vector.scalar_tensor_tensor(ug[:, i, m, :], U[i][:, m * T:(m + 1) * T], w["bu"][:, m:m + 1], ga[:, i, m, :], ALU.add, ALU.mult)
                            last = nc.vector.scalar_tensor_tensor(vg[:, i, m, :], V[i][:, m * T:(m + 1) * T], w["bv"][:, m:m + 1], ga[:, i, m, :], ALU.add, ALU.mult)
                        st.do(last)
                        for m in range(2):
                            last = nc.vector.tensor_tensor_scan(cum[:, i, m, :], ones[:, :], ug[:, i, m, :], 0.0, ALU.mult, ALU.add)
                        st.do(last)
                        nc.vector.tensor_tensor(go[:, i, :, :], cum[:, i, :, :], vg[:, i, :, :], ALU.mult).then_inc(mix_ready, 1)
                    for i in range(2):
                        dve.wait_ge(y_ps, 2 * b + i + 1)
                        add_and_measure(nc, st, x_sb, mv, b * 2 * TT + i * TT, TT, two(HY[i]), lw, z_ready, 2 * b + i + 3)
                    st.end()


L2A_STEPS = 2 * (5 + LN_STEPS)



def l2_ffn(nc, c, x_sb, mv, xT, w, psum):
    I, SETS = 1024, 2
    NH = I // P
    with ExitStack() as ctx:
        sb = lambda name, shape, dt=F32: ctx.enter_context(nc.sbuf_tensor("l2f_" + name, shape, dt))
        sem = lambda name: ctx.enter_context(nc.semaphore("l2f_" + name))
        x_hi = sb("x_hi", [P, KD, TOK], F32R)
        x_lo = xT[:, :, :].bitcast(F32R)
        w_hi = sb("w_hi", [P, 2, 2 * KD, P], F32R)
        w_lo = sb("w_lo", [P, 2, 2 * KD, P], F32R)
        sg = sb("sg", [P, 2, CN])
        hh = sb("hh", [P, SETS, 2, 2, CN])
        ab = sb("ab", [P, 2, 2, CN])
        big = sb("big", [P, 2, CN])
        small = sb("small", [P, 2, CN])
        win = sb("win", [P, 2, 2, CN], BF16)
        both = sb("both", [P, 3, CN], BF16)
        lw = ln_scratch(sb, CH)
        bank = lambda i: psum[:, i, :]
        Y = psum[:, 6:8, :].rearrange("p a (t n) -> p (a t) n", t=2)

        h_ps = sem("h_ps")
        sg_ready = sem("sg_ready")
        hh_ready = sem("hh_ready")
        ab_ready = sem("ab_ready")
        kept = sem("kept")
        y_ps = sem("y_ps")
        xhi_ready, xlo_ready, whi_ready, wlo_ready = c["split_sems"]
        X0, W0 = NCH, 2 + NCH * 10
        z_ready = sem("z_ready")
        steps = sem("steps")

        with nc.Block() as block:
            @block.tensor
            def _(pe):
                mm = nc.tensor.matmul

                def clear_output():
                    for a in (6, 7):
                        mm(bank(a), c["zero"], c["finite"], start=True, stop=False)

                w["early"](pe)
                pe.sem_inc(z_ready, 1)
                w["late"](pe)
                with pe.Fori(0, NCH) as b:
                    pe.wait_ge(xlo_ready, b + 1 + X0)
                    for e in range(NH):
                        if e >= 2:
                            pe.wait_ge(hh_ready, b * NH + e - 1)
                        pe.wait_ge(wlo_ready, b * NH + e + 1 + W0)
                        chunk = bass.ds(b * CN, CN)
                        for first, bk in ((0, 0), (KD, 2)):
                            for k in range(KD):
                                hi, lo = w_hi[:, e % 2, first + k, :], w_lo[:, e % 2, first + k, :]
                                mm(bank(bk + e % 2), hi, x_hi[:, k, chunk], start=(k == 0), stop=False)
                                mm(bank(bk + e % 2), hi, x_lo[:, k, chunk], start=False, stop=False)
                                last = mm(bank(bk + e % 2), lo, x_hi[:, k, chunk], start=False, stop=(k == KD - 1))
                        last.then_inc(h_ps, 1)
                    pe.wait_ge(z_ready, b + 1)
                    clear_output()
                    for s in range(SETS):
                        pe.wait_ge(kept, b * SETS + s + 2)
                        for t in range(CH):
                            for e in range(4 * s, 4 * s + 4):
                                last = mm(Y[:, t, :], hh[:, s, e % 4 // 2, e % 2, t * P:(t + 1) * P], w["down"][:, e, :],
                                          start=False, stop=(e == NH - 1 and t % 2 == 1))
                    last.then_inc(y_ps, 1)

            @block.scalar
            def _(act):
                nc.scalar.preload_act_table(ACT.Silu)
                for j in range(NCH):
                    nc.scalar.activation(x_hi[:, :, j * CN:(j + 1) * CN], xT[:, :, j * CN:(j + 1) * CN], ACT.Copy).then_inc(xhi_ready, 1)

                def weights_hi(e):
                    nc.scalar.activation(w_hi[:, e % 2, :, :], w["all"][:, e, :].rearrange("p (k n) -> p k n", n=P), ACT.Copy).then_inc(whi_ready, 1)

                w["late"](act)
                weights_hi(0)
                weights_hi(1)
                with act.Fori(0, NCH) as b:
                    def magnitudes(s):
                        act.wait_ge(hh_ready, b * NH + 4 * s + 4)
                        act.wait_ge(kept, b * SETS + s + 1)
                        nc.scalar.activation(ab[:, :, :, :], hh[:, s, :, :, :], ACT.Abs).then_inc(ab_ready, 1)

                    for e in range(NH):
                        act.wait_ge(h_ps, b * NH + e + 1)
                        if e >= 2:
                            act.wait_ge(hh_ready, b * NH + e - 1)
                        nc.scalar.activation(sg[:, e % 2, :], bank(e % 2), ACT.Silu).then_inc(sg_ready, 1)
                        weights_hi((e + 2) % NH)
                        if e == 4:
                            magnitudes(0)
                    magnitudes(1)

            @block.vector
            def _(dve):
                st = Steps(dve, steps, L2F_STEPS)
                dve.sem_inc(kept, 1)
                for j in range(NCH):
                    cols = slice(j * CN, (j + 1) * CN)
                    dve.wait_ge(xhi_ready, j + 1 + X0)
                    nc.vector.tensor_tensor(x_lo[:, :, cols], xT[:, :, cols], x_hi[:, :, cols].bitcast(F32), ALU.subtract).then_inc(xlo_ready, 1)
                def weights_lo(e, count):
                    dve.wait_ge(whi_ready, count + 1 + W0)
                    nc.vector.tensor_tensor(w_lo[:, e % 2, :, :], w["all"][:, e, :].rearrange("p (k n) -> p k n", n=P),
                                            w_hi[:, e % 2, :, :].bitcast(F32), ALU.subtract).then_inc(wlo_ready, 1)

                w["late"](dve)
                weights_lo(0, 0)
                weights_lo(1, 1)
                with dve.Fori(0, NCH) as b:
                    st.begin(b)

                    def prune(s):
                        a0, a1 = ab[:, :, 0, :], ab[:, :, 1, :]
                        dve.wait_ge(ab_ready, b * SETS + s + 1)
                        nc.vector.tensor_tensor(win[:, :, 0, :], a0, a1, ALU.is_ge)
                        nc.vector.tensor_tensor(big[:, :, :], a0, a1, ALU.max)
                        st.do(nc.vector.tensor_tensor(small[:, :, :], a0, a1, ALU.min))
                        nc.vector.tensor_scalar(win[:, :, 1, :], win[:, :, 0, :], -1.0, 1.0, ALU.mult, ALU.add)
                        nc.vector.tensor_tensor(both[:, 0, :], small[:, 0, :], big[:, 1, :], ALU.is_ge)
                        st.do(nc.vector.tensor_tensor(both[:, 1, :], small[:, 1, :], big[:, 0, :], ALU.is_gt))
                        st.do(nc.vector.tensor_copy(both[:, 2, :], both[:, 0, :]))
                        for q in range(2):
                            last = nc.vector.tensor_tensor(win[:, q, :, :], win[:, q, :, :], bc(both[:, q + 1, :], 1, 2), ALU.subtract)
                        st.do(last)
                        for q in range(2):
                            last = nc.vector.tensor_tensor(win[:, q, :, :], win[:, q, :, :], bc(both[:, q, :], 1, 2), ALU.max)
                        st.do(last)
                        nc.vector.tensor_tensor(hh[:, s, :, :, :], hh[:, s, :, :, :], win[:, :, :, :], ALU.mult).then_inc(kept, 1)

                    for e in range(NH):
                        dve.wait_ge(sg_ready, b * NH + e + 1)
                        nc.vector.tensor_tensor(hh[:, e // 4, e % 4 // 2, e % 2, :], sg[:, e % 2, :], bank(2 + e % 2), ALU.mult).then_inc(hh_ready, 1)
                        weights_lo((e + 2) % NH, b * NH + e + 2)
                        if e == 5:
                            prune(0)
                    prune(1)
                    dve.wait_ge(y_ps, b + 1)
                    add_and_measure(nc, st, x_sb, mv, b * CH, CH, Y, lw, z_ready, b + 2)
                    st.end()


L2F_STEPS = 2 * 5 + LN_STEPS



def l3_attention(nc, c, x_sb, mv, xT, w, psum):
    HD, G, R, A = 16, 4, 4, 2
    H = G * R
    V1 = HD + 1
    LAM_INIT = 0.8 - 0.6 * float(np.exp(-0.3 * 0))
    EPS = 1e-8
    NG = H // 2
    with ExitStack() as ctx:
        sb = lambda name, shape, dt=F32: ctx.enter_context(nc.sbuf_tensor("l3a_" + name, shape, dt))
        sem = lambda name: ctx.enter_context(nc.semaphore("l3a_" + name))
        q_all = sb("q_all", [P, A, R, TOK])
        qr = sb("qr", [P, A, R, T])
        kr = sb("kr", [P, G, A, T])
        va = sb("va", [P, NT, G, V1])
        lam = sb("lam", [P, 2, H])
        lprod = sb("lprod", [P, 2, H, HD])
        nlam = sb("nlam", [P, H])
        gain = sb("gain", [P, HD])
        nm = sb("nm", [P, 2, TT, A])
        sums = sb("sums", [P, 2, A, 2, TT])
        rec = sb("rec", [P, 4, A, 2, TT])
        ratio = sb("ratio", [P, 2, 2, TT])
        pr_space = sb("pr", [P, 2 * A * 2 * 3 * P])
        pr = pr_space[:, :].rearrange("p (i a j k) -> p i a j k", i=2, a=A, j=2)
        k1 = pr_space[:, 0:A * 2 * CN].rearrange("p (a m t) -> p a m t", a=A, m=2)
        dif = sb("dif", [P, 4, 2, 3 * P])
        nm2 = sb("nm2", [P, 4, 2, TT])
        nb2 = sb("nb2", [P, 4, 2, TT])
        p2 = sb("p2", [P, 2, 2, 3 * P])
        pt = sb("pt", [P, 2, 2, 3 * P])
        recs = sb("recs", [P, TT, H])
        on = sb("on", [P, TT, D])
        osq = sb("osq", [P, TT, D])
        vv = sb("vv", [P, TT * H])
        rs = sb("rs", [P, TT * H])
        tmp = sb("tmp", [P, TT * H])
        oT = sb("oT", [P, KD, T])
        lw = ln_scratch(sb, TT)
        rope_k = w["rope_k"].rearrange("p (a m t) -> p a m t", a=A, m=2)
        S = [psum[:, 0:2, :], psum[:, 2:4, :]]
        PT = [psum[:, 4, :], psum[:, 5, :]]
        k_all = xT
        O = psum[:, 6:8, 0:H * V1].rearrange("p t (h e) -> p t h e", e=V1)

        proj_ps = sem("proj_ps")
        proj_out = sem("proj_out")
        k_rotated = sem("k_rotated")
        q_staged = [sem("q_staged%d" % r) for r in range(R)]
        k_spread = sem("k_spread")
        lam_ready = sem("lam_ready")
        s_ps = sem("s_ps")
        nm_ready = sem("nm_ready")
        p_exp = sem("p_exp")
        nb_ready = sem("nb_ready")
        p_ready = sem("p_ready")
        pt_ps = sem("pt_ps")
        pt_ready = sem("pt_ready")
        av_ps = sem("av_ps")
        dif_ready = sem("dif_ready")
        dif_masked = sem("dif_masked")
        on_raw = sem("on_raw")
        on_ready = sem("on_ready")
        oT_ps = sem("oT_ps")
        oT_ready = sem("oT_ready")
        y_ps = sem("y_ps")
        z_ready = sem("z_ready")
        set_up = sem("set_up")
        steps = sem("steps")

        NP = A * R + A * 2 + 1

        with nc.Block() as block:
            @block.sync
            def _(sp):
                sp.wait_ge(proj_out, NCH * NP)
                for r in range(R):
                    sp.dma_start(qr[:, :, r, :], q_all[:, :, r, 0:T]).then_inc(q_staged[r], 16)
                with sp.Fori(0, B - 1) as b:
                    for r in range(R):
                        sp.wait_ge(s_ps, b * H + 4 * r + 4)
                        sp.dma_start(qr[:, :, r, :], q_all[:, :, r, bass.ds(b * T + T, T)]).then_inc(q_staged[r], 16)

            @block.tensor
            def _(pe):
                mm = nc.tensor.matmul

                def project(j):
                    chunk = slice(j * CN, (j + 1) * CN)
                    for i in range(NP):
                        n = j * NP + i
                        if n >= 8:
                            pe.wait_ge(proj_out, n - 7)
                        for k in range(KD):
                            if i < A * R:
                                last = mm(psum[:, n % 8, :], w["q"][:, k, i * P:(i + 1) * P], xT[:, k, chunk], start=(k == 0), stop=(k == KD - 1))
                            elif i < NP - 1:
                                m = i - A * R
                                last = mm(psum[:, n % 8, :], w["k"][:, k, m * P:(m + 1) * P], xT[:, k, chunk], start=(k == 0), stop=(k == KD - 1))
                        if i == NP - 1:
                            for t in range(CH):
                                for k in range(KD):
                                    last = mm(psum[:, n % 8, t * G * HD:(t + 1) * G * HD], xT[:, k, (j * CH + t) * P:(j * CH + t + 1) * P],
                                              w["v"][:, k, :], start=(k == 0), stop=(k == KD - 1))
                        last.then_inc(proj_ps, 1)

                def scores(b, n):
                    r, g = n // G, n % G
                    if g == 0:
                        pe.wait_ge(q_staged[r], b * 16 + 16)
                    if n < 4:
                        pe.wait_ge(k_spread, b * 4 + g + 1)
                    pe.wait_ge(p_exp, b * H + n + 1)
                    for a in range(A):
                        for t in range(TT):
                            mm(S[n % 2][:, a, t * P:t * P + (t + 1) * P], qr[:, a, r, t * P:(t + 1) * P],
                               kr[:, g, a, 0:(t + 1) * P], start=True, stop=False)
                            last = mm(S[n % 2][:, a, 2 * t * P:(2 * t + 1) * P], c["idb"], c["maskb"], start=False, stop=True)
                    last.then_inc(s_ps, 1)

                def turn(b, m, before=(None, None)):
                    pe.wait_ge(p_ready, b * NG + m + 1)
                    for j in range(2):
                        pe.wait_ge(pt_ready, b * H + 2 * m + j + 1)
                        if before[j] is not None:
                            pe.wait_ge(before[j], b)
                        for i in range(3):
                            last = nc.tensor.transpose(PT[j][:, i * P:(i + 1) * P], p2[:, m % 2, j, i * P:(i + 1) * P], c["id"])
                        last.then_inc(pt_ps, 1)

                def values(b, m):
                    if m == 0:
                        pe.wait_ge(on_raw, b + 1)
                    for j in range(2):
                        pe.wait_ge(pt_ready, b * H + 2 * m + j + 3)
                        n = 2 * (m % NG) + j
                        r, g = n // G, n % G
                        h = 4 * g + r
                        pp = pt[:, m % 2, j, :]
                        v = lambda t: va[:, bass.ds((b + m // NG) * TT + t, 1), g, :].rearrange("p o e -> p (o e)")
                        mm(O[:, 0, h, :], pp[:, 0:P], v(0), start=True, stop=True)
                        mm(O[:, 1, h, :], pp[:, P:2 * P], v(0), start=True, stop=False)
                        last = mm(O[:, 1, h, :], pp[:, 2 * P:3 * P], v(1), start=False, stop=True)
                    last.then_inc(av_ps, 1)

                def turn_output(b):
                    pe.wait_ge(on_ready, b + 1)
                    for h in range(KD):
                        for t in range(TT):
                            last = nc.tensor.transpose(PT[0][:, (h * TT + t) * P:(h * TT + t + 1) * P],
                                                       on[:, t, h * P:(h + 1) * P], c["id"])
                    last.then_inc(oT_ps, 1)

                def project_output(b):
                    pe.wait_ge(oT_ready, b + 1)
                    for t in range(TT):
                        for k in range(KD):
                            last = mm(PT[1][:, t * D:(t + 1) * D], oT[:, k, t * P:(t + 1) * P], w["o"][:, k, :],
                                      start=(k == 0), stop=(k == KD - 1))
                    last.then_inc(y_ps, 1)

                def sequence(b, first):
                    for m in range(NG):
                        scores(b, 2 * m)
                        before = (None, None)
                        if m == 6 and not first:
                            pe.wait_ge(pt_ready, b * H + 2 * (m - 3) + 1)
                            turn_output(b - 1)
                            before = (oT_ready, None)
                        if m == 7 and not first:
                            pe.wait_ge(pt_ready, b * H + 2 * (m - 3) + 2)
                            project_output(b - 1)
                            before = (None, z_ready)
                        scores(b, 2 * m + 1)
                        if not first or m >= 3:
                            turn(b, m - 3, before)
                        if not first or m >= 4:
                            values(b, m - 4)

                w["early"](pe)
                for j in range(NCH):
                    project(j)
                w["late"](pe)
                pe.wait_ge(proj_out, NCH * NP)
                sequence(0, True)
                with pe.Fori(0, B - 1) as b:
                    sequence(b + 1, False)
                for m in range(3):
                    turn(B, m - 3)
                    values(B, m - 4)
                values(B, -1)
                turn_output(B - 1)
                project_output(B - 1)

            @block.gpsimd
            def _(pool):
                with pool.Fori(0, B) as b:
                    for m in range(NG):
                        diagonal = dif[:, m % 4, :, :].rearrange("p j (c k) -> p j c k", c=3)[:, :, 0:3:2, :]
                        pool.wait_ge(dif_ready, b * NG + m + 1)
                        nc.gpsimd.tensor_tensor(diagonal, diagonal, bc(bc(w["mask"], 1, 2), 1, 2), ALU.add).then_inc(dif_masked, 1)

            @block.scalar
            def _(act):
                nc.scalar.preload_act_table(ACT.Exp)
                act.wait_ge(set_up, 2)
                nc.scalar.activation(lam[:, :, :], lam[:, :, :], ACT.Exp).then_inc(lam_ready, 1)
                act.sem_inc(p_exp, 2)
                act.sem_inc(pt_ready, 2)

                def exponentials(b, n, opening):
                    m, j = n // 2, n % 2
                    act.wait_ge(nm_ready, b * H + n + 1)
                    if not (opening and m < 2):
                        act.wait_ge(dif_ready, b * NG + m - 1)
                    for a in range(A):
                        for t in range(TT):
                            s = slice(t * P, t * P + (t + 1) * P)
                            last = nc.scalar.activation(pr[:, m % 2, a, j, s], S[j][:, a, s], ACT.Exp, bias=nm[:, j, t, a:a + 1],
                                                        accum_out=sums[:, m % 2, a, j, t:t + 1])
                    last.then_inc(p_exp, 1)

                def second(b, m, opening=False):
                    act.wait_ge(nb_ready, b * NG + m + 1)
                    if not (opening and m < 2):
                        act.wait_ge(pt_ps, b * H + 2 * m - 2)
                    for j in range(2):
                        for t in range(TT):
                            s = slice(t * P, t * P + (t + 1) * P)
                            last = nc.scalar.activation(p2[:, m % 2, j, s], dif[:, m % 4, j, s], ACT.Exp, bias=nb2[:, m % 4, j, t:t + 1],
                                                        scale=rec[:, m % 4, 0, j, t:t + 1])
                    last.then_inc(p_ready, 1)

                def out_of_psum(b, m, opening=False):
                    for j in range(2):
                        act.wait_ge(pt_ps, b * H + 2 * m + j + 1)
                        if not (opening and m < 2):
                            act.wait_ge(av_ps, b * NG + m - 1)
                        nc.scalar.activation(pt[:, m % 2, j, :], PT[j][:, 0:3 * P], ACT.Copy).then_inc(pt_ready, 1)

                def output(b):
                    act.wait_ge(oT_ps, b + 1)
                    nc.scalar.activation(oT[:, :, :], PT[0].rearrange("p (k t) -> p k t", k=KD), ACT.Copy).then_inc(oT_ready, 1)

                def sequence(b, opening):
                    for m in range(NG):
                        exponentials(b, 2 * m, opening)
                        if m == 6 and not opening:
                            output(b - 1)
                        exponentials(b, 2 * m + 1, opening)
                        if not opening or m >= 2:
                            second(b, m - 2, opening)
                        if not opening or m >= 3:
                            out_of_psum(b, m - 3, opening)

                sequence(0, True)
                with act.Fori(0, B - 1) as b:
                    sequence(b + 1, False)
                second(B, -2)
                out_of_psum(B, -3)
                second(B, -1)
                out_of_psum(B, -2)
                out_of_psum(B, -1)
                output(B - 1)

            @block.vector
            def _(dve):
                st = Steps(dve, steps, L3A_STEPS)
                w["early"](dve)
                w["late"](dve)
                for j in range(2):
                    last = nc.vector.tensor_tensor(lprod[:, j, :, :], w["lq%d" % (j + 1)], w["lk%d" % (j + 1)], ALU.mult)
                last.then_inc(set_up, 1)
                dve.wait_ge(set_up, 1)
                nc.vector.tensor_reduce(lam[:, :, :], lprod[:, :, :, :], AX.X, ALU.add).then_inc(set_up, 1)
                dve.wait_ge(lam_ready, 1)
                nc.vector.tensor_tensor(nlam[:, :], lam[:, 1, :], lam[:, 0, :], ALU.subtract).then_inc(set_up, 1)
                dve.wait_ge(set_up, 3)
                nc.vector.tensor_scalar(nlam[:, :], nlam[:, :], -LAM_INIT, None, ALU.add).then_inc(set_up, 1)
                nc.vector.tensor_scalar(gain[:, :], w["rms"], 1.0 - LAM_INIT, None, ALU.mult).then_inc(set_up, 1)
                nc.vector.memset(va[:, :, :, HD:V1], 1.0)
                nc.vector.memset(kr[:, :, :, :], 0.0).then_inc(set_up, 1)
                dve.wait_ge(set_up, 6)
                dve.sem_inc(on_raw, 1)

                def rotate(j):
                    chunk = slice(j * CN, (j + 1) * CN)
                    two = lambda ap: ap.rearrange("p (s t) -> p s t", s=2)
                    for i in range(NP):
                        n = j * NP + i
                        dve.wait_ge(proj_ps, n + 1)
                        if i < A * R:
                            a, r = i // R, i % R
                            ins = nc.vector.tensor_tensor(two(q_all[:, a, r, chunk]), two(psum[:, n % 8, :]), bc(w["rope_q"][:, a, :], 1, 2), ALU.mult)
                        elif i < NP - 1:
                            a, m = (i - A * R) // 2, (i - A * R) % 2
                            if j > 0:
                                dve.wait_ge(k_rotated, j)
                            ins = nc.vector.tensor_tensor(two(k1[:, a, m, :]), two(psum[:, n % 8, :]), bc(rope_k[:, a, m, :], 1, 2), ALU.mult)
                        else:
                            ins = nc.vector.tensor_copy(va[:, j * CH:(j + 1) * CH, :, 0:HD],
                                                        psum[:, n % 8, 0:CH * G * HD].rearrange("p (t g e) -> p t g e", t=CH, g=G))
                        ins.then_inc(proj_out, 1)
                    dve.wait_ge(proj_out, j * NP + NP)
                    nc.vector.tensor_tensor(k_all[:, :, chunk], k1[:, :, 0, :], k1[:, :, 1, :], ALU.add).then_inc(k_rotated, 1)

                def spread_keys(b):
                    for g in range(G):
                        rows = slice(32 * g, 32 * g + 32)
                        nc.vector.tensor_copy(kr[rows, g, :, :], k_all[rows, :, bass.ds(b * T, T)]).then_inc(k_spread, 1)

                def maxima(b, n):
                    dve.wait_ge(s_ps, b * H + n + 1)
                    dve.wait_ge(p_exp, b * H + n + 1)
                    for t in range(TT):
                        last = nc.vector.tensor_reduce(nm[:, n % 2, t, :], S[n % 2][:, :, t * P:t * P + (t + 1) * P],
                                                       AX.X, ALU.max, negate=True)
                    last.then_inc(nm_ready, 1)

                def difference(b, m, opening, between, with_output=False, with_keys=False):
                    i, i4 = m % 2, m % 4
                    dve.wait_ge(p_exp, b * H + 2 * m + 4)
                    if not (opening and m < 4):
                        dve.wait_ge(p_ready, b * NG + m - 3)
                    reciprocals = st.inc(nc.vector.reciprocal(rec[:, i4, :, :, :], sums[:, i, :, :, :]))
                    if between is not None:
                        maxima(b, between)
                    st.wait(reciprocals)
                    for j in range(2):
                        n = 2 * (m % NG) + j
                        h = 4 * (n % G) + n // G
                        last = nc.vector.scalar_tensor_tensor(ratio[:, i, j, :], sums[:, i, 0, j, :], nlam[:, h:h + 1], rec[:, i4, 1, j, :], ALU.mult, ALU.mult)
                    ratios = st.inc(last)
                    if with_output:
                        output(b - 1)
                    if between is not None:
                        maxima(b, between + 1)
                    if with_keys:
                        spread_keys(b + 1)
                    st.wait(ratios)
                    for j in range(2):
                        for t in range(TT):
                            s = slice(t * P, t * P + (t + 1) * P)
                            last = nc.vector.scalar_tensor_tensor(dif[:, i4, j, s], pr[:, i, 1, j, s], ratio[:, i, j, t:t + 1], pr[:, i, 0, j, s], ALU.mult, ALU.add)
                    last.then_inc(dif_ready, 1)

                def second_maxima(b, m):
                    i4 = m % 4
                    dve.wait_ge(dif_masked, b * NG + m + 1)
                    for t in range(TT):
                        last = nc.vector.tensor_reduce(nm2[:, i4, :, t], dif[:, i4, :, t * P:t * P + (t + 1) * P], AX.X, ALU.max, negate=True)
                    st.do(last)
                    nc.vector.tensor_tensor(nb2[:, i4, :, :], nm2[:, i4, :, :], rec[:, i4, 0, :, :], ALU.mult).then_inc(nb_ready, 1)

                flat = lambda ap: ap.rearrange("p t (h e) -> p (t h) e", e=HD)

                def take_output(b):
                    dve.wait_ge(av_ps, b * NG + NG)
                    st.do(nc.vector.reciprocal(recs[:, :, :], O[:, :, :, HD]))
                    heads = lambda ap: ap.rearrange("p (h e) -> p h e", e=HD)
                    for t in range(TT):
                        last = nc.vector.tensor_tensor(heads(on[:, t, :]), O[:, t, :, 0:HD], bc(recs[:, t, :], 2, HD), ALU.mult)
                    last.then_inc(on_raw, 1)

                def norm_1(b):
                    dve.wait_ge(on_raw, b + 2)
                    st.do(nc.vector.tensor_tensor(osq[:, :, :], on[:, :, :], on[:, :, :], ALU.mult))
                    st.do(nc.vector.tensor_reduce(vv[:, :], flat(osq[:, :, :]), AX.X, ALU.add))
                    st.do(nc.vector.tensor_scalar(vv[:, :], vv[:, :], 1.0 / HD, EPS, ALU.mult, ALU.add))

                def norm_2(b):
                    newton_rsqrt(nc, st, vv[:, :], rs[:, :], tmp[:, :])
                    st.wait()

                def norm_3(b):
                    st.do(nc.vector.tensor_tensor(flat(on[:, :, :]), flat(on[:, :, :]), bc(rs[:, :], 2, HD), ALU.mult))
                    nc.vector.tensor_tensor(flat(on[:, :, :]), flat(on[:, :, :]), bc(gain[:, :], 1, TT * H), ALU.mult).then_inc(on_ready, 1)

                def output(b):
                    dve.wait_ge(y_ps, b + 1)
                    add_output(nc, x_sb, b * TT, TT, PT[1].rearrange("p (t n) -> p t n", t=TT), z_ready)

                def sequence(b, opening, closing):
                    for m in range(NG):
                        if opening and m == 0:
                            maxima(b, 0)
                            maxima(b, 1)
                        else:
                            last_pair = m == NG - 1
                            difference(b, m - 1, opening, 2 * m, last_pair and not opening, last_pair and not closing)
                        if not opening:
                            if m == 3:
                                take_output(b - 1)
                            if m == 4:
                                norm_1(b - 1)
                            if m == 5:
                                norm_2(b - 1)
                                norm_3(b - 1)
                        if not opening or m >= 2:
                            second_maxima(b, m - 2)
                        if not opening and m == 7:
                            dve.wait_ge(z_ready, b)
                            measure(nc, st, x_sb, mv, b * TT - TT, TT, lw)

                for j in range(NCH):
                    rotate(j)
                dve.wait_ge(k_rotated, NCH)
                spread_keys(0)
                st.begin(0)
                sequence(0, True, False)
                st.pad()
                with dve.Fori(0, B - 2) as b:
                    st.begin(b + 1)
                    sequence(b + 1, False, False)
                    st.end()
                st.begin(B - 1)
                sequence(B - 1, False, True)
                st.end()
                st.begin(B)
                difference(B, -1, False, None)
                second_maxima(B, -2)
                second_maxima(B, -1)
                take_output(B - 1)
                norm_1(B - 1)
                norm_2(B - 1)
                norm_3(B - 1)
                output(B - 1)
                dve.wait_ge(z_ready, B)
                measure(nc, st, x_sb, mv, B * TT - TT, TT, lw)


L3A_STEPS = 3 * 8 + 5 + NEWTON_STEPS + LN_STEPS



def l3_ffn(nc, c, x_sb, mv, xT, w, psum):
    E, I, TOP = 32, 96, 4
    NH = E * I // P
    with ExitStack() as ctx:
        sb = lambda name, shape, dt=F32: ctx.enter_context(nc.sbuf_tensor("l3f_" + name, shape, dt))
        sem = lambda name: ctx.enter_context(nc.semaphore("l3f_" + name))
        pb = sb("pb", [P, NT, E + 8 - TOP])
        nm = sb("nm", [P, NT])
        sums = sb("sums", [P, NT])
        top = sb("top", [P, NT, 8])
        pick = sb("pick", [P, NT, 8])
        left = sb("left", [P, NT, E + 8 - TOP])
        wsum = sb("wsum", [P, NT])
        cw = sb("cw", [P, NT, E])
        rest = sb("rest", [P, NT, E])
        c3 = sb("c3", [P, NT, 3, E], BF16)
        c3T = sb("c3T", [3 * E, TOK], BF16)
        sg = sb("sg", [P, 2, CN])
        gu = sb("gu", [P, 2, CN])
        hw = sb("hw", [P, 2, CN])
        x_hi = sb("x_hi", [P, KD, TOK], F32R)
        x_lo = xT[:, :, :].bitcast(F32R)
        w_hi = sb("w_hi", [P, 3, 3 * KD, P], F32R)
        w_lo = sb("w_lo", [P, 3, 3 * KD, P], F32R)
        h_hi = sb("h_hi", [P, 2, CN], F32R)
        h_lo = sb("h_lo", [P, 2, CN], F32R)
        lw = ln_scratch(sb, CH)
        bank = lambda i: psum[:, i, :]
        GB, UB, CB = [bank(0), bank(1)], [bank(2), bank(3)], [bank(4), bank(5)]
        Y = psum[:, 6:8, :].rearrange("p a (t n) -> p (a t) n", t=2)
        LOGITS = bank(0).rearrange("p (t e) -> p t e", t=NT)

        logit_ps = sem("logit_ps")
        nm_ready = sem("nm_ready")
        ex_ready = sem("ex_ready")
        c3_ready = sem("c3_ready")
        c3T_ps = sem("c3T_ps")
        c3T_ready = sem("c3T_ready")
        h_ps = sem("h_ps")
        sg_ready = sem("sg_ready")
        gu_ready = sem("gu_ready")
        hw_ready = sem("hw_ready")
        xhi_ready, xlo_ready, whi_ready, wlo_ready = c["split_sems"]
        X0, W0 = 2 * NCH, 2 + NCH * 10 + 2 + NCH * 8
        hhi_ready = sem("hhi_ready")
        hlo_ready = sem("hlo_ready")
        used = sem("used")
        z_ready = sem("z_ready")
        steps = sem("steps")
        route_steps = sem("route_steps")

        with nc.Block() as block:
            @block.tensor
            def _(pe):
                mm = nc.tensor.matmul

                def clear_output():
                    for a in (6, 7):
                        mm(bank(a), c["zero"], c["finite"], start=True, stop=False)

                w["early"](pe)
                for t in range(NT):
                    for k in range(KD):
                        last = mm(LOGITS[:, t, :], xT[:, k, t * P:(t + 1) * P], w["router"][:, k, :], start=(k == 0), stop=(k == KD - 1))
                last.then_inc(logit_ps, 1)
                pe.wait_ge(c3_ready, 1)
                for t in range(NT):
                    last = nc.tensor.transpose(psum[0:3 * E, 2 + t // 8, (t % 8) * P // 2:(t % 8 + 1) * P // 2].bitcast(BF16),
                                               c3[:, t, :, :].rearrange("p a e -> p (a e)"), c["idb"])
                last.then_inc(c3T_ps, 1)
                pe.wait_ge(c3T_ready, 1)
                pe.wait_ge(xlo_ready, X0 + 1)
                with pe.Fori(0, NCH) as b:
                    chunk = bass.ds(b * CN, CN)

                    def hidden(e):
                        pe.wait_ge(wlo_ready, b * NH + e + 1 + W0)
                        if e >= 2:
                            pe.wait_ge(hw_ready, b * NH + e - 1)
                        for first, bk in ((0, GB), (KD, UB)):
                            for k in range(KD):
                                hi, lo = w_hi[:, e % 3, first + k, :], w_lo[:, e % 3, first + k, :]
                                mm(bk[e % 2], hi, x_hi[:, k, chunk], start=(k == 0), stop=False)
                                mm(bk[e % 2], hi, x_lo[:, k, chunk], start=False, stop=False)
                                mm(bk[e % 2], lo, x_hi[:, k, chunk], start=False, stop=(k == KD - 1))
                        mm(CB[e % 2], c["sel3"][:, e * P:(e + 1) * P], c3T[:, chunk], start=True, stop=True).then_inc(h_ps, 1)

                    def down(e):
                        pe.wait_ge(hlo_ready, b * NH + e + 1)
                        if e == 0:
                            pe.wait_ge(z_ready, b + 1)
                            clear_output()
                        both = lambda ap: ap.rearrange("p k n -> p (k n)")
                        hi, lo = both(w_hi[:, e % 3, 2 * KD:, :]), both(w_lo[:, e % 3, 2 * KD:, :])
                        for t in range(CH):
                            tokens = slice(t * P, (t + 1) * P)
                            mm(Y[:, t, :], h_hi[:, e % 2, tokens], hi, start=False, stop=False)
                            mm(Y[:, t, :], h_hi[:, e % 2, tokens], lo, start=False, stop=False)
                            last = mm(Y[:, t, :], h_lo[:, e % 2, tokens], hi, start=False, stop=(e == NH - 1 and t % 2 == 1))
                        last.then_inc(used, 1)

                    for e in range(NH + 1):
                        if e < NH:
                            hidden(e)
                        if e >= 1:
                            down(e - 1)

            @block.scalar
            def _(act):
                nc.scalar.activation(x_hi[:, :, :], xT[:, :, :], ACT.Copy).then_inc(xhi_ready, 1)

                def weights_hi(e, count):
                    act.wait_ge(used, count + 1)
                    nc.scalar.activation(w_hi[:, e % 3, :, :], w["all"][:, e, :].rearrange("p (k n) -> p k n", n=P), ACT.Copy).then_inc(whi_ready, 1)

                act.sem_inc(used, 3)
                act.wait_ge(nm_ready, 1)
                for t in range(NT):
                    last = nc.scalar.activation(pb[:, t, 0:E], LOGITS[:, t, :], ACT.Exp, bias=nm[:, t:t + 1], accum_out=sums[:, t:t + 1])
                last.then_inc(ex_ready, 1)
                nc.scalar.preload_act_table(ACT.Silu)
                w["late"](act)
                weights_hi(0, 0)
                with act.Fori(0, NCH) as b:
                    for e in range(NH):
                        weights_hi((e + 1) % NH, b * NH + e + 1)
                        act.wait_ge(h_ps, b * NH + e + 1)
                        if e >= 2:
                            act.wait_ge(gu_ready, b * NH + e - 1)
                        nc.scalar.activation(sg[:, e % 2, :], GB[e % 2], ACT.Silu).then_inc(sg_ready, 1)

            @block.vector
            def _(dve):
                nc.vector.memset(pb[:, :, E:], BIG)
                nc.vector.memset(pick[:, :, :], BIG)
                st = Steps(dve, route_steps, 0)
                st.begin(0)
                dve.wait_ge(logit_ps, 1)
                nc.vector.tensor_reduce(nm[:, :], LOGITS, AX.X, ALU.max, negate=True).then_inc(nm_ready, 1)
                dve.wait_ge(xhi_ready, X0 + 1)
                nc.vector.tensor_tensor(x_lo, xT[:, :, :], x_hi[:, :, :].bitcast(F32), ALU.subtract).then_inc(xlo_ready, 1)
                dve.wait_ge(ex_ready, 1)
                st.do(nc.vector.reciprocal(wsum[:, :], sums[:, :]))
                st.do(nc.vector.tensor_tensor(pb[:, :, 0:E], pb[:, :, 0:E], bc(wsum[:, :], 2, E), ALU.mult))
                for t in range(NT):
                    last = nc.vector.max(top[:, t, :], pb[:, t, 0:E])
                st.do(last)
                st.do(nc.vector.tensor_copy(pick[:, :, 0:TOP], top[:, :, 0:TOP]))
                for t in range(NT):
                    last = nc.vector.match_replace(left[:, t, :], pick[:, t, :], pb[:, t, :], -BIG)
                st.do(last)
                st.do(nc.vector.scalar_tensor_tensor(cw[:, :, :], left[:, :, 0:E], -BIG, pb[:, :, 0:E], ALU.is_equal, ALU.mult))
                st.do(nc.vector.tensor_reduce(wsum[:, :], cw[:, :, :], AX.X, ALU.add))
                st.do(nc.vector.reciprocal(wsum[:, :], wsum[:, :]))
                st.do(nc.vector.tensor_tensor(cw[:, :, :], cw[:, :, :], bc(wsum[:, :], 2, E), ALU.mult))
                split3(nc, st, cw[:, :, :], [c3[:, :, j, :] for j in range(3)], rest[:, :, :])
                nc.vector.memset(lw["carrier"][:, :], 0.0).then_inc(c3_ready, 1)
                dve.wait_ge(c3T_ps, 1)
                nc.vector.tensor_copy(c3T[:, :].rearrange("p (a n) -> p a n", a=2), psum[0:3 * E, 2:4, :].bitcast(BF16)).then_inc(c3T_ready, 1)
                dve.sem_inc(z_ready, 1)
                w["late"](dve)

                def weights_lo(e, count):
                    dve.wait_ge(whi_ready, count + 1 + W0)
                    nc.vector.tensor_tensor(w_lo[:, e % 3, :, :], w["all"][:, e, :].rearrange("p (k n) -> p k n", n=P),
                                            w_hi[:, e % 3, :, :].bitcast(F32), ALU.subtract).then_inc(wlo_ready, 1)

                weights_lo(0, 0)
                st = Steps(dve, steps, LN_STEPS)
                with dve.Fori(0, NCH) as b:
                    st.begin(b)

                    for e in range(NH):
                        weights_lo((e + 1) % NH, b * NH + e + 1)
                        dve.wait_ge(sg_ready, b * NH + e + 1)
                        nc.vector.tensor_tensor(gu[:, e % 2, :], sg[:, e % 2, :], UB[e % 2], ALU.mult).then_inc(gu_ready, 1)
                        dve.wait_ge(gu_ready, b * NH + e + 1)
                        nc.vector.tensor_tensor(hw[:, e % 2, :], gu[:, e % 2, :], CB[e % 2], ALU.mult).then_inc(hw_ready, 1)
                        dve.wait_ge(hw_ready, b * NH + e + 1)
                        dve.wait_ge(used, b * NH + e + 2)
                        nc.vector.tensor_copy(h_hi[:, e % 2, :], hw[:, e % 2, :]).then_inc(hhi_ready, 1)
                        dve.wait_ge(hhi_ready, b * NH + e + 1)
                        nc.vector.tensor_tensor(h_lo[:, e % 2, :], hw[:, e % 2, :], h_hi[:, e % 2, :].bitcast(F32), ALU.subtract).then_inc(hlo_ready, 1)
                    dve.wait_ge(used, b * NH + NH + 3)
                    add_and_measure(nc, st, x_sb, mv, b * CH, CH, Y, lw, z_ready, b + 2)
                    st.end()



LAST_STAGE = 8
W_COLS = {
    "l0a_q": KD * 512, "l0a_k": KD * 256, "l0a_v": KD * 64, "l0a_o": KD * D,
    "l0f_w1": 32 * 128, "l0f_w2": 32 * 128, "l0f_fc1": KD * 128, "l0f_fc2": D, "l0f_gate": KD * 32, "l0f_up": KD * 512,
    "l0f_down": 4 * D, "l0f_bias": 32,
    "l1a_q": KD * 2048, "l1a_k": KD * 2048, "l1a_v": KD * 2048, "l1a_o": 16 * D, "l1a_gq": 1, "l1a_gk": 1,
    "l1f_router": KD * 128, "l1f_all": 10 * 2 * D, "l1f_down": D, "l1f_amp": 16, "l1f_escale": 1,
    "l1f_sdown": 2 * D,
    "l2a_u": KD * 256, "l2a_v": KD * 256, "l2a_g1": KD * 64, "l2a_g2": 256, "l2a_bu": 2, "l2a_bv": 2,
    "l2a_bg1": 1, "l2a_bg2": 2, "l2a_conv": KD * 3, "l2a_convb": KD,
    "l2f_all": 8 * 2 * D, "l2f_down": 8 * D,
    "l3a_q": KD * 1024, "l3a_k": KD * 512, "l3a_v": KD * 64, "l3a_o": KD * D, "l3a_lq1": 256, "l3a_lq2": 256, "l3a_lk1": 256,
    "l3a_lk2": 256, "l3a_rms": 16, "l3a_rope_q": 2 * T, "l3a_rope_k": 4 * T, "l3a_mask": P,
    "l3f_router": KD * 32, "l3f_all": 24 * 3 * D,
}
W_CUT = {"l0a_q": KD, "l0a_k": KD, "l0a_v": KD, "l0a_o": KD, "l0f_w1": 32, "l0f_w2": 32, "l0f_fc1": KD, "l0f_gate": KD,
         "l0f_up": KD, "l1a_q": KD, "l1a_k": KD, "l1a_v": KD, "l1a_o": 16,
         "l1f_router": KD, "l1f_all": 10, "l1f_amp": 8, "l1f_sdown": 2,
         "l2a_u": KD, "l2a_v": KD, "l2a_g1": KD, "l2a_conv": KD, "l2f_all": 8, "l2f_down": 8,
         "l3a_q": KD, "l3a_k": KD, "l3a_v": KD, "l3a_o": KD, "l3a_lq1": 16, "l3a_lq2": 16, "l3a_lk1": 16, "l3a_lk2": 16, "l3a_rope_q": 2,
         "l3f_router": KD, "l3f_all": 24, "l0f_down": 4}
C_COLS = {"id": P, "l0_q": T, "l0_k": 2 * T, "one": 1}
CB_COLS = {"idb": P, "maskb": P, "zero": P}


EARLY = ("l0a_q", "l0a_k", "l0a_v", "l0a_o", "l0f_gate", "l0f_bias", "l1a_k", "l1a_gq", "l1a_gk", "l1f_router", "l1f_amp", "l1f_escale",
         "l2a_g1", "l2a_u", "l2a_v", "l2a_conv", "l2a_convb", "l3a_q", "l3a_k", "l3a_v", "l3f_router")
TOGETHER = {0: ("l0a", "l0f", "l1a"), 3: ("l1f", "l2a", "l2f"), 6: ("l3a",), 7: ("l3f",)}
LOAD_AT = {"l0a": "start", "l0f": "in_l0a", "l1a": 1}
STAGES = [("l0a", l0_attention), ("l0f", l0_ffn), ("l1a", l1_attention), ("l1f", l1_ffn), ("l2a", l2_mixing), ("l2f", l2_ffn),
          ("l3a", l3_attention), ("l3f", l3_ffn)]


def network(nc, x_in, cf, cb, wts, out):
    with ExitStack() as ctx:
        x_sb = ctx.enter_context(nc.sbuf_tensor("x_sb", [P, NT, D], F32))
        cf_sb = ctx.enter_context(nc.sbuf_tensor("cf_sb", [P, sum(C_COLS.values())], F32))
        cb_sb = ctx.enter_context(nc.sbuf_tensor("cb_sb", [P, sum(CB_COLS.values())], mybir.dt.uint16))
        sel_sb = ctx.enter_context(nc.sbuf_tensor("sel_sb", [P, 56 * P], mybir.dt.uint16))
        psum = ctx.enter_context(nc.psum_tensor("psum", [P, 8, 512], F32))
        mv = ctx.enter_context(nc.sbuf_tensor("mv", [P, NT, 2], F32))
        xT = ctx.enter_context(nc.sbuf_tensor("xT", [P, KD, TOK], F32))
        loaded = {}

        def sem(name):
            if name not in loaded:
                loaded[name] = ctx.enter_context(nc.semaphore(name))
            return loaded[name]

        c_split = [ctx.enter_context(nc.semaphore("split_" + n)) for n in ("x_hi", "x_lo", "w_hi", "w_lo")]
        shared = {n: ctx.enter_context(nc.semaphore("boundary_" + n)) for n in ("normal", "turned", "steps", "stored")}
        c, at = {"split_sems": c_split}, 0
        for name, n in C_COLS.items():
            c[name] = cf_sb[:, at:at + n]
            at += n
        at = 0
        for name, n in CB_COLS.items():
            c[name] = cb_sb[:, at:at + n].bitcast(BF16)
            at += n
        c["sel0"], c["sel3"] = sel_sb[:, 0:32 * P].bitcast(BF16), sel_sb[:, 32 * P:56 * P].bitcast(BF16)
        c["finite"] = c["sel0"][:, 0:512]
        c["l0_k"] = c["l0_k"].rearrange("p (j t) -> p j t", j=2)
        x_rows = x_in.rearrange("b (t p) d -> p (b t) d", p=P)
        o_rows = out.rearrange("b (t p) d -> p (b t) d", p=P)

        c["sel0"], c["sel3"] = c["sel0"][0:96, :], c["sel3"][0:96, :]

        def weights(scope, stage):
            raw = {n: scope.enter_context(nc.sbuf_tensor("w_" + n, [P, k], F32)) for n, k in W_COLS.items() if n.startswith(stage)}
            view = {n[4:]: t[:, :].rearrange("p (k n) -> p k n", k=W_CUT[n]) if n in W_CUT else t[:, :] for n, t in raw.items()}
            return raw, view

        scopes, waiting, loads = {}, {}, {}
        for s, (stage, run) in enumerate(STAGES[:LAST_STAGE]):
            if s in TOGETHER:
                for other in reversed(TOGETHER[s]):
                    scopes[other] = ExitStack()
                    raw, view = weights(scopes[other], other)
                    waiting[other] = raw, view
                for other in TOGETHER[s]:
                    raw, view = waiting[other]
                    early, late = sem(other + "_late"), sem(other + "_late")
                    if other == stage:
                        early = sem(other + "_early")
                    first = [n for n in raw if n in EARLY] if other == stage else []
                    rest = [n for n in raw if n not in first]
                    loads.setdefault(LOAD_AT.get(other, s), []).extend(
                        [(raw[n][:, :], wts[n], early) for n in first] + [(raw[n][:, :], wts[n], late) for n in rest])
                    if other == "l0f":
                        loads[LOAD_AT[other]].append((sel_sb[:, :], wts["table_select"], late))
                        rest = rest + ["table_select"]
                    view["late"] = (lambda eng, sem=late, n=len(rest): eng.wait_ge(sem, 16 * n)) if rest else (lambda eng: None)
                    view["early"] = (lambda eng, sem=early, n=len(first): eng.wait_ge(sem, 16 * n)) if first else view["late"]

            def issue(sp, at):
                for dst, src, loaded in loads.get(at, ()):
                    sp.dma_start(dst, src).then_inc(loaded, 16)

            if s == 0:
                with nc.Block() as block:
                    @block.sync
                    def _(sp):
                        for dst, src in ((x_sb[:, :, :], x_rows), (cf_sb[:, :], cf), (cb_sb[:, :], cb)):
                            sp.dma_start(dst, src).then_inc(shared["stored"], 16)
                        issue(sp, "start")
                        sp.wait_ge(shared["stored"], 3 * 16)
            waiting[stage][1]["prefetch"] = lambda sp: issue(sp, "in_" + stage)
            boundary(nc, c, x_sb, mv, xT, psum, shared, s, "to_" + stage, lambda sp: issue(sp, s), normalise=(s > 0))
            run(nc, c, x_sb, mv, xT, waiting[stage][1], psum)
            scopes[stage].close()
        boundary(nc, c, x_sb, mv, xT, psum, shared, LAST_STAGE, "end", lambda sp: None, transpose=False, out_rows=o_rows)



def k_major(w):
    k, n = w.shape
    return np.ascontiguousarray(w.reshape(k // P, P, n).transpose(1, 0, 2).reshape(P, -1))


def l0_columns():
    q = [16 * (4 * g + r) + (j if j < 16 else (j - 16 + 8) % 16) for r in range(4) for g in range(4) for j in range(32)]
    k = [16 * g + (j + 8 * s) % 16 for s in range(2) for g in range(4) for j in range(32)]
    return np.array(q), np.array(k)


def rope_l0():
    f = (1.0 / 10000.0 ** (np.arange(0, 16, 2, dtype=np.float32) / np.float32(16))).astype(np.float32)
    ang = (np.arange(T, dtype=np.float32)[:, None] * f[None, :]).astype(np.float32)
    cos, sin = np.cos(ang).astype(np.float32), np.sin(ang).astype(np.float32)
    j = np.arange(P) % 16
    cp, sp = cos[:, j % 8].T, sin[:, j % 8].T * np.where(j < 8, -1, 1)[:, None].astype(np.float32)
    first = (np.arange(P) % 32 < 16)[:, None]
    return (np.where(first, cp, sp) * np.float32(0.25)).astype(np.float32), np.concatenate([cp, sp], 1).astype(np.float32)


def l3_columns():
    q = [32 * (4 * g + r) + ((16 * a + j) if j < 16 else (16 * a + j - 16) ^ 1)
         for a in range(2) for r in range(4) for g in range(4) for j in range(32)]
    k = [32 * g + ((16 * a + j % 16) ^ s) for a in range(2) for s in range(2) for g in range(4) for j in range(32)]
    return np.array(q), np.array(k)


def rope_l3():
    f = (1.0 / 10000.0 ** (np.arange(0, 32, 2, dtype=np.float32) / np.float32(32))).astype(np.float32)
    ang = (np.arange(T, dtype=np.float32)[:, None] * f[None, :]).astype(np.float32)
    cos, sin = np.cos(ang).astype(np.float32), np.sin(ang).astype(np.float32)
    qs, ks = [], []
    for a in range(2):
        dd = 16 * a + np.arange(P) % 16
        cp, sp = cos[:, dd // 2].T, sin[:, dd // 2].T * np.where(dd % 2 == 0, -1, 1)[:, None].astype(np.float32)
        qs.append(np.where((np.arange(P) % 32 < 16)[:, None], cp, sp) * np.float32(0.25))
        ks += [cp, sp]
    return np.concatenate(qs, 1).astype(np.float32), np.concatenate(ks, 1).astype(np.float32)


def causal_mask():
    return np.where(np.arange(P)[None, :] > np.arange(P)[:, None], np.float32(NEG), np.float32(0))


def tables():
    q0, k0 = rope_l0()
    mask = causal_mask()
    cf = np.concatenate([np.eye(P, dtype=np.float32), q0, k0, np.ones((P, 1), np.float32)], 1)
    part = np.arange(P)[:, None]
    sel0 = (part % 32 == np.arange(32 * P)[None, :] // P).astype(np.float32)
    sel3 = (part % 32 == np.arange(24 * P)[None, :] // 96).astype(np.float32)
    bits = lambda a: np.ascontiguousarray((np.concatenate(a, 1).view(np.uint32) >> 16).astype(np.uint16))
    return np.ascontiguousarray(cf), bits([np.eye(P, dtype=np.float32), mask, np.zeros((P, P), np.float32)]), bits([sel0, sel3])


def tiles(a):
    return a.reshape(KD, P, -1, P).transpose(1, 2, 0, 3).reshape(P, -1, KD * P)


def side_by_side(gate, up):
    return np.concatenate([tiles(gate), tiles(up)], 2).reshape(P, -1)


def layouts(i):
    q0, k0 = l0_columns()
    w = {
        "l0a_q": k_major(i["L0_attn_wq"][:, q0]), "l0a_k": k_major(i["L0_attn_wk"][:, k0]),
        "l0a_v": k_major(i["L0_attn_wv"]), "l0a_o": k_major(i["L0_attn_wo"]),
    }
    w |= {
        "l0f_w1": i["L0_ffn_w1"].transpose(2, 0, 1).reshape(P, -1), "l0f_w2": i["L0_ffn_w2"].transpose(2, 0, 1).reshape(P, -1),
        "l0f_fc1": k_major(i["L0_ffn_fc1_w"].T), "l0f_fc2": i["L0_ffn_fc2_w"].T, "l0f_gate": k_major(i["L0_ffn_gate_w"].T),
        "l0f_up": k_major(i["L0_ffn_shared_up_w"].T), "l0f_down": k_major(i["L0_ffn_shared_down_w"].T),
        "l0f_bias": np.broadcast_to(i["L0_ffn_gate_bias"], (P, 32)),
    }
    w |= {
        "l1a_q": k_major(i["L1_attn_Wq"].T), "l1a_k": k_major(i["L1_attn_Wk"].T), "l1a_v": k_major(i["L1_attn_Wv"].T),
        "l1a_o": k_major(i["L1_attn_Wo"].T), "l1a_gq": i["L1_attn_gq"][:, None], "l1a_gk": i["L1_attn_gk"][:, None],
    }
    w |= {
        "l1f_router": k_major(i["L1_ffn_w_router"]),
        "l1f_all": side_by_side(np.concatenate([i["L1_ffn_w_gate"], i["L1_ffn_shared_w_gate"]], 1),
                                np.concatenate([i["L1_ffn_w_up"], i["L1_ffn_shared_w_up"]], 1)),
        "l1f_down": i["L1_ffn_w_down"], "l1f_amp": i["L1_ffn_amplitudes"].reshape(P, -1), "l1f_escale": i["L1_ffn_expert_scale"][:, None],
        "l1f_sdown": k_major(i["L1_ffn_shared_w_down"]),
    }
    halves = lambda v: v.reshape(2, P).T
    down = lambda a: np.pad(a, ((0, P - a.shape[0]), (0, 0)))
    w |= {
        "l2a_u": k_major(i["L2_attn_Wu"].T), "l2a_v": k_major(i["L2_attn_Wv"].T), "l2a_g1": k_major(i["L2_attn_Wg1"].T),
        "l2a_g2": down(i["L2_attn_Wg2"].T), "l2a_bu": halves(i["L2_attn_bu"]),
        "l2a_bv": halves(i["L2_attn_bv"]), "l2a_bg1": down(i["L2_attn_bg1"][:, None]), "l2a_bg2": halves(i["L2_attn_bg2"]),
        "l2a_conv": k_major(i["L2_attn_conv_w"][:, 0, :]), "l2a_convb": halves(i["L2_attn_conv_b"]),
    }
    deal = (512 * np.arange(2)[:, None, None] + 4 * np.arange(P)[None, None, :] + np.arange(4)[None, :, None]).reshape(-1)
    w |= {
        "l2f_all": side_by_side(i["L2_ffn_w_gate"][:, deal], i["L2_ffn_w_up"][:, deal]),
        "l2f_down": k_major(i["L2_ffn_w_down"][deal, :]),
    }
    q3, k3 = l3_columns()
    rope_q, rope_k = rope_l3()
    every = lambda a: np.broadcast_to(a.reshape(-1), (P, a.size))
    g3 = i["L3_ffn_gate_up_proj"].transpose(1, 0, 2)
    w |= {
        "l3a_q": k_major(i["L3_attn_Wq"][:, q3]), "l3a_k": k_major(i["L3_attn_Wk"][:, k3]), "l3a_v": k_major(i["L3_attn_Wv"]),
        "l3a_o": k_major(i["L3_attn_Wo"]), "l3a_rms": every(i["L3_attn_rms_w"]),
        "l3a_rope_q": rope_q, "l3a_rope_k": rope_k, "l3a_mask": causal_mask(),
        **{"l3a_" + n: every(i["L3_attn_" + n]) for n in ("lq1", "lq2", "lk1", "lk2")},
        "l3f_router": k_major(i["L3_ffn_gate"]), "l3f_all": np.concatenate([tiles(g3[:, :, 0:96]), tiles(g3[:, :, 96:192]),
                                                                            i["L3_ffn_down_proj"].reshape(24, P, D).transpose(1, 0, 2)], 2).reshape(P, -1),
    }
    return {n: np.ascontiguousarray(a) for n, a in w.items()}


def kernel(**inputs):
    import concourse.bacc as bacc
    from concourse.bass_utils import run_bass_kernel_spmd

    i = {k: np.asarray(v) for k, v in inputs.items()}
    cf, cb, select = tables()
    host = {"x": np.ascontiguousarray(i["L0_attn_x"]), "table_f32": cf, "table_bf16": cb, "table_select": select, **layouts(i)}
    nc = bacc.Bacc("TRN2", target_bir_lowering=False, num_devices=1)
    arrays, aps = {}, {}
    for name, a in host.items():
        arrays[name + "_dram"] = a
        aps[name] = nc.dram_tensor(name + "_dram", a.shape, mybir.dt.from_np(a.dtype), kind="ExternalInput").ap()
    out = nc.dram_tensor("out_dram", (B, T, D), F32, kind="ExternalOutput").ap()
    network(nc, aps["x"], aps["table_f32"], aps["table_bf16"], aps, out)
    r = run_bass_kernel_spmd(nc, [arrays], core_ids=[0])
    return r.results[0]["out_dram"]
```
